# Optimizing a Trainium2 kernel written in Bass

```python
import numpy as np
import jax
import jax.numpy as jnp

def _softmax(x, axis=-1):
    return jax.nn.softmax(x, axis=axis)

def _gelu(x):
    return jax.nn.gelu(x, approximate=True)

def _silu(x):
    return jax.nn.silu(x)

def _sigmoid(x):
    return jax.nn.sigmoid(x)

def _layernorm(x, axis=-1, eps=1e-05):
    m = jnp.mean(x, axis=axis, keepdims=True)
    v = jnp.var(x, axis=axis, keepdims=True)
    return (x - m) / jnp.sqrt(v + eps)

def _scatter_add(tgt, idx, src, axis=0):
    return tgt.at[idx].add(src)

def _segment_sum(src, seg, n):
    return jax.ops.segment_sum(src, seg, n)
kernel_name = 'mk_decoder_preln_d1_seqx_r4_7b4e37'

def setup_inputs(seed: int=0):
    np.random.seed(seed)
    _w = jnp.asarray

    def _rec_inputs():
        import jax
        import jax.numpy as jnp
        _rk = jax.random.key(seed)
        x = -0.000125 + 0.9999 * jax.random.normal(jax.random.fold_in(_rk, 1), (2, 512, 1024), jnp.float32)
        _lenS = 512 - jax.random.randint(jax.random.fold_in(_rk, 7), (2,), 0, max(1, 512 // 4) + 1, jnp.int32)
        _lenS2 = 1024 - jax.random.randint(jax.random.fold_in(_rk, 8), (2,), 0, max(1, 1024 // 4) + 1, jnp.int32)
        _ctx_4096P = jax.random.normal(jax.random.fold_in(_rk, 11), (2, 16, 1024), jnp.float32)
        _ctx_4096c = jax.random.dirichlet(jax.random.fold_in(_rk, 511), 0.3 * jnp.ones((16,), jnp.float32), (2, 1024))
        _ctx_4096t = jnp.einsum('bsk,bkd->bsd', _ctx_4096c, _ctx_4096P)
        _ctx_4096t = _ctx_4096t * jax.lax.rsqrt(jnp.mean(jnp.square(_ctx_4096t)) + 1e-12) * 0.953939
        ctx_4096 = -5.72187e-05 + 0.999849 * (_ctx_4096t + 0.3 * jax.random.normal(jax.random.fold_in(_rk, 611), (2, 1024, 1024), jnp.float32))
        return (x, ctx_4096)
    x, ctx_4096 = _rec_inputs()

    def _L0_attn_setup():
        import jax, jax.numpy as jnp
        import numpy as np
        NUM_HEADS = 32
        NUM_KV_HEADS = 8
        HEAD_DIM = 128
        ROPE_THETA = 10000.0

        def _rope_cos_sin(seq_len, head_dim, dtype):
            inv_freq = 1.0 / ROPE_THETA ** (jnp.arange(0, head_dim, 2, dtype=jnp.float32) / head_dim)
            t = jnp.arange(seq_len, dtype=jnp.float32)
            freqs = jnp.outer(t, inv_freq)
            emb = jnp.concatenate([freqs, freqs], axis=-1)
            return (jnp.cos(emb).astype(dtype), jnp.sin(emb).astype(dtype))

        def _rotate_half(x):
            h = x.shape[-1] // 2
            return jnp.concatenate([-x[..., h:], x[..., :h]], axis=-1)

        def _apply_rope(x, cos, sin):
            return x * cos[None, None] + _rotate_half(x) * sin[None, None]
        key = jax.random.key(seed)
        ks = jax.random.split(key, 5)
        B, S, H = (1, 512, 1024)
        return {'hidden_states': jax.random.normal(ks[0], (B, S, H), dtype=jnp.float32), 'Wq': jax.random.normal(ks[1], (H, NUM_HEADS * HEAD_DIM), dtype=jnp.float32) * 0.02, 'Wk': jax.random.normal(ks[2], (H, NUM_KV_HEADS * HEAD_DIM), dtype=jnp.float32) * 0.02, 'Wv': jax.random.normal(ks[3], (H, NUM_KV_HEADS * HEAD_DIM), dtype=jnp.float32) * 0.02, 'Wo': jax.random.normal(ks[4], (NUM_HEADS * HEAD_DIM, H), dtype=jnp.float32) * 0.02}
    _L0_attn_all = _L0_attn_setup()
    _L0_attn_in = {k: v for k, v in _L0_attn_all.items() if k in ('Wq', 'Wk', 'Wv', 'Wo')}
    del _L0_attn_all

    def _L0_xattn_setup():
        import jax, jax.numpy as jnp
        import numpy as np
        QMIN = 0.0
        QMAX = 255.0

        def fake_quant(x, scale, zp):
            s = scale.reshape(())
            z = zp.reshape(())
            q = jnp.clip(jnp.round(x / s + z), QMIN, QMAX)
            return (q - z) * s
        key = jax.random.key(seed)
        k1, k2 = jax.random.split(key)
        B, M, K, N = (4, 512, 1024, 1024)
        x1 = jax.random.normal(k1, (B, M, K), dtype=jnp.float32)
        x2 = jax.random.normal(k2, (B, K, N), dtype=jnp.float32)
        x1_scale = jnp.full((1,), 8.0 / 255.0, dtype=jnp.float32)
        x1_zp = jnp.full((1,), 128.0, dtype=jnp.float32)
        x2_scale = jnp.full((1,), 8.0 / 255.0, dtype=jnp.float32)
        x2_zp = jnp.full((1,), 128.0, dtype=jnp.float32)
        return {'x1': x1, 'x2': x2, 'x1_scale': x1_scale, 'x1_zp': x1_zp, 'x2_scale': x2_scale, 'x2_zp': x2_zp}
    _L0_xattn_all = _L0_xattn_setup()
    _L0_xattn_in = {k: v for k, v in _L0_xattn_all.items() if k in ('x1_scale', 'x1_zp', 'x2_scale', 'x2_zp')}
    del _L0_xattn_all

    def _L0_ffn_setup():
        import jax, jax.numpy as jnp
        import numpy as np
        IN_F = 1024
        OUT_F = 1024
        RANK = 8
        NUM_EXPERTS = 64
        TOP_K = 16
        ROUTER_DIM = 16
        ALPHA = 32
        SCALING = ALPHA / TOP_K
        BOTTLENECK = NUM_EXPERTS * RANK
        key = jax.random.key(seed)
        ks = jax.random.split(key, 5)
        x = jax.random.normal(ks[0], (4, 1024, IN_F), dtype=jnp.float32)
        bound_a = float(np.sqrt(6.0 / IN_F))
        A_w = jax.random.uniform(ks[1], (BOTTLENECK, IN_F), jnp.float32, -bound_a, bound_a)
        B_w = jax.random.normal(ks[2], (OUT_F, BOTTLENECK), dtype=jnp.float32) * 0.02
        Wq_w = jax.random.normal(ks[3], (ROUTER_DIM, IN_F), dtype=jnp.float32) * 0.02
        keys = jax.random.normal(ks[4], (NUM_EXPERTS, ROUTER_DIM), dtype=jnp.float32) * 0.01
        return {'x': x, 'A_w': A_w, 'B_w': B_w, 'Wq_w': Wq_w, 'keys': keys}
    _L0_ffn_all = _L0_ffn_setup()
    _L0_ffn_in = {k: v for k, v in _L0_ffn_all.items() if k in ('A_w', 'B_w', 'Wq_w', 'keys')}
    del _L0_ffn_all
    return {'x': x, 'ctx_4096': ctx_4096, 'L0_attn_Wq': _L0_attn_in['Wq'], 'L0_attn_Wk': _L0_attn_in['Wk'], 'L0_attn_Wv': _L0_attn_in['Wv'], 'L0_attn_Wo': _L0_attn_in['Wo'], 'L0_xattn_x1_scale': _L0_xattn_in['x1_scale'], 'L0_xattn_x1_zp': _L0_xattn_in['x1_zp'], 'L0_xattn_x2_scale': _L0_xattn_in['x2_scale'], 'L0_xattn_x2_zp': _L0_xattn_in['x2_zp'], 'L0_ffn_A_w': _L0_ffn_in['A_w'], 'L0_ffn_B_w': _L0_ffn_in['B_w'], 'L0_ffn_Wq_w': _L0_ffn_in['Wq_w'], 'L0_ffn_keys': _L0_ffn_in['keys']}

def reference(x, ctx_4096, L0_attn_Wq, L0_attn_Wk, L0_attn_Wv, L0_attn_Wo, L0_xattn_x1_scale, L0_xattn_x1_zp, L0_xattn_x2_scale, L0_xattn_x2_zp, L0_ffn_A_w, L0_ffn_B_w, L0_ffn_Wq_w, L0_ffn_keys):
    import jax
    import jax.numpy as jnp

    def _L0_attn_ref(hidden_states, Wq, Wk, Wv, Wo):
        import jax, jax.numpy as jnp
        import numpy as np
        NUM_HEADS = 32
        NUM_KV_HEADS = 8
        HEAD_DIM = 128
        ROPE_THETA = 10000.0

        def _rope_cos_sin(seq_len, head_dim, dtype):
            inv_freq = 1.0 / ROPE_THETA ** (jnp.arange(0, head_dim, 2, dtype=jnp.float32) / head_dim)
            t = jnp.arange(seq_len, dtype=jnp.float32)
            freqs = jnp.outer(t, inv_freq)
            emb = jnp.concatenate([freqs, freqs], axis=-1)
            return (jnp.cos(emb).astype(dtype), jnp.sin(emb).astype(dtype))

        def _rotate_half(x):
            h = x.shape[-1] // 2
            return jnp.concatenate([-x[..., h:], x[..., :h]], axis=-1)

        def _apply_rope(x, cos, sin):
            return x * cos[None, None] + _rotate_half(x) * sin[None, None]
        B, S, H = hidden_states.shape
        nh, nkv, hd = (NUM_HEADS, NUM_KV_HEADS, HEAD_DIM)
        groups = nh // nkv
        q = (hidden_states @ Wq).reshape(B, S, nh, hd).transpose(0, 2, 1, 3)
        k = (hidden_states @ Wk).reshape(B, S, nkv, hd).transpose(0, 2, 1, 3)
        v = (hidden_states @ Wv).reshape(B, S, nkv, hd).transpose(0, 2, 1, 3)
        cos, sin = _rope_cos_sin(S, hd, q.dtype)
        q = _apply_rope(q, cos, sin)
        k = _apply_rope(k, cos, sin)
        k = jnp.repeat(k, groups, axis=1)
        v = jnp.repeat(v, groups, axis=1)
        scale = 1.0 / jnp.sqrt(jnp.asarray(hd, dtype=q.dtype))
        logits = jnp.einsum('bhqd,bhkd->bhqk', q, k) * scale
        causal = jnp.tril(jnp.ones((S, S), dtype=bool))
        neg = jnp.asarray(jnp.finfo(logits.dtype).min, dtype=logits.dtype)
        logits = jnp.where(causal[None, None], logits, neg)
        attn = jax.nn.softmax(logits.astype(jnp.float32), axis=-1).astype(q.dtype)
        out = jnp.einsum('bhqk,bhkd->bhqd', attn, v)
        out = out.transpose(0, 2, 1, 3).reshape(B, S, nh * hd)
        return out @ Wo

    def _L0_xattn_ref(x1, x2, x1_scale, x1_zp, x2_scale, x2_zp):
        import jax, jax.numpy as jnp
        import numpy as np
        QMIN = 0.0
        QMAX = 255.0

        def fake_quant(x, scale, zp):
            s = scale.reshape(())
            z = zp.reshape(())
            q = jnp.clip(jnp.round(x / s + z), QMIN, QMAX)
            return (q - z) * s
        q1 = fake_quant(x1, x1_scale, x1_zp)
        q2 = fake_quant(x2, x2_scale, x2_zp)
        return jnp.matmul(q1, q2)

    def _L0_ffn_ref(x, A_w, B_w, Wq_w, keys):
        import jax, jax.numpy as jnp
        import numpy as np
        IN_F = 1024
        OUT_F = 1024
        RANK = 8
        NUM_EXPERTS = 64
        TOP_K = 16
        ROUTER_DIM = 16
        ALPHA = 32
        SCALING = ALPHA / TOP_K
        BOTTLENECK = NUM_EXPERTS * RANK
        q = jnp.einsum('bsd,rd->bsr', x, Wq_w)
        scores = jnp.einsum('bsr,er->bse', q, keys)
        top_vals, top_idx = jax.lax.top_k(scores, TOP_K)
        top_w = jax.nn.softmax(top_vals, axis=-1)
        gate = jnp.sum(jax.nn.one_hot(top_idx, NUM_EXPERTS, dtype=top_w.dtype) * top_w[..., None], axis=-2)
        z = jnp.einsum('bsd,nd->bsn', x, A_w)
        z = z.reshape(*z.shape[:-1], NUM_EXPERTS, RANK)
        z_gated = (z * gate[..., None]).reshape(*z.shape[:-2], BOTTLENECK)
        out = jnp.einsum('bsn,on->bso', z_gated, B_w) * SCALING
        return out
    x = x + _L0_attn_ref(_layernorm(x, axis=-1), L0_attn_Wq, L0_attn_Wk, L0_attn_Wv, L0_attn_Wo)
    x = x + _L0_xattn_ref(_layernorm(x, axis=-1), ctx_4096, L0_xattn_x1_scale, L0_xattn_x1_zp, L0_xattn_x2_scale, L0_xattn_x2_zp)
    x = x + _L0_ffn_ref(_layernorm(x, axis=-1), L0_ffn_A_w, L0_ffn_B_w, L0_ffn_Wq_w, L0_ffn_keys)
    return x

_drawn_inputs = setup_inputs


def setup_inputs(seed=0):
    import zlib

    import numpy as np

    out = dict(_drawn_inputs(seed))
    spreads = {}
    factors = {'L0_ffn_A_w': 8.0, 'L0_ffn_B_w': 8.0, 'L0_ffn_Wq_w': 8.0, 'L0_ffn_keys': 8.0}
    for name, (base, spread) in spreads.items():
        noise = np.random.default_rng([zlib.crc32(name.encode()), seed]).standard_normal(out[name].shape)
        drawn = base * np.exp(spread * noise) if base else spread * noise
        out[name] = jnp.asarray(drawn.astype(out[name].dtype))
    for name, factor in factors.items():
        out[name] = (out[name] * factor).astype(out[name].dtype)
    return out
```

```python
from contextlib import ExitStack

import numpy as np

import concourse.bass as bass
from concourse import mybir

BACC = {"dynamic_dma_scratch_size": 2048}
P = 128
ALU = mybir.AluOpType
ACT = mybir.ActivationFunctionType
AX = mybir.AxisListType
F32 = mybir.dt.float32
F32R = mybir.dt.float32r
BF16 = mybir.dt.bfloat16

HEAD = 128
GROUPS = 8
HPG = 4
ROPE_THETA = 10000.0
EPS = 1e-5
EXPERTS, RANK, TOP_K, ROUTER = 64, 8, 16, 16
SCALING = 32 / TOP_K
MAGIC = 1.5 * 2.0 ** 23
MIDDLE = 128.0
NEVER = -3.0e38
MASKED = -1.0e30

BODY = ["Q1", "Q2", "Q3", "Q0'", "K'", "V'", "A0", "A1", "B0", "B1"]
LAST = ["Q1", "Q2", "Q3", "A0", "A1", "B0", "B1"]
FIRST = ["Q0'", "K'", "V'"]
PLACE = dict(zip(BODY, [2, 0, 1, 2, 0, 1, 2, 0, 1, 0]))
PIECES = 28
ROPED = 10
SCORE_AT = {3: (0, 0), 2: (1, 0), 1: (2, 0), 0: (1, 384)}
PROB_AT = {3: 0, 2: 512, 1: 896, 0: 1152}
TILE_ORDER = (3, 2, 0, 1)
TILES_NEEDED = (1, 3, 3, 4)
KEYS_AT = {0: 0, 1: 512, 3: 896, 2: 1024}
CHUNKS = ((0, (0,)), (512, (1, 3)), (1024, (2,)))
CHUNK_WIDTH = (512, 512, 256)


def build(nc, x, ctx_in, Wq, Wk, Wv, Wo, x1s, x1z, x2s, x2z, A_w, B_w, Wr, keys, cos_in, sin_in, out,
          stages=3):
    NB, S, D = x.shape
    KT = D // P
    TT = NB * S // P
    TPB = TT // NB
    H = S

    x_t = x.rearrange("b (t p) d -> (b t) p d", p=P)
    out_t = out.rearrange("b (t p) d -> (b t) p d", p=P)

    def hold(es):
        def sb(name, shape, dt):
            return es.enter_context(nc.sbuf_tensor(name, shape, dt))

        def ps(name, shape, dt):
            return es.enter_context(nc.psum_tensor(name, shape, dt))

        def sem(name):
            return es.enter_context(nc.semaphore(name))
        return sb, ps, sem

    with ExitStack() as whole:
        sb, _, _ = hold(whole)
        resid = sb("resid", [P, TT, D], F32)
        ident = sb("ident", [P, P], F32)
        identb = sb("identb", [P, P], BF16)
        stats = sb("stats", [P, TT, 2, 6], F32)
        moments = sb("moments", [P, TT, 2], F32)
        rstd = sb("rstd", [P, TT], F32)
        lnw = sb("lnw", [P, 4, TT], F32)

        with ExitStack() as es:
            attention(nc, hold(es), es, x_t, Wq, Wk, Wv, Wo, cos_in, sin_in,
                      resid, ident, identb, stats, moments, rstd, lnw, KT, TT, TPB, H)
        if stages == 1:
            store(nc, hold, out_t, resid, TT)
            return
        with ExitStack() as es:
            sbw, _, _ = hold(es)
            aT = [sbw(f"aT{n}", [P, KT, EXPERTS * RANK], F32R) for n in ("h", "l")]
            rT = [sbw(f"rT{n}", [P, KT, P], F32R) for n in ("h", "l")]
            with ExitStack() as es2:
                context(nc, hold(es2), es2, ctx_in, x1s, x1z, x2s, x2z, A_w, Wr, aT, rT,
                        resid, ident, identb, stats, moments, rstd, lnw, KT, TT, TPB, H)
            if stages == 2:
                store(nc, hold, out_t, resid, TT)
                return
            with ExitStack() as es2:
                experts(nc, hold(es2), es2, out_t, B_w, keys, aT, rT,
                        resid, ident, identb, stats, moments, rstd, lnw, KT, TT, TPB, H)


def store(nc, hold, out_t, resid, TT):
    with ExitStack() as es:
        _, _, sem = hold(es)
        stored = sem("stored")
        block = es.enter_context(nc.Block())

        @block.sync
        def _(sp):
            for t in range(TT):
                sp.dma_start(out_t[t], resid[:, t, :]).then_inc(stored, 16)
            sp.wait_ge(stored, 16 * TT)


class Links:

    def __init__(self, eng, s):
        self.eng, self.s, self.n = eng, s, 0

    def __call__(self, ins):
        self.n += 1
        ins.then_inc(self.s, 1)
        self.eng.wait_ge(self.s, self.n)


def row_stats(nc, resid, stats, moments, t, link):
    nc.vector.bn_stats(stats[:, t, 0, :], resid[:, t, 0:512])
    link(nc.vector.bn_stats(stats[:, t, 1, :], resid[:, t, 512:1024]))
    link(nc.vector.bn_aggr(moments[:, t, :], stats[:, t, :, :]))


def row_scale_in(nc, moments, lnw, ts, var_ready):
    nc.vector.tensor_scalar(lnw[:, 0, ts], moments[:, ts, 1], EPS, None, ALU.add).then_inc(var_ready, 1)


def row_scale_out(nc, lnw, rstd, ts, link):
    link(nc.vector.reciprocal(lnw[:, 2, ts], lnw[:, 1, ts]))
    link(nc.vector.tensor_tensor(lnw[:, 3, ts], lnw[:, 0, ts], lnw[:, 2, ts], ALU.mult))
    link(nc.vector.tensor_tensor(lnw[:, 2, ts], lnw[:, 3, ts], lnw[:, 1, ts], ALU.add))
    link(nc.vector.tensor_scalar(lnw[:, 3, ts], lnw[:, 2, ts], 0.5, None, ALU.mult))
    link(nc.vector.reciprocal(rstd[:, ts], lnw[:, 3, ts]))


def attention(nc, held, es, x_t, Wq, Wk, Wv, Wo, cos_in, sin_in,
              resid, ident, identb, stats, moments, rstd, lnw, KT, TT, TPB, H):
    sb, psum, sem = held
    SCALE = float(HEAD) ** -0.5
    D = KT * P

    xn = [sb(f"xn_{n}", [P, KT, TT * P], F32R) for n in ("hi", "lo")]
    kT = [sb(f"kT_{n}", [P, 2, H], F32R) for n in ("hi", "lo")]
    vv = [sb(f"v_{n}", [P, 2, TPB, HEAD], F32R) for n in ("hi", "lo")]
    qo = [sb(f"qo_{n}", [P, HPG + 1, 2, H], F32R) for n in ("hi", "lo")]
    ring = [sb(f"ring_{n}", [P, 3, D], F32R) for n in ("hi", "lo")]
    raw = sb("raw", [P, 2, D], F32)
    prob = sb("prob", [P, 1280], F32)
    pT = [sb(f"pT_{n}", [P, 1280], F32R) for n in ("hi", "lo")]
    rope = sb("rope", [P, 2, H], F32)
    cos = sb("cos", [P, H], F32)
    sin = sb("sin", [P, H], F32)
    maskb = sb("maskb", [P, P], BF16)
    peak = sb("peak", [P, 4], F32)
    shift = sb("shift", [P, 4], F32)
    total = sb("total", [P, 4], F32)
    inv = sb("inv", [P, 4], F32)

    bank = [psum(f"bank{n}", [P, H], F32) for n in range(2)]
    score = psum("score", [P, 3, H], F32)
    turned = psum("turned", [P, 2, H], F32)
    mixed = psum("mixed", [P, H], F32)

    x_in = [sem(f"x_in{t}") for t in range(TT)]
    tables_in = sem("tables_in")
    ident_made = sem("ident_made")
    pool_link = sem("pool_link")
    var_ready, root_ready = sem("var_ready"), sem("root_ready")
    dve_link = sem("dve_link")
    ln_out, ln_turned, ln_hi, ln_lo = sem("ln_out"), sem("ln_turned"), sem("ln_hi"), sem("ln_lo")
    raw_in = [sem("raw_in0"), sem("raw_in1")]
    block_hi, block_lo = sem("block_hi"), sem("block_lo")
    piece_done = sem("piece_done")
    added = sem("added")
    rope_parts, rope_sum, rope_hi, rope_done = (sem("rope_parts"), sem("rope_sum"), sem("rope_hi"),
                                                sem("rope_done"))
    v_staged, v_turned, v_hi, v_done = sem("v_staged"), sem("v_turned"), sem("v_hi"), sem("v_done")
    score_done = sem("score_done")
    peak_done, shift_done = sem("peak_done"), sem("shift_done")
    exp_done = sem("exp_done")
    inv_done, prob_done = sem("inv_done"), sem("prob_done")
    turn_done, pT_hi, pT_lo = sem("turn_done"), sem("pT_hi"), sem("pT_lo")
    mix_done, o_hi, o_lo = sem("mix_done"), sem("o_hi"), sem("o_lo")

    def as32(ap):
        return ap.bitcast(F32)

    def o_place(h):
        return HPG if h == 0 else h

    def number(g, name, last):
        return len(FIRST) + len(BODY) * g + (LAST if last else BODY).index(name)

    def first_wo(last):
        return 6 if last else 12

    def freed(g, name, last):
        base = 6 + PIECES * g
        w = base + first_wo(last)
        return {"Q1": base, "Q2": base, "Q3": base, "Q0'": base + 2, "K'": base + 4, "V'": base + 6,
                "A0": base + (2 if last else 8), "A1": base + (4 if last else 10),
                "B0": base + (6 if last else 12), "B1": w + TT}[name]

    def source(g, name):
        if name[0] in "QKV":
            w, col = {"Q": (Wq, HPG), "K": (Wk, 1), "V": (Wv, 1)}[name[0]]
            head = g + 1 if name.endswith("'") else g
            head = head * col + (int(name[1]) if name[0] == "Q" else 0)
            return (w[:, bass.ds(head * HEAD, HEAD)].rearrange("(k p) c -> p k c", p=P), KT)
        half, pair = "AB".index(name[0]), int(name[1])
        return (Wo[bass.ds((g * HPG + 2 * pair) * HEAD, 2 * HEAD), half * 512:half * 512 + 512]
                .rearrange("(k p) c -> p k c", p=P), 2)

    block = es.enter_context(nc.Block())

    @block.sync
    def _(sp):
        def load(g, name, last, n, slot):
            if not isinstance(n, int) or n >= 2:
                sp.wait_ge(block_lo, n - 1)
            src, k = source(g, name)
            sp.dma_start(raw[:, slot, :].rearrange("p (k c) -> p k c", k=k), src).then_inc(raw_in[slot], 16)

        for t in range(TT):
            sp.dma_start(resid[:, t, :], x_t[t]).then_inc(x_in[t], 16)
            if t == 3:
                load(-1, "Q0'", False, 0, 0)
                load(-1, "K'", False, 1, 1)
        sp.dma_start(cos[:], cos_in).then_inc(tables_in, 16)
        sp.dma_start(sin[:], sin_in).then_inc(tables_in, 16)
        load(-1, "V'", False, 2, 0)
        with sp.Fori(0, GROUPS - 1) as g:
            for i, name in enumerate(BODY):
                load(g, name, False, g * len(BODY) + (3 + i), (3 + i) % 2)
        for i, name in enumerate(LAST):
            n = number(GROUPS - 1, name, True)
            load(GROUPS - 1, name, True, n, n % 2)

    @block.gpsimd
    def _(pool):
        link = Links(pool, pool_link)
        link(nc.gpsimd.memset(ident[:], 0.0))
        link(nc.gpsimd.memset(maskb[:], 0.0))
        nc.gpsimd.affine_select(out=ident[:], in_=ident[:], compare_op=ALU.not_equal, fill=1.0, base=0,
                                pattern=[[-1, P]], channel_multiplier=1).then_inc(ident_made, 1)
        nc.gpsimd.affine_select(out=maskb[:], in_=maskb[:], compare_op=ALU.is_ge, fill=MASKED, base=0,
                                pattern=[[-1, P]], channel_multiplier=1).then_inc(ident_made, 1)
        pool.wait_ge(ident_made, 2)
        nc.gpsimd.tensor_copy(identb[:], ident[:]).then_inc(ident_made, 1)

        def split(n, name, slot):
            pool.wait_ge(block_hi, n + 1)
            nc.gpsimd.tensor_tensor(ring[1][:, PLACE[name], :], raw[:, slot, :],
                                    as32(ring[0][:, PLACE[name], :]), ALU.subtract).then_inc(block_lo, 1)

        def rope_add(n):
            pool.wait_ge(rope_parts, n + 1)
            nc.gpsimd.tensor_tensor(rope[:, 0, :], rope[:, 0, :], rope[:, 1, :], ALU.add).then_inc(rope_sum, 1)

        def body(g, last):
            def sp(name):
                if last:
                    n = number(g, name, True)
                    split(n, name, n % 2)
                else:
                    i = BODY.index(name)
                    split(g * len(BODY) + (3 + i), name, (3 + i) % 2)
            rb = g * ROPED + 4
            sp("Q2")
            rope_add(rb)
            sp("Q3")
            rope_add(rb + 1)
            sp("A0" if last else "Q0'")
            rope_add(rb + 2)
            rope_add(rb + 3)
            sp("A1" if last else "K'")
            rope_add(rb + 4)
            rope_add(rb + 5)
            sp("B0" if last else "V'")
            if last:
                sp("B1")
                return
            rope_add(rb + 6)
            rope_add(rb + 7)
            sp("A0")
            rope_add(rb + 8)
            sp("A1")
            rope_add(rb + 9)
            sp("B0")
            sp("B1")
            split(g * len(BODY) + 13, "Q1", 1)

        split(0, "Q0'", 0)
        split(1, "K'", 1)
        split(2, "V'", 0)
        rope_add(0)
        rope_add(1)
        split(3, "Q1", 1)
        rope_add(2)
        rope_add(3)
        with pool.Fori(0, GROUPS - 1) as g:
            body(g, False)
        body(GROUPS - 1, True)

    @block.scalar
    def _(act):
        def root(h):
            act.wait_ge(var_ready, h + 1)
            nc.scalar.activation(lnw[:, 1, h * TPB:(h + 1) * TPB], lnw[:, 0, h * TPB:(h + 1) * TPB],
                                 ACT.Sqrt).then_inc(root_ready, 1)

        root(0)
        for n in range(2 * TT):
            if n == TT - 2:
                root(1)
            t, k0 = n // 2, 4 * (n % 2)
            act.wait_ge(ln_turned, n + 1)
            nc.scalar.copy(xn[0][:, k0:k0 + 4, t * P:(t + 1) * P],
                           ln_bank(score, turned, n)).then_inc(ln_hi, 1)

        def split(n, name, slot, uses, free):
            act.wait_ge(raw_in[slot], uses)
            if free is not None:
                act.wait_ge(piece_done, free)
            nc.scalar.copy(ring[0][:, PLACE[name], :], raw[:, slot, :]).then_inc(block_hi, 1)

        def rope_high(n, dst):
            act.wait_ge(rope_sum, n + 1)
            nc.scalar.copy(dst, rope[:, 0, :]).then_inc(rope_hi, 1)

        def v_high(n, b):
            act.wait_ge(v_turned, n + 1)
            nc.scalar.copy(vv[0][:, b, :, :], turned[:, b, :].rearrange("p (j c) -> p j c", c=HEAD)).then_inc(v_hi, 1)

        def body(g, last):
            def sp(name):
                if last:
                    n = number(g, name, True)
                    split(n, name, n % 2, 16 * (n // 2 + 1), freed(g, name, True))
                else:
                    i = BODY.index(name)
                    slot = (3 + i) % 2
                    split(None, name, slot, g * (16 * len(BODY) // 2) + 16 * ((3 + i) // 2 + 1),
                          freed(g, name, False))
            rb = g * ROPED + 4
            ub = g * 8

            def probs_high(u):
                for c in range(3):
                    act.wait_ge(turn_done, ub * 3 + (3 * u + c + 1))
                    if c == 0 and u > 0:
                        act.wait_ge(mix_done, ub + u)
                    nc.scalar.copy(pT[0][:, CHUNKS[c][0]:CHUNKS[c][0] + CHUNK_WIDTH[c]],
                                   turned_chunk(turned, mixed, c)).then_inc(pT_hi, 1)

            def exps(u):
                act.wait_ge(shift_done, ub + (u + 1))
                if u > 0:
                    act.wait_ge(turn_done, ub * 3 + 3 * u)
                for i in TILE_ORDER:
                    w = P * (i + 1)
                    s, c = SCORE_AT[i]
                    nc.scalar.activation(prob[:, PROB_AT[i]:PROB_AT[i] + w], score[:, s, c:c + w], ACT.Exp,
                                         bias=shift[:, i:i + 1], scale=SCALE,
                                         accum_out=total[:, i:i + 1]).then_inc(exp_done, 1)

            def out_high(u):
                act.wait_ge(mix_done, ub + (u + 1))
                nc.scalar.copy(qo[0][:, o_place(u // 2), u % 2, :], mixed[:]).then_inc(o_hi, 1)

            for u in range(8):
                if u > 0:
                    probs_high(u - 1)
                    if u < 7 or not last:
                        h = u - 1
                        rope_high(rb + h, qo[0][:, (h // 2 + 1) % HPG, h % 2, :])
                exps_first = {0: "Q2", 1: "Q3"}
                if u in exps_first:
                    sp(exps_first[u])
                elif not last and u in (2, 4, 6):
                    sp({2: "Q0'", 4: "K'", 6: "V'"}[u])
                elif last and u in (2, 4, 6):
                    sp({2: "A0", 4: "A1", 6: "B0"}[u])
                exps(u)
                if u > 0:
                    out_high(u - 1)
            probs_high(7)
            if last:
                out_high(7)
                sp("B1")
                return
            rope_high(rb + 7, qo[0][:, 0, 1, :])
            sp("A0")
            rope_high(rb + 8, kT[0][:, 0, :])
            out_high(7)
            sp("A1")
            rope_high(rb + 9, kT[0][:, 1, :])
            sp("B0")
            v_high(g * 2 + 2, 0)
            v_high(g * 2 + 3, 1)
            sp("B1")
            split(None, "Q1", 1, g * (16 * len(BODY) // 2) + 16 * 7, 6 + PIECES * g + 12 + TT)

        split(0, "Q0'", 0, 16, None)
        split(1, "K'", 1, 16, None)
        split(2, "V'", 0, 32, None)
        rope_high(0, qo[0][:, 0, 0, :])
        rope_high(1, qo[0][:, 0, 1, :])
        split(3, "Q1", 1, 32, 2)
        rope_high(2, kT[0][:, 0, :])
        rope_high(3, kT[0][:, 1, :])
        v_high(0, 0)
        v_high(1, 1)
        with act.Fori(0, GROUPS - 1) as g:
            body(g, False)
        body(GROUPS - 1, True)

    @block.vector
    def _(dve):
        link = Links(dve, dve_link)

        def stage(t):
            return prob[:, 0:D] if t % 2 == 0 else rope[:, :, :].rearrange("p a c -> p (a c)")

        def ln_low(n):
            t, k0 = n // 2, 4 * (n % 2)
            dve.wait_ge(ln_hi, n + 1)
            nc.vector.tensor_tensor(xn[1][:, k0:k0 + 4, t * P:(t + 1) * P], ln_bank(score, turned, n),
                                    as32(xn[0][:, k0:k0 + 4, t * P:(t + 1) * P]), ALU.subtract).then_inc(ln_lo, 1)

        for h in range(2):
            ts = slice(h * TPB, (h + 1) * TPB)
            for t in range(h * TPB, (h + 1) * TPB):
                dve.wait_ge(x_in[t], 16)
                row_stats(nc, resid, stats, moments, t, link)
            row_scale_in(nc, moments, lnw, ts, var_ready)
            dve.wait_ge(root_ready, h + 1)
            row_scale_out(nc, lnw, rstd, ts, link)
            for t in range(h * TPB, (h + 1) * TPB):
                if t >= 2:
                    dve.wait_ge(ln_turned, 2 * t - 2)
                nc.vector.tensor_scalar(stage(t), resid[:, t, :], moments[:, t, 0:1], rstd[:, t:t + 1],
                                        ALU.subtract, ALU.mult).then_inc(ln_out, 1)
                if t >= 1:
                    ln_low(2 * t - 2)
                    ln_low(2 * t - 1)
        ln_low(2 * TT - 2)
        ln_low(2 * TT - 1)
        dve.wait_ge(tables_in, 32)

        def rope_products(m, n):
            b = bank[m[1]]
            if not isinstance(n, int) or n > 0:
                dve.wait_ge(rope_done, n)
            dve.wait_ge(piece_done, m[0] + 1)
            nc.vector.tensor_tensor(rope[:, 0, :], b[:], cos[:], ALU.mult)
            nc.vector.tensor_tensor(rope[0:64, 1, :], b[64:128, :], sin[64:128, :], ALU.mult)
            (nc.vector.tensor_tensor(rope[64:128, 1, :], b[0:64, :], sin[0:64, :], ALU.mult)
             .then_inc(rope_parts, 1))

        def rope_low(n, hi, lo):
            dve.wait_ge(rope_hi, n + 1)
            nc.vector.tensor_tensor(lo, rope[:, 0, :], as32(hi), ALU.subtract).then_inc(rope_done, 1)

        def v_stage(m, n, b):
            dve.wait_ge(rope_done, n)
            dve.wait_ge(piece_done, m[0] + 1)
            nc.vector.tensor_copy(rope[:, b, :], bank[m[1]][:]).then_inc(v_staged, 1)

        def v_low(n, b):
            dve.wait_ge(v_hi, n + 1)
            nc.vector.tensor_tensor(vv[1][:, b, :, :], turned[:, b, :].rearrange("p (j c) -> p j c", c=HEAD),
                                    as32(vv[0][:, b, :, :]), ALU.subtract).then_inc(v_done, 1)

        def body(g, last):
            rb, ub = g * ROPED + 4, g * 8
            mb = 6 + PIECES * g if isinstance(g, int) else g * PIECES + 6

            def m(j):
                return mb + j, j % 2

            def probs_low(u):
                for c in range(3):
                    sl = slice(CHUNKS[c][0], CHUNKS[c][0] + CHUNK_WIDTH[c])
                    dve.wait_ge(pT_hi, ub * 3 + (3 * u + c + 1))
                    nc.vector.tensor_tensor(pT[1][:, sl], turned_chunk(turned, mixed, c), as32(pT[0][:, sl]),
                                            ALU.subtract).then_inc(pT_lo, 1)

            def peaks(u):
                for n, i in enumerate(TILE_ORDER):
                    w = P * (i + 1)
                    s, c = SCORE_AT[i]
                    dve.wait_ge(score_done, ub * 4 + (4 * u + TILES_NEEDED[n]))
                    ins = nc.vector.reduce_max(peak[:, i:i + 1], score[:, s, c:c + w], AX.X)
                ins.then_inc(peak_done, 1)
                dve.wait_ge(peak_done, ub + (u + 1))
                nc.vector.tensor_scalar(shift[:], peak[:], -SCALE, None, ALU.mult).then_inc(shift_done, 1)

            def normalise(u):
                dve.wait_ge(exp_done, ub * 4 + (4 * u + 4))
                nc.vector.reciprocal(inv[:], total[:]).then_inc(inv_done, 1)
                dve.wait_ge(inv_done, ub + (u + 1))
                for i in TILE_ORDER:
                    sl = slice(PROB_AT[i], PROB_AT[i] + P * (i + 1))
                    ins = nc.vector.tensor_scalar(prob[:, sl], prob[:, sl], inv[:, i:i + 1], None, ALU.mult)
                ins.then_inc(prob_done, 1)

            def out_low(u):
                dve.wait_ge(o_hi, ub + (u + 1))
                nc.vector.tensor_tensor(qo[1][:, o_place(u // 2), u % 2, :], mixed[:],
                                        as32(qo[0][:, o_place(u // 2), u % 2, :]), ALU.subtract).then_inc(o_lo, 1)

            def add_piece(j, t, half):
                dve.wait_ge(piece_done, mb + (j + 1))
                sl = slice(half * 512, half * 512 + 512)
                nc.vector.tensor_tensor(resid[:, t, sl], bank[j % 2][:], resid[:, t, sl], ALU.add).then_inc(added, 1)

            def q_slot(h):
                return (h // 2 + 1) % HPG, h % 2

            for u in range(8):
                if u > 0:
                    probs_low(u - 1)
                peaks(u)
                if u > 0 and (u < 7 or not last):
                    s, b = q_slot(u - 1)
                    rope_low(rb + (u - 1), qo[0][:, s, b, :], qo[1][:, s, b, :])
                normalise(u)
                if u > 0:
                    out_low(u - 1)
                if u < 6 or not last:
                    rope_products(m(u), rb + u)
            probs_low(7)
            if last:
                out_low(7)
            else:
                rope_low(rb + 7, qo[0][:, 0, 1, :], qo[1][:, 0, 1, :])
                rope_products(m(8), rb + 8)
                out_low(7)
                rope_low(rb + 8, kT[0][:, 0, :], kT[1][:, 0, :])
                rope_products(m(9), rb + 9)
                rope_low(rb + 9, kT[0][:, 1, :], kT[1][:, 1, :])
                v_stage(m(10), rb + 10, 0)
                v_stage(m(11), rb + 10, 1)
                v_low(g * 2 + 2, 0)
            w = first_wo(last)
            for half in range(2):
                for t in range(TT):
                    add_piece(w + half * TT + t, t, half)
                    if half == 0 and t == 0 and not last:
                        v_low(g * 2 + 3, 1)

        dve.sem_inc(added, 1)
        rope_products((0, 0), 0)
        rope_low(0, qo[0][:, 0, 0, :], qo[1][:, 0, 0, :])
        rope_products((1, 1), 1)
        rope_low(1, qo[0][:, 0, 1, :], qo[1][:, 0, 1, :])
        rope_products((2, 0), 2)
        rope_low(2, kT[0][:, 0, :], kT[1][:, 0, :])
        rope_products((3, 1), 3)
        rope_low(3, kT[0][:, 1, :], kT[1][:, 1, :])
        v_stage((4, 0), 4, 0)
        v_stage((5, 1), 4, 1)
        v_low(0, 0)
        v_low(1, 1)
        with dve.Fori(0, GROUPS - 1) as g:
            body(g, False)
        body(GROUPS - 1, True)

    @block.tensor
    def _(pe):
        PASSES = ((0, 0), (0, 1), (1, 0))

        pe.wait_ge(ident_made, 3)
        for n in range(2 * TT):
            t, k0 = n // 2, 4 * (n % 2)
            if n % 2 == 0:
                pe.wait_ge(ln_out, t + 1)
            if n >= 4:
                pe.wait_ge(ln_lo, n - 3)
            src = prob[:, 0:D] if t % 2 == 0 else rope[:, :, :].rearrange("p a c -> p (a c)")
            dst = ln_bank(score, turned, n)
            for k in range(4):
                ins = nc.tensor.transpose(dst[:, k, :], src[:, (k0 + k) * P:(k0 + k + 1) * P], ident[:])
            ins.then_inc(ln_turned, 1)

        def project(par, name, b, n, steps=range(24)):
            place = PLACE[name]
            for s in steps:
                k, (a, c) = s // 3, PASSES[s % 3]
                if s == 0:
                    if b == 0:
                        pe.wait_ge(block_lo, n + 1)
                ins = nc.tensor.matmul(bank[par][:], ring[a][:, place, k * P:(k + 1) * P],
                                       xn[c][:, k, b * H:(b + 1) * H], start=(s == 0), stop=(s == 23))
                if s == 23:
                    ins.then_inc(piece_done, 1)

        def turn_values(n, b):
            pe.wait_ge(v_staged, n + 1)
            for j in range(TPB):
                ins = nc.tensor.transpose(turned[:, b, j * P:(j + 1) * P], rope[:, b, j * P:(j + 1) * P], ident[:])
            ins.then_inc(v_turned, 1)

        def body(g, last):
            rb, ub = g * ROPED + 4, g * 8

            def scores(u):
                h, b = u // 2, u % 2
                pe.wait_ge(rope_done, rb - 1 + u)
                if u > 0:
                    pe.wait_ge(exp_done, ub * 4 + 4 * u)
                for i in TILE_ORDER:
                    w = P * (i + 1)
                    s, c = SCORE_AT[i]
                    dst = score[:, s, c:c + w]
                    for p, (a, e) in enumerate(PASSES):
                        nc.tensor.matmul(dst, qo[a][:, h, b, i * P:(i + 1) * P], kT[e][:, b, 0:w],
                                         start=(p == 0), stop=False)
                    nc.tensor.matmul(score[:, s, c + w - P:c + w], identb[:], maskb[:],
                                     start=False, stop=True).then_inc(score_done, 1)

            def turn_probs(u):
                pe.wait_ge(prob_done, ub + (u + 1))
                if u > 0:
                    pe.wait_ge(pT_lo, ub * 3 + 3 * u)
                    pe.wait_ge(o_lo, ub + u)
                for c in range(3):
                    dst = turned_chunk(turned, mixed, c)
                    for j in CHUNKS[c][1]:
                        for i in range(j, TPB):
                            col = KEYS_AT[j] - CHUNKS[c][0] + (i - j) * P
                            ins = nc.tensor.transpose(dst[:, col:col + P],
                                                      prob[:, PROB_AT[i] + j * P:PROB_AT[i] + (j + 1) * P], ident[:])
                    ins.then_inc(turn_done, 1)

            def mix(u):
                b = u % 2
                pe.wait_ge(v_done, g * 2 + (1 + b))
                pe.wait_ge(pT_lo, ub * 3 + (3 * u + 3))
                for j in range(TPB):
                    w = H - j * P
                    for p, (a, c) in enumerate(PASSES):
                        ins = nc.tensor.matmul(mixed[:, j * P:H], vv[a][:, b, j, :],
                                               pT[c][:, KEYS_AT[j]:KEYS_AT[j] + w],
                                               start=(j == 0 and p == 0), stop=(j == TPB - 1 and p == 2))
                ins.then_inc(mix_done, 1)

            def filler(u, steps):
                name = ("Q1", "Q1", "Q2", "Q2", "Q3", "Q3", "Q0'", "Q0'", "K'", "K'", "V'", "V'")[u]
                n = number(g, name, True) if last else g * len(BODY) + (3 + BODY.index(name))
                if steps[0] == 0:
                    if u < 2:
                        pe.wait_ge(added, g * (2 * TT) + 1)
                    else:
                        pe.wait_ge(rope_parts, rb + (u - 1))
                project(u % 2, name, u % 2, n, steps)

            def out_part(j, t, half, pairs):
                if pairs[0] == 0:
                    before = j - 2 - first_wo(last)
                    if before >= 0:
                        pe.wait_ge(added, g * (2 * TT) + (before + 2))
                    elif last:
                        pe.wait_ge(rope_parts, rb + (j - 1))
                    else:
                        pe.wait_ge(v_staged, g * 2 + (before + 5))
                for pair in pairs:
                    name = "AB"[half] + str(pair)
                    if t == 0:
                        n = number(g, name, True) if last else g * len(BODY) + (3 + BODY.index(name))
                        pe.wait_ge(block_lo, n + 1)
                    for k in (2 * pair, 2 * pair + 1):
                        for p, (a, c) in enumerate(PASSES):
                            ins = nc.tensor.matmul(
                                bank[j % 2][:], qo[a][:, o_place(k), t // TPB, (t % TPB) * P:(t % TPB + 1) * P],
                                ring[c][:, PLACE[name], (k % 2) * 512:(k % 2) * 512 + 512],
                                start=(k == 0 and p == 0), stop=(k == HPG - 1 and p == 2))
                if pairs[-1] == 1:
                    ins.then_inc(piece_done, 1)

            for u in range(8):
                scores(u)
                some = u < 6 or not last
                if some:
                    filler(u, range(0, 6))
                if u > 0:
                    mix(u - 1)
                if some:
                    filler(u, range(6, 24))
                turn_probs(u)
            if not last:
                filler(8, range(24))
            mix(7)
            if not last:
                filler(9, range(24))
                filler(10, range(24))
                filler(11, range(24))
                turn_values(g * 2 + 2, 0)
            w = first_wo(last)
            pe.wait_ge(o_lo, ub + 8)
            for half in range(2):
                out_part(w + half * TT, 0, half, (0,))
                out_part(w + half * TT + 1, 1, half, (0,))
                out_part(w + half * TT, 0, half, (1,))
                out_part(w + half * TT + 1, 1, half, (1,))
                if half == 0 and not last:
                    turn_values(g * 2 + 3, 1)
                for t in range(2, TT):
                    out_part(w + half * TT + t, t, half, (0, 1))

        pe.wait_ge(ln_lo, TT)
        project(0, "Q0'", 0, 0)
        pe.wait_ge(ln_lo, 2 * TT)
        project(1, "Q0'", 1, 0)
        pe.wait_ge(rope_parts, 1)
        project(0, "K'", 0, 1)
        pe.wait_ge(rope_parts, 2)
        project(1, "K'", 1, 1)
        pe.wait_ge(rope_parts, 3)
        project(0, "V'", 0, 2)
        pe.wait_ge(rope_parts, 4)
        project(1, "V'", 1, 2)
        turn_values(0, 0)
        turn_values(1, 1)
        with pe.Fori(0, GROUPS - 1) as g:
            body(g, False)
        body(GROUPS - 1, True)


def ln_bank(score, turned, n):
    b = score[:, n % 4, :] if n % 4 < 3 else turned[:, 0, :]
    return b.rearrange("p (k c) -> p k c", c=P)


def turned_chunk(turned, mixed, c):
    return turned[:, c, :] if c < 2 else mixed[:, 0:256]


def context(nc, held, es, ctx_in, x1s, x1z, x2s, x2z, A_w, Wr, aT, rT,
            resid, ident, identb, stats, moments, rstd, lnw, KT, TT, TPB, H):
    sb, psum, sem = held
    D = KT * P
    NB = TT // TPB
    NT = NB * KT
    NC = 4

    scal = sb("scal", [P, 4], F32)
    calc = sb("calc", [P, 12], F32)
    one = sb("one", [P, P], BF16)
    craw = sb("craw", [P, NC, D], F32)
    q2 = sb("q2", [P, NB, KT, D], BF16)
    q1 = sb("q1", [P, 2, D], BF16)
    q1T = sb("q1T", [P, KT, TT * P], BF16)
    norm = sb("norm", [P, 2, D], F32)
    colterm = sb("colterm", [P, NB, D], F32)
    rowterm = sb("rowterm", [P, TT], F32)
    araw = sb("araw", [P, 4, D], F32)
    rraw = sb("rraw", [ROUTER, D], F32)

    ab = [psum(f"ab{n}", [P, 4, P], F32) for n in range(2)]
    qb = [psum(f"qb{n}", [P, KT, P], BF16) for n in range(2)]
    cb = [psum(f"cb{n}", [P, 512], F32) for n in range(2)]
    mb = [psum(f"mb{n}", [P, 512], F32) for n in range(2)]

    scal_in = sem("scal_in")
    ctx_sem = [sem(f"ctx_in{n}") for n in range(NC)]
    w_in = [sem(f"w_in{n}") for n in range(5)]
    ones_made, calc_done = sem("ones_made"), sem("calc_done")
    dve_link, var_ready, root_ready = sem("dve_link2"), sem("var_ready2"), sem("root_ready2")
    c_scaled, c_quant = sem("c_scaled"), sem("c_quant")
    normed, n_scaled, n_quant = sem("normed"), sem("n_scaled"), sem("n_quant")
    q_turned, q_copied = sem("q_turned"), sem("q_copied")
    w_turned, w_hi, w_lo = sem("w_turned"), sem("w_hi"), sem("w_lo")
    col_summed, col_done = sem("col_summed"), sem("col_done")
    row_summed = sem("row_summed")
    mul_done, mul_read = sem("mul_done"), sem("mul_read")

    S1, Z1, S2, Z2 = (scal[:, n:n + 1] for n in range(4))
    R1, R2, Z1M, Z2M, S12, COL, ROW, BOTH, T0, T1 = (calc[:, n:n + 1] for n in range(10))
    block = es.enter_context(nc.Block())

    @block.sync
    def _(sp):
        for n, v in enumerate((x1s, x1z, x2s, x2z)):
            sp.dma_start(scal[:, n:n + 1], v.rearrange("(a b) -> a b", a=1).to_broadcast([P, 1])).then_inc(scal_in, 16)
        for n in range(4):
            sp.dma_start(craw[:, n, :], ctx_in[n // KT, (n % KT) * P:(n % KT + 1) * P, :]).then_inc(ctx_sem[n], 16)
        for n in range(4):
            sp.dma_start(araw[:, n, :], A_w[n * P:(n + 1) * P, :]).then_inc(w_in[n], 16)
        sp.dma_start(rraw[:], Wr).then_inc(w_in[4], 16)
        for n in range(NC, NT):
            sp.wait_ge(c_quant, n - NC + 1)
            sp.dma_start(craw[:, n % NC, :],
                         ctx_in[n // KT, (n % KT) * P:(n % KT + 1) * P, :]).then_inc(ctx_sem[n % NC], 16)

    @block.gpsimd
    def _(pool):
        nc.gpsimd.memset(one[:], 1.0).then_inc(ones_made, 1)
        nc.gpsimd.memset(rT[0][:].bitcast(F32), 0.0).then_inc(ones_made, 1)
        nc.gpsimd.memset(rT[1][:].bitcast(F32), 0.0).then_inc(ones_made, 1)

    @block.scalar
    def _(act):
        def scale_ctx(n):
            act.wait_ge(ctx_sem[n % NC], 16 * (n // NC + 1))
            nc.scalar.activation(craw[:, n % NC, :], craw[:, n % NC, :], ACT.Identity, bias=Z2, scale=R2).then_inc(c_scaled, 1)

        def w_high(n):
            act.wait_ge(w_turned, n + 1)
            if n < 8:
                nc.scalar.copy(aT[0][:, 4 * (n % 2):4 * (n % 2) + 4, (n // 2) * P:(n // 2 + 1) * P],
                               ab[n % 2][:]).then_inc(w_hi, 1)
            else:
                act.wait_ge(ones_made, 3)
                nc.scalar.copy(rT[0][:, :, 0:ROUTER], router_bank(ab[0], KT)).then_inc(w_hi, 1)

        for h in range(2):
            act.wait_ge(var_ready, h + 1)
            nc.scalar.activation(lnw[:, 1, h * TPB:(h + 1) * TPB], lnw[:, 0, h * TPB:(h + 1) * TPB],
                                 ACT.Sqrt).then_inc(root_ready, 1)
        act.wait_ge(calc_done, 1)
        for t in range(TT):
            w_high(t)
            scale_ctx(2 * t)
            act.wait_ge(normed, t + 1)
            nc.scalar.activation(norm[:, t % 2, :], norm[:, t % 2, :], ACT.Identity, bias=Z1, scale=R1).then_inc(n_scaled, 1)
            scale_ctx(2 * t + 1)
            act.wait_ge(q_turned, t + 1)
            nc.scalar.copy(q1T[:, :, t * P:(t + 1) * P], qb[t % 2][:]).then_inc(q_copied, 1)
        w_high(8)

    @block.vector
    def _(dve):
        link = Links(dve, dve_link)
        for t in range(TT):
            row_stats(nc, resid, stats, moments, t, link)
            if t % TPB == TPB - 1:
                row_scale_in(nc, moments, lnw, slice(t - TPB + 1, t + 1), var_ready)
        dve.wait_ge(scal_in, 64)
        nc.vector.reciprocal(R1, S1)
        nc.vector.reciprocal(R2, S2)
        link(nc.vector.tensor_scalar(Z1M, Z1, -MIDDLE, None, ALU.add))
        link(nc.vector.tensor_scalar(Z2M, Z2, -MIDDLE, None, ALU.add))
        link(nc.vector.tensor_tensor(S12, S1, S2, ALU.mult))
        link(nc.vector.tensor_tensor(T0, Z1M, S12, ALU.mult))
        link(nc.vector.tensor_tensor(T1, Z2M, S12, ALU.mult))
        nc.vector.tensor_scalar(COL, T0, -1.0, None, ALU.mult)
        nc.vector.tensor_scalar(ROW, T1, -1.0, None, ALU.mult)
        link(nc.vector.tensor_tensor(BOTH, T0, Z2M, ALU.mult))
        nc.vector.tensor_scalar(BOTH, BOTH, float(D), None, ALU.mult).then_inc(calc_done, 1)
        dve.wait_ge(root_ready, 2)
        row_scale_out(nc, lnw, rstd, slice(0, TT), link)

        def to_integer(dst, v, done, wait=()):
            link(nc.vector.tensor_scalar(v, v, MAGIC, MAGIC, ALU.add, ALU.max))
            for s, n in wait:
                dve.wait_ge(s, n)
            nc.vector.tensor_scalar(dst, v, MAGIC + 255.0, MAGIC + MIDDLE, ALU.min, ALU.subtract).then_inc(done, 1)

        def quant_ctx(n):
            dve.wait_ge(c_scaled, n + 1)
            to_integer(q2[:, n // KT, n % KT, :], craw[:, n % NC, :], c_quant)

        def w_low(n):
            dve.wait_ge(w_hi, n + 1)
            if n < 8:
                d = (slice(None), slice(4 * (n % 2), 4 * (n % 2) + 4), slice((n // 2) * P, (n // 2 + 1) * P))
                nc.vector.tensor_tensor(aT[1][d], ab[n % 2][:], aT[0][d].bitcast(F32), ALU.subtract).then_inc(w_lo, 1)
            else:
                nc.vector.tensor_tensor(rT[1][:, :, 0:ROUTER], router_bank(ab[0], KT),
                                        rT[0][:, :, 0:ROUTER].bitcast(F32), ALU.subtract).then_inc(w_lo, 1)

        for t in range(TT):
            if t >= 2:
                dve.wait_ge(n_quant, t - 1)
            nc.vector.tensor_scalar(norm[:, t % 2, :], resid[:, t, :], moments[:, t, 0:1], rstd[:, t:t + 1],
                                    ALU.subtract, ALU.mult).then_inc(normed, 1)
            w_low(t)
            quant_ctx(2 * t)
            dve.wait_ge(n_scaled, t + 1)
            to_integer(q1[:, t % 2, :], norm[:, t % 2, :], n_quant,
                       ((q_turned, t - 1),) if t >= 2 else ())
            quant_ctx(2 * t + 1)
        w_low(8)
        for n in range(2 * NB):
            dve.wait_ge(col_summed, n + 1)
            ins = nc.vector.tensor_scalar(colterm[:, n // 2, (n % 2) * 512:(n % 2) * 512 + 512], cb[n % 2][:],
                                          COL, BOTH, ALU.mult, ALU.add)
            ins.then_inc(col_done, 1)
        dve.wait_ge(row_summed, 1)
        link(nc.vector.tensor_scalar(rowterm[:], ab[0][:, 0, 0:2 * TT:2], ROW, None, ALU.mult))
        dve.wait_ge(col_done, 2 * NB)

        def add_terms(t):
            link(nc.vector.scalar_tensor_tensor(resid[:, t, :], colterm[:, t // TPB, :], rowterm[:, t:t + 1],
                                                resid[:, t, :], ALU.add, ALU.add))

        for t in range(TT):
            add_terms(t)
            for half in range(2):
                m = 2 * t + half
                sl = slice(half * 512, half * 512 + 512)
                dve.wait_ge(mul_done, m + 1)
                nc.vector.scalar_tensor_tensor(resid[:, t, sl], mb[m % 2][:], S12, resid[:, t, sl],
                                               ALU.mult, ALU.add).then_inc(mul_read, 1)

    @block.tensor
    def _(pe):
        def turn_w(n):
            pe.wait_ge(w_in[n // 2], 16)
            if n >= 2:
                pe.wait_ge(w_lo, n - 1)
            if n < 8:
                for k in range(4):
                    kk = 4 * (n % 2) + k
                    ins = nc.tensor.transpose(ab[n % 2][:, k, :], araw[:, n // 2, kk * P:(kk + 1) * P], ident[:])
            else:
                for k in range(KT):
                    ins = nc.tensor.transpose(router_bank(ab[0], KT)[:, k, :], rraw[:, k * P:(k + 1) * P],
                                              ident[0:ROUTER, 0:ROUTER])
            ins.then_inc(w_turned, 1)

        turn_w(0)
        turn_w(1)
        pe.wait_ge(ones_made, 1)
        for t in range(TT):
            if t + 2 < 9:
                turn_w(t + 2)
            pe.wait_ge(n_quant, t + 1)
            if t >= 2:
                pe.wait_ge(q_copied, t - 1)
            for k in range(KT):
                ins = nc.tensor.transpose(qb[t % 2][:, k, :], q1[:, t % 2, k * P:(k + 1) * P], identb[:])
            ins.then_inc(q_turned, 1)
        for n in range(2 * NB):
            pe.wait_ge(c_quant, KT * (n // 2 + 1))
            if n >= 2:
                pe.wait_ge(col_done, n - 1)
            for k in range(KT):
                ins = nc.tensor.matmul(cb[n % 2][:], one[:], q2[:, n // 2, k, (n % 2) * 512:(n % 2) * 512 + 512],
                                       start=(k == 0), stop=(k == KT - 1))
            ins.then_inc(col_summed, 1)
        pe.wait_ge(w_lo, 9)
        pe.wait_ge(q_copied, TT)
        for t in range(TT):
            for k in range(KT):
                ins = nc.tensor.matmul(ab[0][:, 0, 2 * t:2 * t + 2], q1T[:, k, t * P:(t + 1) * P], one[:, 0:2],
                                       start=(k == 0), stop=(k == KT - 1))
        ins.then_inc(row_summed, 1)
        for t in range(TT):
            for half in range(2):
                m = 2 * t + half
                if m >= 2:
                    pe.wait_ge(mul_read, m - 1)
                for k in range(KT):
                    ins = nc.tensor.matmul(mb[m % 2][:], q1T[:, k, t * P:(t + 1) * P],
                                           q2[:, t // TPB, k, half * 512:half * 512 + 512],
                                           start=(k == 0), stop=(k == KT - 1))
                ins.then_inc(mul_done, 1)


def router_bank(bank, KT):
    return bank[:, 0, :].rearrange("p (k r) -> p k r", k=KT)


def experts(nc, held, es, out_t, B_w, keys, aT, rT,
            resid, ident, identb, stats, moments, rstd, lnw, KT, TT, TPB, H):
    sb, psum, sem = held
    D = KT * P
    N = EXPERTS * RANK
    NT = N // P
    PASSES = ((0, 0), (0, 1), (1, 0))

    xn = [sb(f"xe_{n}", [P, KT, TT * P], F32R) for n in ("hi", "lo")]
    bT = [sb(f"bT_{n}", [P, NT, D], F32R) for n in ("hi", "lo")]
    braw = sb("braw", [P, 4, N], F32)
    norm = sb("norme", [P, 2, D], F32)
    zg = sb("zg", [P, 2, N], F32)
    zT = [sb(f"zT_{n}", [P, NT, P], F32R) for n in ("hi", "lo")]
    kraw = sb("kraw", [EXPERTS, ROUTER], F32)
    keysT = sb("keysT", [ROUTER, EXPERTS], F32)
    seen = sb("seen", [P, TT, EXPERTS], F32)
    left = sb("left", [P, TT, EXPERTS], F32)
    weight = sb("weight", [P, TT, EXPERTS], F32)
    top = sb("top", [P, TT, 2, 8], F32)
    gsum = sb("gsum", [P, 2, TT], F32)
    qT = norm[0:ROUTER, 0, :]

    lb = [psum(f"lb{n}", [P, 4, P], F32) for n in range(2)]
    zb = [psum(f"zb{n}", [P, N], F32) for n in range(2)]
    ob = [psum(f"ob{n}", [P, 512], F32) for n in range(2)]
    sbk = psum("sbk", [P, TT, EXPERTS], F32)
    kb = psum("kb", [P, 512], F32)

    dve_link, var_ready, root_ready = sem("dve_link3"), sem("var_ready3"), sem("root_ready3")
    b_in = [sem(f"b_in{n}") for n in range(4)]
    k_in = sem("k_in")
    normed, turned, hi, lo = sem("normed3"), sem("turned3"), sem("hi3"), sem("lo3")
    k_turned, k_done = sem("k_turned"), sem("k_done")
    q_done, q_read = sem("q_done3"), sem("q_read3")
    s_done, s_read = sem("s_done"), sem("s_read")
    shifted, exped = sem("shifted"), sem("exped")
    z_done, z_gated = sem("z_done"), sem("z_gated")
    o_done, o_added = sem("o_done"), sem("o_added")
    stored = sem("stored")
    block = es.enter_context(nc.Block())

    LN_FILLS, B_FILLS = 2 * TT, KT

    def target(n):
        if n < LN_FILLS:
            t, k0 = n // 2, 4 * (n % 2)
            return [x[:, k0:k0 + 4, t * P:(t + 1) * P] for x in xn]
        n -= LN_FILLS
        if n < B_FILLS:
            return [x[:, :, n * P:(n + 1) * P] for x in bT]
        return [x[:] for x in zT]

    @block.sync
    def _(sp):
        for n in range(4):
            sp.dma_start(braw[:, n, :], B_w[n * P:(n + 1) * P, :]).then_inc(b_in[n], 16)
        sp.dma_start(kraw[:], keys).then_inc(k_in, 16)
        for n in range(4, KT):
            sp.wait_ge(turned, LN_FILLS + n - 3)
            sp.dma_start(braw[:, n % 4, :], B_w[n * P:(n + 1) * P, :]).then_inc(b_in[n % 4], 16)
        for t in range(TT):
            sp.wait_ge(o_added, 2 * t + 2)
            sp.dma_start(out_t[t], resid[:, t, :]).then_inc(stored, 16)
        sp.wait_ge(stored, 16 * TT)

    @block.scalar
    def _(act):
        for h in range(2):
            act.wait_ge(var_ready, h + 1)
            nc.scalar.activation(lnw[:, 1, h * TPB:(h + 1) * TPB], lnw[:, 0, h * TPB:(h + 1) * TPB],
                                 ACT.Sqrt).then_inc(root_ready, 1)

        def high(n):
            act.wait_ge(turned, n + 1)
            if n > LN_FILLS + B_FILLS:
                act.wait_ge(o_done, 2 * (n - LN_FILLS - B_FILLS))
            nc.scalar.copy(target(n)[0], lb[n % 2][:]).then_inc(hi, 1)

        for n in range(LN_FILLS + B_FILLS):
            high(n)
        act.wait_ge(k_turned, 1)
        nc.scalar.copy(keysT[:], kb[0:ROUTER, 0:EXPERTS]).then_inc(k_done, 1)
        for b in range(2):
            act.wait_ge(q_done, b + 1)
            nc.scalar.copy(qT[:, b * 512:(b + 1) * 512], ob[b][0:ROUTER, :]).then_inc(q_read, 1)
        act.wait_ge(shifted, 1)
        nc.scalar.activation(weight[:], weight[:], ACT.Exp).then_inc(exped, 1)
        for t in range(TT):
            high(LN_FILLS + B_FILLS + t)

    @block.vector
    def _(dve):
        link = Links(dve, dve_link)

        def low(n):
            dve.wait_ge(hi, n + 1)
            h, l = target(n)
            nc.vector.tensor_tensor(l, lb[n % 2][:], h.bitcast(F32), ALU.subtract).then_inc(lo, 1)

        for t in range(TT):
            row_stats(nc, resid, stats, moments, t, link)
            if t % TPB == TPB - 1:
                row_scale_in(nc, moments, lnw, slice(t - TPB + 1, t + 1), var_ready)
        dve.wait_ge(root_ready, 2)
        row_scale_out(nc, lnw, rstd, slice(0, TT), link)
        for t in range(TT):
            if t >= 2:
                dve.wait_ge(turned, 2 * t - 2)
            nc.vector.tensor_scalar(norm[:, t % 2, :], resid[:, t, :], moments[:, t, 0:1], rstd[:, t:t + 1],
                                    ALU.subtract, ALU.mult).then_inc(normed, 1)
            if t >= 1:
                low(2 * t - 2)
                low(2 * t - 1)
        for n in range(2 * TT - 2, LN_FILLS + B_FILLS):
            low(n)
        dve.wait_ge(s_done, 1)
        link(nc.vector.tensor_copy(seen[:], sbk[:]))
        for t in range(TT):
            last = nc.vector.max(top[:, t, 0, :], seen[:, t, :])
        link(last)
        for t in range(TT):
            last = nc.vector.match_replace(left[:, t, :], top[:, t, 0, :], seen[:, t, :], NEVER)
        link(last)
        for t in range(TT):
            last = nc.vector.max(top[:, t, 1, :], left[:, t, :])
        link(last)
        nc.vector.tensor_tensor(weight[:], seen[:], top[:, :, 0, 0:1].to_broadcast([P, TT, EXPERTS]),
                                ALU.subtract).then_inc(shifted, 1)
        for t in range(TT):
            last = nc.vector.match_replace(left[:, t, :], top[:, t, 1, :], left[:, t, :], NEVER)
        link(last)
        link(nc.vector.tensor_scalar(left[:], left[:], NEVER, None, ALU.is_equal))
        dve.wait_ge(exped, 1)
        link(nc.vector.tensor_tensor(weight[:], weight[:], left[:], ALU.mult))
        link(nc.vector.reduce_sum(gsum[:, 0, :], weight[:], AX.X))
        link(nc.vector.reciprocal(gsum[:, 1, :], gsum[:, 0, :]))
        link(nc.vector.tensor_scalar(gsum[:, 0, :], gsum[:, 1, :], SCALING, None, ALU.mult))
        link(nc.vector.tensor_tensor(weight[:], weight[:], gsum[:, 0, :].unsqueeze(2).to_broadcast([P, TT, EXPERTS]), ALU.mult))

        def gate(t):
            dve.wait_ge(z_done, t + 1)
            if t >= 2:
                dve.wait_ge(turned, LN_FILLS + B_FILLS + t - 1)
            nc.vector.tensor_tensor(zg[:, t % 2, :].rearrange("p (e r) -> p e r", r=RANK),
                                    zb[t % 2][:].rearrange("p (e r) -> p e r", r=RANK),
                                    weight[:, t, :].unsqueeze(2).to_broadcast([P, EXPERTS, RANK]),
                                    ALU.mult).then_inc(z_gated, 1)

        def add_out(t):
            for half in range(2):
                m = 2 * t + half
                sl = slice(half * 512, half * 512 + 512)
                dve.wait_ge(o_done, m + 1)
                nc.vector.tensor_tensor(resid[:, t, sl], ob[m % 2][:], resid[:, t, sl], ALU.add).then_inc(o_added, 1)

        gate(0)
        for t in range(TT):
            if t + 1 < TT:
                gate(t + 1)
            low(LN_FILLS + B_FILLS + t)
            add_out(t)

    @block.tensor
    def _(pe):
        def free(n):
            if n >= 2:
                pe.wait_ge(lo, n - 1)

        for t in range(TT):
            pe.wait_ge(normed, t + 1)
            for n in (2 * t, 2 * t + 1):
                free(n)
                for k in range(4):
                    kk = 4 * (n % 2) + k
                    ins = nc.tensor.transpose(lb[n % 2][:, k, :], norm[:, t % 2, kk * P:(kk + 1) * P], ident[:])
                ins.then_inc(turned, 1)
        for o in range(KT):
            n = LN_FILLS + o
            pe.wait_ge(b_in[o % 4], 16 * (o // 4 + 1))
            free(n)
            for j in range(NT):
                ins = nc.tensor.transpose(lb[n % 2][:, j, :], braw[:, o % 4, j * P:(j + 1) * P], ident[:])
            ins.then_inc(turned, 1)
        pe.wait_ge(k_in, 16)
        nc.tensor.transpose(kb[0:ROUTER, 0:EXPERTS], kraw[:], ident[0:EXPERTS, 0:EXPERTS]).then_inc(k_turned, 1)
        pe.wait_ge(lo, LN_FILLS)
        for b in range(2):
            for k in range(KT):
                for p, (a, c) in enumerate(PASSES):
                    ins = nc.tensor.matmul(ob[b][:], rT[a][:, k, :], xn[c][:, k, b * 512:(b + 1) * 512],
                                           start=(k == 0 and p == 0), stop=(k == KT - 1 and p == 2))
            ins.then_inc(q_done, 1)
        pe.wait_ge(k_done, 1)
        pe.wait_ge(q_read, 2)
        for t in range(TT):
            ins = nc.tensor.matmul(sbk[:, t, :], qT[:, t * P:(t + 1) * P], keysT[:], start=True, stop=True)
        ins.then_inc(s_done, 1)

        def hidden(t):
            if t >= 2:
                pe.wait_ge(z_gated, t - 1)
            for k in range(KT):
                for p, (a, c) in enumerate(PASSES):
                    ins = nc.tensor.matmul(zb[t % 2][:], xn[a][:, k, t * P:(t + 1) * P], aT[c][:, k, :],
                                           start=(k == 0 and p == 0), stop=(k == KT - 1 and p == 2))
            ins.then_inc(z_done, 1)

        hidden(0)
        hidden(1)
        for t in range(TT):
            n = LN_FILLS + B_FILLS + t
            pe.wait_ge(z_gated, t + 1)
            free(n)
            for j in range(NT):
                ins = nc.tensor.transpose(lb[n % 2][:, j, :], zg[:, t % 2, j * P:(j + 1) * P], ident[:])
            ins.then_inc(turned, 1)
            if t + 2 < TT:
                hidden(t + 2)
            pe.wait_ge(lo, n + 1)
            for half in range(2):
                m = 2 * t + half
                if m >= 2:
                    pe.wait_ge(o_added, m - 1)
                for j in range(NT):
                    for p, (a, c) in enumerate(PASSES):
                        ins = nc.tensor.matmul(ob[m % 2][:], zT[a][:, j, :], bT[c][:, j, half * 512:half * 512 + 512],
                                               start=(j == 0 and p == 0), stop=(j == NT - 1 and p == 2))
                ins.then_inc(o_done, 1)


def rope_tables():
    inv_freq = (np.float32(1.0) / np.power(np.float32(ROPE_THETA), np.arange(0, HEAD, 2, dtype=np.float32) / np.float32(HEAD))).astype(np.float32)
    freqs = np.outer(np.arange(512, dtype=np.float32), inv_freq).astype(np.float32)
    cos = np.cos(freqs).T
    sin = np.sin(freqs).T
    return (np.ascontiguousarray(np.concatenate([cos, cos]), np.float32),
            np.ascontiguousarray(np.concatenate([sin, -sin]), np.float32))


_INS = ["x", "ctx_4096", "L0_attn_Wq", "L0_attn_Wk", "L0_attn_Wv", "L0_attn_Wo", "L0_xattn_x1_scale",
        "L0_xattn_x1_zp", "L0_xattn_x2_scale", "L0_xattn_x2_zp", "L0_ffn_A_w", "L0_ffn_B_w",
        "L0_ffn_Wq_w", "L0_ffn_keys"]


def kernel(**inputs):
    import concourse.bacc as bacc
    from concourse.bass_utils import run_bass_kernel_spmd

    nc = bacc.Bacc("TRN2", target_bir_lowering=False, num_devices=1, **BACC)
    arrays = {f"in_{n}": np.ascontiguousarray(inputs[n]) for n in _INS}
    arrays["in_cos"], arrays["in_sin"] = rope_tables()
    args = [nc.dram_tensor(n, a.shape, mybir.dt.from_np(a.dtype), kind="ExternalInput").ap() for n, a in arrays.items()]
    x = arrays["in_x"]
    out = nc.dram_tensor("out", x.shape, F32, kind="ExternalOutput").ap()
    build(nc, *args, out)
    r = run_bass_kernel_spmd(nc, [arrays], core_ids=[0])
    return r.results[0]["out"]
```

```python
from contextlib import ExitStack

import numpy as np

import concourse.bass as bass
from concourse import mybir

BACC = {"dynamic_dma_scratch_size": 2048}
P = 128
ALU = mybir.AluOpType
ACT = mybir.ActivationFunctionType
AX = mybir.AxisListType
F32 = mybir.dt.float32
F32R = mybir.dt.float32r
BF16 = mybir.dt.bfloat16

HEAD = 128
GROUPS = 8
HPG = 4
ROPE_THETA = 10000.0
EPS = 1e-5
EXPERTS, RANK, TOP_K, ROUTER = 64, 8, 16, 16
SCALING = 32 / TOP_K
MAGIC = 1.5 * 2.0 ** 23
MIDDLE = 128.0
NEVER = -3.0e38
MASKED = -1.0e30

BODY = ["Q1", "Q2", "Q3", "Q0'", "K'", "V'", "A0", "A1", "B0", "B1"]
LAST = ["Q1", "Q2", "Q3", "A0", "A1", "B0", "B1"]
FIRST = ["Q0'", "K'", "V'"]
PLACE = dict(zip(BODY, [2, 0, 1, 2, 0, 1, 2, 0, 1, 0]))
PIECES = 28
ROPED = 10
SCORE_AT = {3: (0, 0), 2: (1, 0), 1: (2, 0), 0: (1, 384)}
PROB_AT = {3: 0, 2: 512, 1: 896, 0: 1152}
TILE_ORDER = (3, 2, 0, 1)
TILES_NEEDED = (1, 3, 3, 4)
KEYS_AT = {0: 0, 1: 512, 3: 896, 2: 1024}
CHUNKS = ((0, (0,)), (512, (1, 3)), (1024, (2,)))
CHUNK_WIDTH = (512, 512, 256)


def build(nc, x, ctx_in, Wq, Wk, Wv, Wo, x1s, x1z, x2s, x2z, A_w, B_w, Wr, keys, cos_in, sin_in, out,
          stages=3):
    NB, S, D = x.shape
    KT = D // P
    TT = NB * S // P
    TPB = TT // NB
    H = S

    x_t = x.rearrange("b (t p) d -> (b t) p d", p=P)
    out_t = out.rearrange("b (t p) d -> (b t) p d", p=P)

    def hold(es):
        def sb(name, shape, dt):
            return es.enter_context(nc.sbuf_tensor(name, shape, dt))

        def ps(name, shape, dt):
            return es.enter_context(nc.psum_tensor(name, shape, dt))

        def sem(name):
            return es.enter_context(nc.semaphore(name))
        return sb, ps, sem

    with ExitStack() as whole:
        sb, _, _ = hold(whole)
        resid = sb("resid", [P, TT, D], F32)
        ident = sb("ident", [P, P], F32)
        identb = sb("identb", [P, P], BF16)
        stats = sb("stats", [P, TT, 2, 6], F32)
        moments = sb("moments", [P, TT, 2], F32)
        rstd = sb("rstd", [P, TT], F32)
        lnw = sb("lnw", [P, 4, TT], F32)

        mean_rstd = sb("mean_rstd", [P, TT], F32)
        scal = sb("scal", [P, 4], F32)
        calc = sb("calc", [P, 10], F32)
        q2_dram = nc.dram_tensor("q2_dram", [NB * D, D], BF16, kind="Internal").ap()
        shared = (resid, ident, identb, stats, moments, rstd, lnw, mean_rstd, scal, calc, KT, TT, TPB, H)

        with ExitStack() as es:
            attention(nc, hold(es), es, x_t, Wq, Wk, Wv, Wo, cos_in, sin_in, (x1s, x1z, x2s, x2z),
                      ctx_in.rearrange("b k n -> (b k) n"), q2_dram, *shared)
        if stages == 1:
            store(nc, hold, out_t, resid, TT)
            return
        with ExitStack() as es:
            mix_and_experts(nc, hold(es), es, out_t, q2_dram, A_w, B_w, Wr, keys, *shared)


def store(nc, hold, out_t, resid, TT):
    with ExitStack() as es:
        _, _, sem = hold(es)
        stored = sem("stored")
        block = es.enter_context(nc.Block())

        @block.sync
        def _(sp):
            for t in range(TT):
                sp.dma_start(out_t[t], resid[:, t, :]).then_inc(stored, 16)
            sp.wait_ge(stored, 16 * TT)


class Links:

    def __init__(self, eng, s):
        self.eng, self.s, self.n = eng, s, 0

    def __call__(self, ins):
        self.n += 1
        ins.then_inc(self.s, 1)
        self.eng.wait_ge(self.s, self.n)


def row_stats(nc, resid, stats, moments, t, link):
    nc.vector.bn_stats(stats[:, t, 0, :], resid[:, t, 0:512])
    link(nc.vector.bn_stats(stats[:, t, 1, :], resid[:, t, 512:1024]))
    link(nc.vector.bn_aggr(moments[:, t, :], stats[:, t, :, :]))


def quant_constants(nc, scal, calc, D, link):
    S1, Z1, S2, Z2 = (scal[:, n:n + 1] for n in range(4))
    R1, R2, Z1M, Z2M, S12, COL, ROW, BOTH, T0, T1 = (calc[:, n:n + 1] for n in range(10))
    nc.vector.reciprocal(R1, S1)
    nc.vector.reciprocal(R2, S2)
    nc.vector.tensor_scalar(Z1M, Z1, -MIDDLE, None, ALU.add)
    nc.vector.tensor_scalar(Z2M, Z2, -MIDDLE, None, ALU.add)
    link(nc.vector.tensor_tensor(S12, S1, S2, ALU.mult))
    nc.vector.tensor_tensor(T0, Z1M, S12, ALU.mult)
    link(nc.vector.tensor_tensor(T1, Z2M, S12, ALU.mult))
    nc.vector.tensor_scalar(COL, T0, -1.0, None, ALU.mult)
    nc.vector.tensor_scalar(ROW, T1, -1.0, None, ALU.mult)
    link(nc.vector.tensor_tensor(BOTH, T0, Z2M, ALU.mult))
    link(nc.vector.tensor_scalar(BOTH, BOTH, float(D), None, ALU.mult))


def row_scale_in(nc, moments, lnw, ts, var_ready):
    nc.vector.tensor_scalar(lnw[:, 0, ts], moments[:, ts, 1], EPS, None, ALU.add).then_inc(var_ready, 1)


def row_scale_out(nc, lnw, rstd, ts, link):
    link(nc.vector.reciprocal(lnw[:, 2, ts], lnw[:, 1, ts]))
    link(nc.vector.tensor_tensor(lnw[:, 3, ts], lnw[:, 0, ts], lnw[:, 2, ts], ALU.mult))
    link(nc.vector.tensor_tensor(lnw[:, 2, ts], lnw[:, 3, ts], lnw[:, 1, ts], ALU.add))
    link(nc.vector.tensor_scalar(lnw[:, 3, ts], lnw[:, 2, ts], 0.5, None, ALU.mult))
    link(nc.vector.reciprocal(rstd[:, ts], lnw[:, 3, ts]))


def attention(nc, held, es, x_t, Wq, Wk, Wv, Wo, cos_in, sin_in, quant_in, ctx_rows, q2_rows,
              resid, ident, identb, stats, moments, rstd, lnw, mean_rstd, scal, calc, KT, TT, TPB, H):
    sb, psum, sem = held
    SCALE = float(HEAD) ** -0.5
    D = KT * P

    xn = [sb(f"xn_{n}", [P, KT, TT * P], F32R) for n in ("hi", "lo")]
    kT = [sb(f"kT_{n}", [P, 2, H], F32R) for n in ("hi", "lo")]
    vv = [sb(f"v_{n}", [P, 2, TPB, HEAD], F32R) for n in ("hi", "lo")]
    qo = [sb(f"qo_{n}", [P, HPG + 1, 2, H], F32R) for n in ("hi", "lo")]
    ring = [sb(f"ring_{n}", [P, 3, D], F32R) for n in ("hi", "lo")]
    raw = sb("raw", [P, 2, D], F32)
    prob = sb("prob", [P, 1280], F32)
    pT = [sb(f"pT_{n}", [P, 1280], F32R) for n in ("hi", "lo")]
    rope = sb("rope", [P, 2, H], F32)
    cos = sb("cos", [P, H], F32)
    sin = sb("sin", [P, H], F32)
    mask = sb("mask", [P, H], F32)
    shift = sb("shift", [P, 4], F32)
    spare = sb("spare", [P, D], F32)
    cq = sb("cq", [P, D], BF16)
    total = sb("total", [P, 4], F32)
    inv = sb("inv", [P, 4], F32)

    bank = [psum(f"bank{n}", [P, H], F32) for n in range(2)]
    score = psum("score", [P, 3, H], F32)
    turned = psum("turned", [P, 2, H], F32)
    mixed = psum("mixed", [P, H], F32)

    x_in = [sem(f"x_in{t}") for t in range(TT)]
    tables_in = sem("tables_in")
    ident_made = sem("ident_made")
    pool_link = sem("pool_link")
    var_ready, root_ready = sem("var_ready"), sem("root_ready")
    dve_link = sem("dve_link")
    scaled_mean = sem("scaled_mean")
    scal_in, ctx_in_sem = sem("scal_in"), sem("ctx_in")
    c_scaled, c_rounded, c_quant, c_stored = sem("c_scaled"), sem("c_rounded"), sem("c_quant"), sem("c_stored")
    ln_out, ln_turned, ln_hi, ln_lo = sem("ln_out"), sem("ln_turned"), sem("ln_hi"), sem("ln_lo")
    raw_in = [sem("raw_in0"), sem("raw_in1")]
    block_hi, block_lo = sem("block_hi"), sem("block_lo")
    piece_done = sem("piece_done")
    added = sem("added")
    rope_parts, rope_sum, rope_hi, rope_done = (sem("rope_parts"), sem("rope_sum"), sem("rope_hi"),
                                                sem("rope_done"))
    v_staged, v_turned, v_hi, v_done = sem("v_staged"), sem("v_turned"), sem("v_hi"), sem("v_done")
    score_done = sem("score_done")
    score_seen = sem("score_seen")
    masked_done = sem("masked_done")
    exp_done = sem("exp_done")
    inv_done, prob_done = sem("inv_done"), sem("prob_done")
    turn_done, pT_hi, pT_lo = sem("turn_done"), sem("pT_hi"), sem("pT_lo")
    mix_done, o_hi, o_lo = sem("mix_done"), sem("o_hi"), sem("o_lo")

    Z2, R2 = scal[:, 3:4], calc[:, 1:2]

    def as32(ap):
        return ap.bitcast(F32)

    def stage(t):
        return prob[:, 0:D] if t % 2 == 0 else spare[:]

    def o_place(h):
        return HPG if h == 0 else h

    def number(g, name, last):
        return len(FIRST) + len(BODY) * g + (LAST if last else BODY).index(name)

    def first_wo(last):
        return 6 if last else 12

    def freed(g, name, last):
        base = 6 + PIECES * g
        w = base + first_wo(last)
        return {"Q1": base, "Q2": base, "Q3": base, "Q0'": base + 2, "K'": base + 4, "V'": base + 6,
                "A0": base + (2 if last else 8), "A1": base + (4 if last else 10),
                "B0": base + (6 if last else 12), "B1": w + TT}[name]

    def source(g, name):
        if name[0] in "QKV":
            w, col = {"Q": (Wq, HPG), "K": (Wk, 1), "V": (Wv, 1)}[name[0]]
            head = g + 1 if name.endswith("'") else g
            head = head * col + (int(name[1]) if name[0] == "Q" else 0)
            return (w[:, bass.ds(head * HEAD, HEAD)].rearrange("(k p) c -> p k c", p=P), KT)
        half, pair = "AB".index(name[0]), int(name[1])
        return (Wo[bass.ds((g * HPG + 2 * pair) * HEAD, 2 * HEAD), half * 512:half * 512 + 512]
                .rearrange("(k p) c -> p k c", p=P), 2)

    block = es.enter_context(nc.Block())

    @block.sync
    def _(sp):
        def load(g, name, last, n, slot):
            if not isinstance(n, int) or n >= 2:
                sp.wait_ge(block_lo, n - 1)
            src, k = source(g, name)
            sp.dma_start(raw[:, slot, :].rearrange("p (k c) -> p k c", k=k), src).then_inc(raw_in[slot], 16)

        for t in range(TT):
            sp.dma_start(resid[:, t, :], x_t[t]).then_inc(x_in[t], 16)
            if t == 2:
                load(-1, "Q0'", False, 0, 0)
                load(-1, "K'", False, 1, 1)
        for n, v in enumerate(quant_in):
            sp.dma_start(scal[:, n:n + 1], v.rearrange("(a b) -> a b", a=1).to_broadcast([P, 1])).then_inc(scal_in, 16)
        sp.dma_start(cos[:], cos_in).then_inc(tables_in, 16)
        sp.dma_start(sin[:], sin_in).then_inc(tables_in, 16)
        load(-1, "V'", False, 2, 0)
        with sp.Fori(0, GROUPS - 1) as g:
            for i, name in enumerate(BODY):
                load(g, name, False, g * len(BODY) + (3 + i), (3 + i) % 2)
        for i, name in enumerate(LAST):
            n = number(GROUPS - 1, name, True)
            load(GROUPS - 1, name, True, n, n % 2)

    @block.gpsimd
    def _(pool):
        link = Links(pool, pool_link)
        link(nc.gpsimd.memset(ident[:], 0.0))
        link(nc.gpsimd.memset(mask[:], 0.0))
        nc.gpsimd.affine_select(out=ident[:], in_=ident[:], compare_op=ALU.not_equal, fill=1.0, base=0,
                                pattern=[[-1, P]], channel_multiplier=1).then_inc(ident_made, 1)
        nc.gpsimd.affine_select(out=mask[:, H - P:H], in_=mask[:, H - P:H], compare_op=ALU.is_ge, fill=MASKED,
                                base=0, pattern=[[-1, P]], channel_multiplier=1).then_inc(ident_made, 1)
        pool.wait_ge(ident_made, 2)
        nc.gpsimd.tensor_copy(identb[:], ident[:]).then_inc(ident_made, 1)

        def split(n, name, slot):
            pool.wait_ge(block_hi, n + 1)
            nc.gpsimd.tensor_tensor(ring[1][:, PLACE[name], :], raw[:, slot, :],
                                    as32(ring[0][:, PLACE[name], :]), ALU.subtract).then_inc(block_lo, 1)

        def rope_add(n):
            pool.wait_ge(rope_parts, n + 1)
            nc.gpsimd.tensor_tensor(rope[:, 0, :], rope[:, 0, :], rope[:, 1, :], ALU.add).then_inc(rope_sum, 1)

        def body(g, last):
            def sp(name):
                if last:
                    n = number(g, name, True)
                    split(n, name, n % 2)
                else:
                    i = BODY.index(name)
                    split(g * len(BODY) + (3 + i), name, (3 + i) % 2)
            rb = g * ROPED + 4
            sp("Q2")
            rope_add(rb)
            sp("Q3")
            rope_add(rb + 1)
            sp("A0" if last else "Q0'")
            rope_add(rb + 2)
            rope_add(rb + 3)
            sp("A1" if last else "K'")
            rope_add(rb + 4)
            rope_add(rb + 5)
            sp("B0" if last else "V'")
            if last:
                sp("B1")
                return
            rope_add(rb + 6)
            rope_add(rb + 7)
            sp("A0")
            rope_add(rb + 8)
            sp("A1")
            rope_add(rb + 9)
            sp("B0")
            sp("B1")
            split(g * len(BODY) + 13, "Q1", 1)

        split(0, "Q0'", 0)
        split(1, "K'", 1)
        split(2, "V'", 0)
        rope_add(0)
        rope_add(1)
        rope_add(2)
        split(3, "Q1", 1)
        rope_add(3)
        with pool.Fori(0, GROUPS - 1) as g:
            body(g, False)
        body(GROUPS - 1, True)

    @block.scalar
    def _(act):
        def root(h):
            act.wait_ge(var_ready, h + 1)
            nc.scalar.activation(lnw[:, 1, h * TPB:(h + 1) * TPB], lnw[:, 0, h * TPB:(h + 1) * TPB],
                                 ACT.Sqrt).then_inc(root_ready, 1)

        def ln_scale(t):
            act.wait_ge(scaled_mean, 1 if t < TPB else 2)
            if t >= 2:
                act.wait_ge(ln_turned, 2 * t - 2)
            nc.scalar.activation(stage(t), resid[:, t, :], ACT.Identity, bias=mean_rstd[:, t:t + 1],
                                 scale=rstd[:, t:t + 1]).then_inc(ln_out, 1)

        def ln_high(t):
            for n in (2 * t, 2 * t + 1):
                k0 = 4 * (n % 2)
                act.wait_ge(ln_turned, n + 1)
                nc.scalar.copy(xn[0][:, k0:k0 + 4, t * P:(t + 1) * P], ln_bank(score, turned, n)).then_inc(ln_hi, 1)

        def split(n, name, slot, uses, free):
            act.wait_ge(raw_in[slot], uses)
            if free is not None:
                act.wait_ge(piece_done, free)
            nc.scalar.copy(ring[0][:, PLACE[name], :], raw[:, slot, :]).then_inc(block_hi, 1)

        def rope_high(n, dst):
            act.wait_ge(rope_sum, n + 1)
            nc.scalar.copy(dst, rope[:, 0, :]).then_inc(rope_hi, 1)

        def v_high(n, b):
            act.wait_ge(v_turned, n + 1)
            nc.scalar.copy(vv[0][:, b, :, :], turned[:, b, :].rearrange("p (j c) -> p j c", c=HEAD)).then_inc(v_hi, 1)

        def body(g, last):
            def sp(name):
                if last:
                    n = number(g, name, True)
                    split(n, name, n % 2, 16 * (n // 2 + 1), freed(g, name, True))
                else:
                    i = BODY.index(name)
                    slot = (3 + i) % 2
                    split(None, name, slot, g * (16 * len(BODY) // 2) + 16 * ((3 + i) // 2 + 1),
                          freed(g, name, False))
            rb = g * ROPED + 4
            ub = g * 8

            def probs_high(u):
                for c in range(3):
                    act.wait_ge(turn_done, ub * 3 + (3 * u + c + 1))
                    if c == 0 and u > 0:
                        act.wait_ge(mix_done, ub + u)
                    nc.scalar.copy(pT[0][:, CHUNKS[c][0]:CHUNKS[c][0] + CHUNK_WIDTH[c]],
                                   turned_chunk(turned, mixed, c)).then_inc(pT_hi, 1)

            def exps(u):
                for n, i in enumerate(TILE_ORDER):
                    sl = slice(PROB_AT[i], PROB_AT[i] + P * (i + 1))
                    act.wait_ge(masked_done, ub * 4 + (4 * u + n + 1))
                    nc.scalar.activation(prob[:, sl], prob[:, sl], ACT.Exp, bias=shift[:, i:i + 1], scale=-1.0,
                                         accum_out=total[:, i:i + 1]).then_inc(exp_done, 1)

            def out_high(u):
                act.wait_ge(mix_done, ub + (u + 1))
                nc.scalar.copy(qo[0][:, o_place(u // 2), u % 2, :], mixed[:]).then_inc(o_hi, 1)

            def scale_ctx(j):
                act.wait_ge(ctx_in_sem, g * 32 + 16 * (j + 1))
                nc.scalar.activation(spare[:], spare[:], ACT.Identity, bias=Z2, scale=R2).then_inc(c_scaled, 1)

            def store_ctx(j):
                act.wait_ge(c_quant, g * 2 + (j + 1))
                act.dma_start(q2_rows[bass.ds((g * 2 + j) * P, P), :], cq[:]).then_inc(c_stored, 16)

            load_ctx(g * 2)
            for u in range(8):
                if u > 0:
                    probs_high(u - 1)
                    if u < 7 or not last:
                        h = u - 1
                        rope_high(rb + h, qo[0][:, (h // 2 + 1) % HPG, h % 2, :])
                exps_first = {0: "Q2", 1: "Q3"}
                if u in exps_first:
                    sp(exps_first[u])
                elif not last and u in (2, 4, 6):
                    sp({2: "Q0'", 4: "K'", 6: "V'"}[u])
                elif last and u in (2, 4, 6):
                    sp({2: "A0", 4: "A1", 6: "B0"}[u])
                exps(u)
                if u > 0:
                    out_high(u - 1)
            probs_high(7)
            if last:
                out_high(7)
                scale_ctx(0)
                store_ctx(0)
                load_ctx(g * 2 + 1)
                sp("B1")
                scale_ctx(1)
                store_ctx(1)
                act.wait_ge(c_stored, 16 * 2 * GROUPS)
                return
            rope_high(rb + 7, qo[0][:, 0, 1, :])
            sp("A0")
            rope_high(rb + 8, kT[0][:, 0, :])
            out_high(7)
            sp("A1")
            rope_high(rb + 9, kT[0][:, 1, :])
            sp("B0")
            v_high(g * 2 + 2, 0)
            v_high(g * 2 + 3, 1)
            scale_ctx(0)
            store_ctx(0)
            load_ctx(g * 2 + 1)
            sp("B1")
            split(None, "Q1", 1, g * (16 * len(BODY) // 2) + 16 * 7, 6 + PIECES * g + 12 + TT)
            scale_ctx(1)
            store_ctx(1)

        def load_ctx(n):
            act.dma_start(spare[:], ctx_rows[bass.ds(n * P, P), :]).then_inc(ctx_in_sem, 16)

        split(0, "Q0'", 0, 16, None)
        root(0)
        ln_scale(0)
        ln_scale(1)
        ln_high(0)
        ln_scale(2)
        ln_high(1)
        ln_scale(3)
        split(1, "K'", 1, 16, None)
        ln_high(2)
        ln_high(3)
        split(2, "V'", 0, 32, None)
        root(1)
        ln_scale(4)
        ln_scale(5)
        ln_high(4)
        ln_scale(6)
        ln_high(5)
        ln_scale(7)
        rope_high(0, qo[0][:, 0, 0, :])
        ln_high(6)
        ln_high(7)
        rope_high(1, kT[0][:, 0, :])
        v_high(0, 0)
        rope_high(2, qo[0][:, 0, 1, :])
        split(3, "Q1", 1, 32, 4)
        rope_high(3, kT[0][:, 1, :])
        v_high(1, 1)
        with act.Fori(0, GROUPS - 1) as g:
            body(g, False)
        body(GROUPS - 1, True)

    @block.vector
    def _(dve):
        link = Links(dve, dve_link)

        def ln_low(n):
            t, k0 = n // 2, 4 * (n % 2)
            dve.wait_ge(ln_hi, n + 1)
            nc.vector.tensor_tensor(xn[1][:, k0:k0 + 4, t * P:(t + 1) * P], ln_bank(score, turned, n),
                                    as32(xn[0][:, k0:k0 + 4, t * P:(t + 1) * P]), ALU.subtract).then_inc(ln_lo, 1)

        def ln_rows(h):
            ts = slice(h * TPB, (h + 1) * TPB)
            dve.wait_ge(root_ready, h + 1)
            row_scale_out(nc, lnw, rstd, ts, link)
            nc.vector.scalar_tensor_tensor(mean_rstd[:, ts], moments[:, ts, 0], -1.0, rstd[:, ts],
                                           ALU.mult, ALU.mult).then_inc(scaled_mean, 1)

        def ln_stats(t):
            dve.wait_ge(x_in[t], 16)
            row_stats(nc, resid, stats, moments, t, link)

        for t in range(TPB):
            ln_stats(t)
        row_scale_in(nc, moments, lnw, slice(0, TPB), var_ready)
        ln_rows(0)
        for t in range(TPB, TT):
            ln_stats(t)
            ln_low(2 * (t - TPB))
            ln_low(2 * (t - TPB) + 1)
        row_scale_in(nc, moments, lnw, slice(TPB, TT), var_ready)
        ln_rows(1)
        dve.wait_ge(scal_in, 64)
        quant_constants(nc, scal, calc, D, link)

        def rope_products(m, n):
            b = bank[m[1]]
            if not isinstance(n, int) or n > 0:
                dve.wait_ge(rope_done, n)
            dve.wait_ge(piece_done, m[0] + 1)
            nc.vector.tensor_tensor(rope[:, 0, :], b[:], cos[:], ALU.mult)
            nc.vector.tensor_tensor(rope[0:64, 1, :], b[64:128, :], sin[64:128, :], ALU.mult)
            (nc.vector.tensor_tensor(rope[64:128, 1, :], b[0:64, :], sin[0:64, :], ALU.mult)
             .then_inc(rope_parts, 1))

        def rope_low(n, hi, lo):
            dve.wait_ge(rope_hi, n + 1)
            nc.vector.tensor_tensor(lo, rope[:, 0, :], as32(hi), ALU.subtract).then_inc(rope_done, 1)

        def v_stage(m, n, b):
            dve.wait_ge(rope_done, n)
            dve.wait_ge(piece_done, m[0] + 1)
            nc.vector.tensor_copy(rope[:, b, :], bank[m[1]][:]).then_inc(v_staged, 1)

        def v_low(n, b):
            dve.wait_ge(v_hi, n + 1)
            nc.vector.tensor_tensor(vv[1][:, b, :, :], turned[:, b, :].rearrange("p (j c) -> p j c", c=HEAD),
                                    as32(vv[0][:, b, :, :]), ALU.subtract).then_inc(v_done, 1)

        def body(g, last):
            rb, ub = g * ROPED + 4, g * 8
            mb = 6 + PIECES * g if isinstance(g, int) else g * PIECES + 6

            def m(j):
                return mb + j, j % 2

            def probs_low(u):
                for c in range(3):
                    sl = slice(CHUNKS[c][0], CHUNKS[c][0] + CHUNK_WIDTH[c])
                    dve.wait_ge(pT_hi, ub * 3 + (3 * u + c + 1))
                    nc.vector.tensor_tensor(pT[1][:, sl], turned_chunk(turned, mixed, c), as32(pT[0][:, sl]),
                                            ALU.subtract).then_inc(pT_lo, 1)

            def peaks(u):
                for n, i in enumerate(TILE_ORDER):
                    w = P * (i + 1)
                    s, c = SCORE_AT[i]
                    if n != 2:
                        dve.wait_ge(score_done, ub * 4 + (4 * u + TILES_NEEDED[n]))
                        dve.sem_inc(score_seen, 1)
                    nc.vector.tensor_tensor_reduce(
                        out=prob[:, PROB_AT[i]:PROB_AT[i] + w], in0=score[:, s, c:c + w], in1=mask[:, H - w:H],
                        scale=-SCALE, scalar=-NEVER, op0=ALU.add, op1=ALU.min,
                        accum_out=shift[:, i:i + 1]).then_inc(masked_done, 1)

            def normalise(u):
                dve.wait_ge(exp_done, ub * 4 + (4 * u + 4))
                nc.vector.reciprocal(inv[:], total[:]).then_inc(inv_done, 1)
                dve.wait_ge(inv_done, ub + (u + 1))
                for i in TILE_ORDER:
                    sl = slice(PROB_AT[i], PROB_AT[i] + P * (i + 1))
                    ins = nc.vector.tensor_scalar(prob[:, sl], prob[:, sl], inv[:, i:i + 1], None, ALU.mult)
                ins.then_inc(prob_done, 1)

            def out_low(u):
                dve.wait_ge(o_hi, ub + (u + 1))
                nc.vector.tensor_tensor(qo[1][:, o_place(u // 2), u % 2, :], mixed[:],
                                        as32(qo[0][:, o_place(u // 2), u % 2, :]), ALU.subtract).then_inc(o_lo, 1)

            def add_piece(j, t, half):
                dve.wait_ge(piece_done, mb + (j + 1))
                sl = slice(half * 512, half * 512 + 512)
                nc.vector.tensor_tensor(resid[:, t, sl], bank[j % 2][:], resid[:, t, sl], ALU.add).then_inc(added, 1)

            def q_slot(h):
                return (h // 2 + 1) % HPG, h % 2

            for u in range(8):
                if u > 0:
                    probs_low(u - 1)
                peaks(u)
                if u > 0 and (u < 7 or not last):
                    s, b = q_slot(u - 1)
                    rope_low(rb + (u - 1), qo[0][:, s, b, :], qo[1][:, s, b, :])
                normalise(u)
                if u > 0:
                    out_low(u - 1)
                if u < 6 or not last:
                    rope_products(m(u), rb + u)
            probs_low(7)
            if last:
                out_low(7)
            else:
                rope_low(rb + 7, qo[0][:, 0, 1, :], qo[1][:, 0, 1, :])
                rope_products(m(8), rb + 8)
                out_low(7)
                rope_low(rb + 8, kT[0][:, 0, :], kT[1][:, 0, :])
                rope_products(m(9), rb + 9)
                rope_low(rb + 9, kT[0][:, 1, :], kT[1][:, 1, :])
                v_stage(m(10), rb + 10, 0)
                v_stage(m(11), rb + 10, 1)
                v_low(g * 2 + 2, 0)
            def quant_ctx(j):
                dve.wait_ge(c_scaled, g * 2 + (j + 1))
                nc.vector.tensor_scalar(spare[:], spare[:], MAGIC, MAGIC, ALU.add, ALU.max).then_inc(c_rounded, 1)
                dve.wait_ge(c_rounded, g * 2 + (j + 1))
                if j == 1 or not isinstance(g, int) or g > 0:
                    dve.wait_ge(c_stored, g * 32 + 16 * j)
                nc.vector.tensor_scalar(cq[:], spare[:], MAGIC + 255.0, MAGIC + MIDDLE,
                                        ALU.min, ALU.subtract).then_inc(c_quant, 1)

            w = first_wo(last)
            for half in range(2):
                for t in range(TT):
                    add_piece(w + half * TT + t, t, half)
                    if half == 0 and t == 0 and not last:
                        v_low(g * 2 + 3, 1)
                    if t == (3, 1)[half]:
                        quant_ctx(half)
                    if half == 1 and last:
                        dve.wait_ge(added, 2 * TT * (g + 1) - TT + t + 2)
                        row_stats(nc, resid, stats, moments, t, link)
            if last:
                row_scale_in(nc, moments, lnw, slice(0, TT), var_ready)

        dve.sem_inc(added, 1)
        for n in range(TT, TT + 4):
            ln_low(n)
        dve.wait_ge(tables_in, 32)
        rope_products((0, 0), 0)
        rope_low(0, qo[0][:, 0, 0, :], qo[1][:, 0, 0, :])
        for n in range(TT + 4, 2 * TT):
            ln_low(n)
        rope_products((1, 1), 1)
        rope_low(1, kT[0][:, 0, :], kT[1][:, 0, :])
        v_stage((2, 0), 2, 0)
        v_low(0, 0)
        rope_products((3, 1), 2)
        rope_low(2, qo[0][:, 0, 1, :], qo[1][:, 0, 1, :])
        rope_products((4, 0), 3)
        rope_low(3, kT[0][:, 1, :], kT[1][:, 1, :])
        v_stage((5, 1), 4, 1)
        v_low(1, 1)
        with dve.Fori(0, GROUPS - 1) as g:
            body(g, False)
        body(GROUPS - 1, True)

    @block.tensor
    def _(pe):
        PASSES = ((0, 0), (0, 1), (1, 0))

        pe.wait_ge(ident_made, 3)

        def ln_turn(t):
            pe.wait_ge(ln_out, t + 1)
            for n in (2 * t, 2 * t + 1):
                k0 = 4 * (n % 2)
                if n >= 4:
                    pe.wait_ge(ln_lo, n - 3)
                dst = ln_bank(score, turned, n)
                for k in range(4):
                    ins = nc.tensor.transpose(dst[:, k, :], stage(t)[:, (k0 + k) * P:(k0 + k + 1) * P], ident[:])
                ins.then_inc(ln_turned, 1)

        def project(par, name, b, n, steps=range(24)):
            place = PLACE[name]
            for s in steps:
                k, (a, c) = s // 3, PASSES[s % 3]
                if s == 0:
                    if b == 0:
                        pe.wait_ge(block_lo, n + 1)
                ins = nc.tensor.matmul(bank[par][:], ring[a][:, place, k * P:(k + 1) * P],
                                       xn[c][:, k, b * H:(b + 1) * H], start=(s == 0), stop=(s == 23))
                if s == 23:
                    ins.then_inc(piece_done, 1)

        def turn_values(n, b):
            pe.wait_ge(v_staged, n + 1)
            for j in range(TPB):
                ins = nc.tensor.transpose(turned[:, b, j * P:(j + 1) * P], rope[:, b, j * P:(j + 1) * P], ident[:])
            ins.then_inc(v_turned, 1)

        def body(g, last):
            rb, ub = g * ROPED + 4, g * 8

            def scores(u):
                h, b = u // 2, u % 2
                pe.wait_ge(rope_done, rb - 1 + u)
                if u > 0:
                    pe.wait_ge(masked_done, ub * 4 + 4 * u)
                for i in TILE_ORDER:
                    w = P * (i + 1)
                    s, c = SCORE_AT[i]
                    dst = score[:, s, c:c + w]
                    for p, (a, e) in enumerate(PASSES):
                        ins = nc.tensor.matmul(dst, qo[a][:, h, b, i * P:(i + 1) * P], kT[e][:, b, 0:w],
                                               start=(p == 0), stop=(p == 2))
                    ins.then_inc(score_done, 1)

            def turn_probs(u):
                pe.wait_ge(prob_done, ub + (u + 1))
                if u > 0:
                    pe.wait_ge(pT_lo, ub * 3 + 3 * u)
                    pe.wait_ge(o_lo, ub + u)
                for c in range(3):
                    dst = turned_chunk(turned, mixed, c)
                    for j in CHUNKS[c][1]:
                        for i in range(j, TPB):
                            col = KEYS_AT[j] - CHUNKS[c][0] + (i - j) * P
                            ins = nc.tensor.transpose(dst[:, col:col + P],
                                                      prob[:, PROB_AT[i] + j * P:PROB_AT[i] + (j + 1) * P], ident[:])
                    ins.then_inc(turn_done, 1)

            def mix(u):
                b = u % 2
                pe.wait_ge(v_done, g * 2 + (1 + b))
                pe.wait_ge(pT_lo, ub * 3 + (3 * u + 3))
                for j in range(TPB):
                    w = H - j * P
                    for p, (a, c) in enumerate(PASSES):
                        ins = nc.tensor.matmul(mixed[:, j * P:H], vv[a][:, b, j, :],
                                               pT[c][:, KEYS_AT[j]:KEYS_AT[j] + w],
                                               start=(j == 0 and p == 0), stop=(j == TPB - 1 and p == 2))
                ins.then_inc(mix_done, 1)

            def filler(u, steps):
                name = ("Q1", "Q1", "Q2", "Q2", "Q3", "Q3", "Q0'", "Q0'", "K'", "K'", "V'", "V'")[u]
                n = number(g, name, True) if last else g * len(BODY) + (3 + BODY.index(name))
                if steps[0] == 0:
                    if u < 2:
                        pe.wait_ge(added, g * (2 * TT) + 1)
                    else:
                        pe.wait_ge(rope_parts, rb + (u - 1))
                project(u % 2, name, u % 2, n, steps)

            def out_part(j, t, half, pairs):
                if pairs[0] == 0:
                    before = j - 2 - first_wo(last)
                    if before >= 0:
                        pe.wait_ge(added, g * (2 * TT) + (before + 2))
                    elif last:
                        pe.wait_ge(rope_parts, rb + (j - 1))
                    else:
                        pe.wait_ge(v_staged, g * 2 + (before + 5))
                for pair in pairs:
                    name = "AB"[half] + str(pair)
                    if t == 0:
                        n = number(g, name, True) if last else g * len(BODY) + (3 + BODY.index(name))
                        pe.wait_ge(block_lo, n + 1)
                    for k in (2 * pair, 2 * pair + 1):
                        for p, (a, c) in enumerate(PASSES):
                            ins = nc.tensor.matmul(
                                bank[j % 2][:], qo[a][:, o_place(k), t // TPB, (t % TPB) * P:(t % TPB + 1) * P],
                                ring[c][:, PLACE[name], (k % 2) * 512:(k % 2) * 512 + 512],
                                start=(k == 0 and p == 0), stop=(k == HPG - 1 and p == 2))
                if pairs[-1] == 1:
                    ins.then_inc(piece_done, 1)

            for u in range(8):
                scores(u)
                some = u < 6 or not last
                if some:
                    filler(u, range(0, 6))
                if u > 0:
                    mix(u - 1)
                if some:
                    filler(u, range(6, 24))
                turn_probs(u)
            if not last:
                filler(8, range(24))
            mix(7)
            if not last:
                filler(9, range(24))
                filler(10, range(24))
                filler(11, range(24))
                turn_values(g * 2 + 2, 0)
            w = first_wo(last)
            pe.wait_ge(o_lo, ub + 8)
            for half in range(2):
                out_part(w + half * TT, 0, half, (0,))
                out_part(w + half * TT + 1, 1, half, (0,))
                out_part(w + half * TT, 0, half, (1,))
                out_part(w + half * TT + 1, 1, half, (1,))
                if half == 0 and not last:
                    turn_values(g * 2 + 3, 1)
                for t in range(2, TT):
                    out_part(w + half * TT + t, t, half, (0, 1))

        for t in range(TPB):
            ln_turn(t)
        pe.wait_ge(ln_lo, TT)
        project(0, "Q0'", 0, 0)
        ln_turn(4)
        ln_turn(5)
        project(1, "K'", 0, 1)
        ln_turn(6)
        ln_turn(7)
        pe.wait_ge(rope_parts, 1)
        project(0, "V'", 0, 2)
        pe.wait_ge(ln_lo, 2 * TT)
        turn_values(0, 0)
        pe.wait_ge(rope_parts, 2)
        project(1, "Q0'", 1, 0)
        project(0, "K'", 1, 1)
        pe.wait_ge(rope_parts, 3)
        project(1, "V'", 1, 2)
        turn_values(1, 1)
        with pe.Fori(0, GROUPS - 1) as g:
            body(g, False)
        body(GROUPS - 1, True)


def ln_bank(score, turned, n):
    b = score[:, n % 4, :] if n % 4 < 3 else turned[:, 0, :]
    return b.rearrange("p (k c) -> p k c", c=P)


def turned_chunk(turned, mixed, c):
    return turned[:, c, :] if c < 2 else mixed[:, 0:256]


def mix_and_experts(nc, held, es, out_t, q2_dram, A_w, B_w, Wr, keys, resid, ident, identb, stats, moments,
                    rstd, lnw, mean_rstd, scal, calc, KT, TT, TPB, H):
    sb, psum, sem = held
    D = KT * P
    N = EXPERTS * RANK
    NT = N // P
    NB = TT // TPB
    AHEAD = 2
    PASSES = ((0, 0), (0, 1), (1, 0))

    aT = [sb(f"aT_{n}", [P, KT, N], F32R) for n in ("hi", "lo")]
    bT = [sb(f"bT_{n}", [P, NT, D], F32R) for n in ("hi", "lo")]
    rT = [sb(f"rT_{n}", [P, KT, P], F32R) for n in ("hi", "lo")]
    q2 = sb("q2", [P, NB * KT, D], BF16)
    colterm = sb("colterm", [P, NB, D], F32)
    rowterm = sb("rowterm", [P, TT], F32)
    one = sb("one", [P, P], BF16)
    wraw = sb("wraw", [P, 2, D], F32)
    rraw = sb("rraw", [ROUTER, D], F32)
    kraw = sb("kraw", [EXPERTS, ROUTER], F32)
    keysT = sb("keysT", [ROUTER, EXPERTS], F32)
    scl = sb("scl", [P, 2, TT], F32)
    v1 = sb("v1", [P, 2, D], F32)
    q1 = sb("q1", [P, 2, D], BF16)
    q1T = sb("q1T", [P, 2, KT, P], BF16)
    part = sb("part", [P, 2, 512], F32)
    norm = sb("norm", [P, D], F32)
    xe = [sb(f"xe_{n}", [P, KT, P], F32R) for n in ("hi", "lo")]
    qT = sb("qT", [ROUTER, P], F32)
    zg = sb("zg", [P, N], F32)
    zT = [sb(f"zT_{n}", [P, NT, P], F32R) for n in ("hi", "lo")]
    seen = sb("seen", [P, EXPERTS], F32)
    left = sb("left", [P, 2, EXPERTS], F32)
    weight = sb("weight", [P, 3, EXPERTS], F32)
    top = sb("top", [P, 2, 8], F32)
    peak = sb("peak", [P, 3], F32)

    lb = [psum(f"lb{n}", [P, 4, P], F32) for n in range(2)]
    qb = psum("qb", [P, KT, P], BF16)
    pb = [psum(f"pb{n}", [P, 512], F32) for n in range(2)]
    zb = psum("zb", [P, N], F32)
    sbk = psum("sbk", [P, 512], F32)
    rb = psum("rb", [P, TT, 2], F32)

    q2_in = [sem(f"q2_in{b}") for b in range(NB)]
    w_in = [sem("w_in0"), sem("w_in1")]
    r_in, k_in = sem("r_in"), sem("k_in")
    ones_made = sem("ones_made")
    dve_link = sem("dve_link_e")
    rooted2 = sem("rooted2")
    scl_done = sem("scl_done")
    v_scaled, v_quant, q_turned, q_copied = sem("v_scaled"), sem("v_quant"), sem("q_turned"), sem("q_copied")
    f_turned, f_hi, f_lo = sem("f_turned"), sem("f_hi"), sem("f_lo")
    p_done = sem("p_done")
    col_done = sem("col_done")
    summed, row_done = sem("summed"), sem("row_done")
    col_added = sem("col_added")
    m_read, m_added = sem("m_read"), sem("m_added")
    var3, root3, scale3 = sem("var3"), sem("root3"), sem("scale3")
    n_done = sem("n_done")
    k_done = sem("k_done")
    r_done, r_read, s_done, s_read = sem("r_done"), sem("r_read"), sem("s_done"), sem("s_read")
    z_done, z_gated = sem("z_done"), sem("z_gated")
    peak_done, exp_done = sem("peak_done"), sem("exp_done_e")
    o_added, stored = sem("o_added"), sem("stored")

    S1, Z1, S2, Z2 = (scal[:, n:n + 1] for n in range(4))
    R1, R2, Z1M, Z2M, S12, COL, ROW, BOTH, T0, T1 = (calc[:, n:n + 1] for n in range(10))

    turns = range(-AHEAD, TT)
    a_turn = {-2: range(0, 4), -1: range(4, 8)}
    lb_order, pb_order = [], [("col", 0), ("col", 1)]
    for i in turns:
        if i >= 0:
            lb_order += [("x", 2 * i), ("x", 2 * i + 1)]
        if i + AHEAD < TT:
            pb_order += [("mul", 2 * (i + AHEAD)), ("mul", 2 * (i + AHEAD) + 1)]
        lb_order += [("a", f) for f in a_turn.get(i, ())]
        if i == -1:
            lb_order += [("r", 0), ("k", 0)]
        if i == 0:
            lb_order += [("b", f) for f in range(KT)]
            pb_order += [("col", 2), ("col", 3)]
        if i >= 1:
            pb_order += [("out", 2 * (i - 1)), ("out", 2 * (i - 1) + 1)]
        if i >= 0:
            lb_order += [("z", i)]
    pb_order += [("out", 2 * TT - 2), ("out", 2 * TT - 1)]
    LB = {f: n for n, f in enumerate(lb_order)}
    PB = {f: n for n, f in enumerate(pb_order)}

    def reads_of(kind, upto):
        return sum(f[0] in kind for f in pb_order[:upto])

    def router_bank(b):
        return b[:, 0, :].rearrange("p (k r) -> p k r", k=KT)

    def target(kind, f):
        if kind == "x":
            return [x[:, 4 * (f % 2):4 * (f % 2) + 4, :] for x in xe]
        if kind == "a":
            return [x[:, 4 * (f % 2):4 * (f % 2) + 4, (f // 2) * P:(f // 2 + 1) * P] for x in aT]
        if kind == "b":
            return [x[:, :, f * P:(f + 1) * P] for x in bT]
        if kind == "r":
            return [x[:, :, 0:ROUTER] for x in rT]
        return [x[:] for x in zT]

    def filled(kind, f):
        b = lb[LB[kind, f] % 2]
        return router_bank(b) if kind == "r" else b[:]

    block = es.enter_context(nc.Block())

    @block.sync
    def _(sp):
        def load_q2(b):
            sp.dma_start(q2[:, b * KT:(b + 1) * KT, :],
                         q2_dram[b * D:(b + 1) * D, :].rearrange("(k p) n -> p k n", p=P)).then_inc(q2_in[b], 16)

        def load_w(n):
            if n < 4:
                src, dst = A_w[n * P:(n + 1) * P, :], wraw[:, n % 2, :]
            else:
                m = n - 4
                src = B_w[2 * m * P:2 * (m + 1) * P, :].rearrange("(a p) c -> p a c", p=P)
                dst = wraw[:, n % 2, :].rearrange("p (a c) -> p a c", a=2)
            if n >= 2:
                m = n - 2
                sp.wait_ge(f_turned, LB["a", 2 * m + 1] + 1 if m < 4 else LB["b", 2 * (m - 4) + 1] + 1)
            sp.dma_start(dst, src).then_inc(w_in[n % 2], 16)

        load_q2(0)
        load_w(0)
        load_w(1)
        sp.dma_start(rraw[:], Wr).then_inc(r_in, 16)
        sp.dma_start(kraw[:], keys).then_inc(k_in, 16)
        load_w(2)
        load_w(3)
        load_q2(1)
        for n in range(4, 8):
            load_w(n)
        for t in range(TT):
            sp.wait_ge(o_added, 2 * t + 2)
            sp.dma_start(out_t[t], resid[:, t, :]).then_inc(stored, 16)
        sp.wait_ge(stored, 16 * TT)

    @block.gpsimd
    def _(pool):
        nc.gpsimd.memset(one[:], 1.0).then_inc(ones_made, 1)
        nc.gpsimd.memset(rT[0][:].bitcast(F32), 0.0).then_inc(ones_made, 1)
        nc.gpsimd.memset(rT[1][:].bitcast(F32), 0.0).then_inc(ones_made, 1)
        for t in range(TT):
            pool.wait_ge(col_done, 2 * (t // TPB + 1))
            pool.wait_ge(v_scaled, t + 1)
            nc.gpsimd.tensor_tensor(resid[:, t, :], resid[:, t, :], colterm[:, t // TPB, :], ALU.add).then_inc(col_added, 1)

    @block.scalar
    def _(act):
        def scale_tile(t):
            act.wait_ge(scl_done, 1)
            if t >= 2:
                act.wait_ge(v_quant, t - 1)
            nc.scalar.activation(v1[:, t % 2, :], resid[:, t, :], ACT.Identity, bias=scl[:, 1, t:t + 1],
                                 scale=scl[:, 0, t:t + 1]).then_inc(v_scaled, 1)

        def copy_turned(t):
            act.wait_ge(q_turned, t + 1)
            if t >= 2:
                act.wait_ge(p_done, PB["mul", 2 * (t - 2) + 1] + 1)
            nc.scalar.copy(q1T[:, t % 2, :, :], qb[:]).then_inc(q_copied, 1)

        def high(kind, f):
            act.wait_ge(f_turned, LB[kind, f] + 1)
            if kind == "x" and f >= 2:
                act.wait_ge(z_done, f // 2)
            if kind == "z" and f >= 1:
                act.wait_ge(p_done, PB["out", 2 * f - 1] + 1)
            if kind == "r":
                act.wait_ge(ones_made, 3)
            if kind == "k":
                nc.scalar.copy(keysT[:], lb[LB[kind, f] % 2][0:ROUTER, 0, 0:EXPERTS]).then_inc(f_hi, 1)
            else:
                nc.scalar.copy(target(kind, f)[0], filled(kind, f)).then_inc(f_hi, 1)

        def read_product(t):
            for half in range(2):
                m = 2 * t + half
                act.wait_ge(p_done, PB["mul", m] + 1)
                act.wait_ge(row_done, t + 1)
                if m >= 2:
                    act.wait_ge(m_added, m - 1)
                nc.scalar.activation(part[:, half, :], pb[PB["mul", m] % 2][:], ACT.Identity,
                                     bias=rowterm[:, t:t + 1], scale=S12).then_inc(m_read, 1)

        def root(t):
            act.wait_ge(var3, t + 1)
            nc.scalar.activation(lnw[:, 1, t:t + 1], lnw[:, 0, t:t + 1], ACT.Sqrt).then_inc(root3, 1)

        def normalise(t):
            act.wait_ge(scale3, t + 1)
            if t >= 1:
                act.wait_ge(f_turned, LB["x", 2 * t - 1] + 1)
            nc.scalar.activation(norm[:], resid[:, t, :], ACT.Identity, bias=mean_rstd[:, t:t + 1],
                                 scale=rstd[:, t:t + 1]).then_inc(n_done, 1)

        nc.scalar.activation(lnw[:, 1, :], lnw[:, 0, :], ACT.Sqrt).then_inc(rooted2, 1)
        scale_tile(0)
        scale_tile(1)
        copy_turned(0)
        for i in turns:
            if i >= 1:
                high("z", i - 1)
            if i >= 0:
                high("x", 2 * i)
                high("x", 2 * i + 1)
            if i + 4 < TT:
                scale_tile(i + 4)
            if i + AHEAD < TT:
                read_product(i + AHEAD)
            for f in a_turn.get(i, ()):
                high("a", f)
            if i == -1:
                high("r", 0)
                high("k", 0)
            if i >= 0:
                act.wait_ge(r_done, i + 1)
                nc.scalar.copy(qT[:], sbk[0:ROUTER, 0:P]).then_inc(r_read, 1)
            if 0 <= i + 1 < TT:
                normalise(i + 1)
            if i + AHEAD < TT:
                root(i + AHEAD)
            if i >= 0:
                act.wait_ge(peak_done, i + 1)
                nc.scalar.activation(weight[:, 0, :], seen[:], ACT.Exp, bias=peak[:, 0:1]).then_inc(exp_done, 1)
            if i == 0:
                for f in range(KT):
                    high("b", f)
            if i + 3 < TT:
                copy_turned(i + 3)
        high("z", TT - 1)

    @block.vector
    def _(dve):
        link = Links(dve, dve_link)
        dve.wait_ge(rooted2, 1)
        row_scale_out(nc, lnw, rstd, slice(0, TT), link)
        link(nc.vector.tensor_scalar(scl[:, 0, :], rstd[:], R1, None, ALU.mult))
        link(nc.vector.tensor_tensor(lnw[:, 2, :], moments[:, :, 0], scl[:, 0, :], ALU.mult))
        nc.vector.tensor_scalar(scl[:, 1, :], lnw[:, 2, :], -1.0, Z1, ALU.mult, ALU.add).then_inc(scl_done, 1)

        def quantise(t):
            dve.wait_ge(v_scaled, t + 1)
            link(nc.vector.tensor_scalar(v1[:, t % 2, :], v1[:, t % 2, :], MAGIC, MAGIC, ALU.add, ALU.max))
            if t >= 2:
                dve.wait_ge(q_turned, t - 1)
            nc.vector.tensor_scalar(q1[:, t % 2, :], v1[:, t % 2, :], MAGIC + 255.0, MAGIC + MIDDLE,
                                    ALU.min, ALU.subtract).then_inc(v_quant, 1)

        def low(kind, f):
            dve.wait_ge(f_hi, LB[kind, f] + 1)
            if kind == "k":
                dve.wait_ge(f_lo, LB[kind, f])
                dve.sem_inc(f_lo, 1)
                return
            h, l = target(kind, f)
            nc.vector.tensor_tensor(l, filled(kind, f), h.bitcast(F32), ALU.subtract).then_inc(f_lo, 1)

        def column_term(n):
            dve.wait_ge(p_done, PB["col", n] + 1)
            nc.vector.tensor_scalar(colterm[:, n // 2, (n % 2) * 512:(n % 2) * 512 + 512], pb[PB["col", n] % 2][:],
                                    COL, BOTH, ALU.mult, ALU.add).then_inc(col_done, 1)

        def add_product(t):
            dve.wait_ge(summed, t + 1)
            nc.vector.tensor_scalar(rowterm[:, t:t + 1], rb[:, t, 0:1], ROW, None, ALU.mult).then_inc(row_done, 1)
            dve.wait_ge(col_added, t + 1)
            for half in range(2):
                sl = slice(half * 512, half * 512 + 512)
                dve.wait_ge(m_read, 2 * t + half + 1)
                nc.vector.tensor_tensor(resid[:, t, sl], part[:, half, :], resid[:, t, sl], ALU.add).then_inc(m_added, 1)
            dve.wait_ge(m_added, 2 * t + 2)
            row_stats(nc, resid, stats, moments, t, link)
            row_scale_in(nc, moments, lnw, slice(t, t + 1), var3)

        def scale_of(t):
            dve.wait_ge(root3, t + 1)
            row_scale_out(nc, lnw, rstd, slice(t, t + 1), link)
            nc.vector.scalar_tensor_tensor(mean_rstd[:, t:t + 1], moments[:, t, 0:1], -1.0, rstd[:, t:t + 1],
                                           ALU.mult, ALU.mult).then_inc(scale3, 1)

        def gate(t):
            dve.wait_ge(s_done, t + 1)
            nc.vector.tensor_copy(seen[:], sbk[:, 0:EXPERTS]).then_inc(s_read, 1)
            dve.wait_ge(s_read, t + 1)
            link(nc.vector.max(top[:, 0, :], seen[:]))
            nc.vector.tensor_scalar(peak[:, 0:1], top[:, 0, 0:1], -1.0, None, ALU.mult).then_inc(peak_done, 1)
            link(nc.vector.match_replace(left[:, 0, :], top[:, 0, :], seen[:], NEVER))
            link(nc.vector.max(top[:, 1, :], left[:, 0, :]))
            link(nc.vector.match_replace(left[:, 1, :], top[:, 1, :], left[:, 0, :], NEVER))
            dve.wait_ge(exp_done, t + 1)
            link(nc.vector.scalar_tensor_tensor(weight[:, 1, :], left[:, 1, :], NEVER, weight[:, 0, :],
                                                ALU.is_equal, ALU.mult, accum_out=peak[:, 1:2]))
            link(nc.vector.reciprocal(peak[:, 2:3], peak[:, 1:2]))
            link(nc.vector.tensor_scalar(weight[:, 2, :], weight[:, 1, :], peak[:, 2:3], SCALING, ALU.mult, ALU.mult))
            dve.wait_ge(z_done, t + 1)
            if t >= 1:
                dve.wait_ge(f_turned, LB["z", t - 1] + 1)
            nc.vector.tensor_tensor(zg[:].rearrange("p (e r) -> p e r", r=RANK),
                                    zb[:].rearrange("p (e r) -> p e r", r=RANK),
                                    weight[:, 2, :].unsqueeze(2).to_broadcast([P, EXPERTS, RANK]),
                                    ALU.mult).then_inc(z_gated, 1)

        def add_out(t):
            for half in range(2):
                sl = slice(half * 512, half * 512 + 512)
                n = PB["out", 2 * t + half]
                dve.wait_ge(p_done, n + 1)
                nc.vector.tensor_tensor(resid[:, t, sl], pb[n % 2][:], resid[:, t, sl], ALU.add).then_inc(o_added, 1)

        quantise(0)
        quantise(1)
        column_term(0)
        column_term(1)
        for i in turns:
            if i >= 1:
                low("z", i - 1)
            if i + 4 < TT:
                quantise(i + 4)
            if i >= 0:
                low("x", 2 * i)
                low("x", 2 * i + 1)
            if i + AHEAD < TT:
                add_product(i + AHEAD)
            for f in a_turn.get(i, ()):
                low("a", f)
            if i == -1:
                low("r", 0)
                low("k", 0)
            if i + AHEAD < TT:
                scale_of(i + AHEAD)
            if i >= 0:
                gate(i)
            if i == 0:
                for f in range(KT):
                    low("b", f)
                column_term(2)
                column_term(3)
            if i >= 1:
                add_out(i - 1)
        low("z", TT - 1)
        add_out(TT - 1)

    @block.tensor
    def _(pe):
        def lb_free(kind, f):
            if LB[kind, f] >= 2:
                pe.wait_ge(f_lo, LB[kind, f] - 1)

        def pb_free(kind, f):
            n = PB[kind, f] - 2
            if n < 0:
                return
            was = pb_order[n][0]
            s = {"col": col_done, "mul": m_read, "out": o_added}[was]
            pe.wait_ge(s, sum(x[0] == was for x in pb_order[:n + 1]))

        def turn_fill(kind, f):
            b = lb[LB[kind, f] % 2]
            lb_free(kind, f)
            if kind == "x":
                if f % 2 == 0:
                    pe.wait_ge(n_done, f // 2 + 1)
                blocks = [(b[:, k, :], norm[:, (4 * (f % 2) + k) * P:(4 * (f % 2) + k + 1) * P]) for k in range(4)]
            elif kind == "a":
                pe.wait_ge(w_in[(f // 2) % 2], 16 * (f // 4 + 1))
                blocks = [(b[:, k, :], wraw[:, (f // 2) % 2, (4 * (f % 2) + k) * P:(4 * (f % 2) + k + 1) * P])
                          for k in range(4)]
            elif kind == "b":
                m = f // 2
                pe.wait_ge(w_in[m % 2], 16 * (2 + m // 2 + 1))
                blocks = [(b[:, j, :], wraw[:, m % 2, (f % 2) * N + j * P:(f % 2) * N + (j + 1) * P]) for j in range(NT)]
            elif kind == "r":
                pe.wait_ge(r_in, 16)
                blocks = [(router_bank(b)[:, k, :], rraw[:, k * P:(k + 1) * P]) for k in range(KT)]
            elif kind == "k":
                pe.wait_ge(k_in, 16)
                blocks = [(b[0:ROUTER, 0, 0:EXPERTS], kraw[:])]
            else:
                pe.wait_ge(z_gated, f + 1)
                blocks = [(b[:, j, :], zg[:, j * P:(j + 1) * P]) for j in range(NT)]
            for dst, src in blocks:
                rows = src.shape[0]
                ins = nc.tensor.transpose(dst, src, ident[0:rows, 0:rows])
            ins.then_inc(f_turned, 1)

        def turn_quantised(t):
            pe.wait_ge(v_quant, t + 1)
            if t >= 1:
                pe.wait_ge(q_copied, t)
            for k in range(KT):
                ins = nc.tensor.transpose(qb[:, k, :], q1[:, t % 2, k * P:(k + 1) * P], identb[:])
            ins.then_inc(q_turned, 1)

        def column_sums(n):
            b = n // 2
            pb_free("col", n)
            for k in range(KT):
                ins = nc.tensor.matmul(pb[PB["col", n] % 2][:], one[:], q2[:, b * KT + k, (n % 2) * 512:(n % 2) * 512 + 512],
                                       start=(k == 0), stop=(k == KT - 1))
            ins.then_inc(p_done, 1)

        def multiply(t):
            pe.wait_ge(q_copied, t + 1)
            for k in range(KT):
                ins = nc.tensor.matmul(rb[:, t, :], q1T[:, t % 2, k, :], one[:, 0:2], start=(k == 0), stop=(k == KT - 1))
            ins.then_inc(summed, 1)
            if t == TPB:
                pe.wait_ge(q2_in[1], 16)
            for half in range(2):
                pb_free("mul", 2 * t + half)
                for k in range(KT):
                    ins = nc.tensor.matmul(pb[PB["mul", 2 * t + half] % 2][:], q1T[:, t % 2, k, :],
                                           q2[:, (t // TPB) * KT + k, half * 512:half * 512 + 512],
                                           start=(k == 0), stop=(k == KT - 1))
                ins.then_inc(p_done, 1)

        def router_query(t):
            pe.wait_ge(f_lo, LB["x", 2 * t + 1] + 1)
            if t >= 1:
                pe.wait_ge(s_read, t)
            for k in range(KT):
                for p, (a, c) in enumerate(PASSES):
                    ins = nc.tensor.matmul(sbk[:, 0:P], rT[a][:, k, :], xe[c][:, k, :],
                                           start=(k == 0 and p == 0), stop=(k == KT - 1 and p == 2))
            ins.then_inc(r_done, 1)

        def router_score(t):
            pe.wait_ge(r_read, t + 1)
            nc.tensor.matmul(sbk[:, 0:EXPERTS], qT[:], keysT[:], start=True, stop=True).then_inc(s_done, 1)

        def hidden(t, ks):
            if ks[0] == 0 and t >= 1:
                pe.wait_ge(z_gated, t)
            for k in ks:
                for p, (a, c) in enumerate(PASSES):
                    ins = nc.tensor.matmul(zb[:], xe[a][:, k, :], aT[c][:, k, :],
                                           start=(k == 0 and p == 0), stop=(k == KT - 1 and p == 2))
            if ks[-1] == KT - 1:
                ins.then_inc(z_done, 1)

        def expand(t):
            pe.wait_ge(f_lo, LB["z", t] + 1)
            for half in range(2):
                pb_free("out", 2 * t + half)
                for j in range(NT):
                    for p, (a, c) in enumerate(PASSES):
                        ins = nc.tensor.matmul(pb[PB["out", 2 * t + half] % 2][:], zT[a][:, j, :],
                                               bT[c][:, j, half * 512:half * 512 + 512],
                                               start=(j == 0 and p == 0), stop=(j == NT - 1 and p == 2))
                ins.then_inc(p_done, 1)

        turn_quantised(0)
        pe.wait_ge(ones_made, 1)
        pe.wait_ge(q2_in[0], 16)
        column_sums(0)
        column_sums(1)
        for i in turns:
            if i >= 0:
                turn_fill("x", 2 * i)
                turn_fill("x", 2 * i + 1)
            if i + AHEAD < TT:
                multiply(i + AHEAD)
            for f in a_turn.get(i, ()):
                turn_fill("a", f)
            if i == -1:
                turn_fill("r", 0)
                turn_fill("k", 0)
            if i >= 0:
                router_query(i)
                hidden(i, range(0, KT // 2))
                router_score(i)
                hidden(i, range(KT // 2, KT))
            if i == 0:
                for f in range(KT):
                    turn_fill("b", f)
                pe.wait_ge(q2_in[1], 16)
                column_sums(2)
                column_sums(3)
            if i + 3 < TT:
                turn_quantised(i + 3)
            if i >= 1:
                expand(i - 1)
            if i >= 0:
                turn_fill("z", i)
        expand(TT - 1)


def rope_tables():
    inv_freq = (np.float32(1.0) / np.power(np.float32(ROPE_THETA), np.arange(0, HEAD, 2, dtype=np.float32) / np.float32(HEAD))).astype(np.float32)
    freqs = np.outer(np.arange(512, dtype=np.float32), inv_freq).astype(np.float32)
    cos = np.cos(freqs).T
    sin = np.sin(freqs).T
    return (np.ascontiguousarray(np.concatenate([cos, cos]), np.float32),
            np.ascontiguousarray(np.concatenate([sin, -sin]), np.float32))


_INS = ["x", "ctx_4096", "L0_attn_Wq", "L0_attn_Wk", "L0_attn_Wv", "L0_attn_Wo", "L0_xattn_x1_scale",
        "L0_xattn_x1_zp", "L0_xattn_x2_scale", "L0_xattn_x2_zp", "L0_ffn_A_w", "L0_ffn_B_w",
        "L0_ffn_Wq_w", "L0_ffn_keys"]


def kernel(**inputs):
    import concourse.bacc as bacc
    from concourse.bass_utils import run_bass_kernel_spmd

    nc = bacc.Bacc("TRN2", target_bir_lowering=False, num_devices=1, **BACC)
    arrays = {f"in_{n}": np.ascontiguousarray(inputs[n]) for n in _INS}
    arrays["in_cos"], arrays["in_sin"] = rope_tables()
    args = [nc.dram_tensor(n, a.shape, mybir.dt.from_np(a.dtype), kind="ExternalInput").ap() for n, a in arrays.items()]
    x = arrays["in_x"]
    out = nc.dram_tensor("out", x.shape, F32, kind="ExternalOutput").ap()
    build(nc, *args, out)
    r = run_bass_kernel_spmd(nc, [arrays], core_ids=[0])
    return r.results[0]["out"]
```

```python
from contextlib import ExitStack

import numpy as np

import concourse.bass as bass
from concourse import mybir

BACC = {"dynamic_dma_scratch_size": 2048}
P = 128
ALU = mybir.AluOpType
ACT = mybir.ActivationFunctionType
F32 = mybir.dt.float32
F32R = mybir.dt.float32r
BF16 = mybir.dt.bfloat16

HEAD = 128
GROUPS = 8
HPG = 4
ROPE_THETA = 10000.0
EPS = 1e-5
EXPERTS, RANK, TOP_K, ROUTER = 64, 8, 16, 16
SCALING = 32 / TOP_K
MAGIC = 1.5 * 2.0 ** 23
MIDDLE = 128.0
NEVER = -3.0e38
MASKED = -1.0e30

BODY = ["Q1", "Q2", "Q3", "Q0'", "K'", "V'", "A0", "A1", "B0", "B1"]
LAST = ["Q1", "Q2", "Q3", "A0", "A1", "B0", "B1"]
FIRST = ["Q0'", "K'", "V'"]
PLACE = dict(zip(BODY, [2, 0, 1, 2, 0, 1, 0, 2, 1, 0]))
OPENING = 2 * len(FIRST)
PIECES = 28
EARLY = 6
ROPED = 10
SCORE_AT = {3: (0, 0), 2: (1, 0), 1: (2, 0), 0: (1, 384)}
PROB_AT = {3: 0, 2: 512, 1: 896, 0: 1152}
TILE_ORDER = (3, 2, 0, 1)
TILES_NEEDED = (1, 3, 3, 4)
KEYS_AT = {0: 0, 1: 512, 3: 896, 2: 1024}
CHUNKS = ((0, (0,)), (512, (1, 3)), (1024, (2,)))
CHUNK_WIDTH = (512, 512, 256)


def build(nc, x, ctx_in, Wq, Wk, Wv, Wo, x1s, x1z, x2s, x2z, A_w, B_w, Wr, keys, cos_in, sin_in, out):
    NB, S, D = x.shape
    KT = D // P
    TT = NB * S // P
    TPB = TT // NB
    H = S

    x_t = x.rearrange("b (t p) d -> (b t) p d", p=P)
    out_t = out.rearrange("b (t p) d -> (b t) p d", p=P)

    def hold(es):
        def sb(name, shape, dt):
            return es.enter_context(nc.sbuf_tensor(name, shape, dt))

        def sem(name):
            return es.enter_context(nc.semaphore(name))
        return sb, sem

    with ExitStack() as whole:
        sb, _ = hold(whole)
        resid = sb("resid", [P, TT, D], F32)
        ident = sb("ident", [P, P], F32)
        identb = sb("identb", [P, P], BF16)
        stats = sb("stats", [P, TT, 2, 6], F32)
        moments = sb("moments", [P, TT, 2], F32)
        rstd = sb("rstd", [P, TT], F32)
        lnw = sb("lnw", [P, 4, TT], F32)

        mean_rstd = sb("mean_rstd", [P, TT], F32)
        scal = sb("scal", [P, 4], F32)
        calc = sb("calc", [P, 10], F32)
        scl = sb("scl", [P, 2, TT], F32)
        one = sb("one", [P, P], BF16)
        raw = sb("raw", [P, 2, D], F32)
        with ExitStack() as first:
            xn = [first.enter_context(nc.sbuf_tensor(f"xn_{n}", [P, KT, TT * P], F32R)) for n in ("hi", "lo")]
        NR = EXPERTS * RANK
        a_rows = sb("a_rows", [P, NR // P, D], F32)
        b_rows = sb("b_rows", [P, D // P, NR], F32)
        q2 = sb("q2", [P, NB * KT, D], BF16)
        banks = whole.enter_context(nc.psum_tensor("banks", [P, 8, 512], F32))
        q2_dram = nc.dram_tensor("q2_dram", [NB * D, D], BF16, kind="Internal").ap()
        shared = (resid, ident, identb, stats, moments, rstd, lnw, mean_rstd, scal, calc, scl, one, raw,
                  a_rows, b_rows, q2, banks, KT, TT, TPB, H)

        with ExitStack() as es:
            attention(nc, hold(es), es, x_t, Wq, Wk, Wv, Wo, cos_in, sin_in, (x1s, x1z, x2s, x2z),
                      ctx_in.rearrange("b k n -> (b k) n"), q2_dram, A_w, B_w, xn, *shared)
        with ExitStack() as es:
            mix_and_experts(nc, hold(es), es, out_t, Wr, keys, *shared)


class Links:

    def __init__(self, eng, s):
        self.eng, self.s, self.n = eng, s, 0

    def __call__(self, ins):
        self.n += 1
        ins.then_inc(self.s, 1)
        self.eng.wait_ge(self.s, self.n)


def row_stats(nc, resid, stats, moments, t, link):
    nc.vector.bn_stats(stats[:, t, 0, :], resid[:, t, 0:512])
    link(nc.vector.bn_stats(stats[:, t, 1, :], resid[:, t, 512:1024]))
    link(nc.vector.bn_aggr(moments[:, t, :], stats[:, t, :, :]))


def quant_constants(nc, scal, calc, D, link):
    S1, Z1, S2, Z2 = (scal[:, n:n + 1] for n in range(4))
    R1, R2, Z1M, Z2M, S12, COL, ROW, BOTH, T0, T1 = (calc[:, n:n + 1] for n in range(10))
    nc.vector.reciprocal(R1, S1)
    nc.vector.reciprocal(R2, S2)
    nc.vector.tensor_scalar(Z1M, Z1, -MIDDLE, None, ALU.add)
    nc.vector.tensor_scalar(Z2M, Z2, -MIDDLE, None, ALU.add)
    link(nc.vector.tensor_tensor(S12, S1, S2, ALU.mult))
    nc.vector.tensor_tensor(T0, Z1M, S12, ALU.mult)
    link(nc.vector.tensor_tensor(T1, Z2M, S12, ALU.mult))
    nc.vector.tensor_scalar(COL, T0, -1.0, None, ALU.mult)
    nc.vector.tensor_scalar(ROW, T1, -1.0, None, ALU.mult)
    link(nc.vector.tensor_tensor(BOTH, T0, Z2M, ALU.mult))
    link(nc.vector.tensor_scalar(BOTH, BOTH, float(D), None, ALU.mult))


def row_scale_in(nc, moments, lnw, ts, var_ready):
    nc.vector.tensor_scalar(lnw[:, 0, ts], moments[:, ts, 1], EPS, None, ALU.add).then_inc(var_ready, 1)


def row_scale_out(nc, lnw, rstd, ts, link):
    link(nc.vector.reciprocal(lnw[:, 2, ts], lnw[:, 1, ts]))
    link(nc.vector.tensor_tensor(lnw[:, 3, ts], lnw[:, 0, ts], lnw[:, 2, ts], ALU.mult))
    link(nc.vector.tensor_tensor(lnw[:, 2, ts], lnw[:, 3, ts], lnw[:, 1, ts], ALU.add))
    link(nc.vector.tensor_scalar(lnw[:, 3, ts], lnw[:, 2, ts], 0.5, None, ALU.mult))
    link(nc.vector.reciprocal(rstd[:, ts], lnw[:, 3, ts]))


def attention(nc, held, es, x_t, Wq, Wk, Wv, Wo, cos_in, sin_in, quant_in, ctx_rows, q2_rows, A_w, B_w, xn,
              resid, ident, identb, stats, moments, rstd, lnw, mean_rstd, scal, calc, scl, one, raw,
              a_rows, b_rows, q2, banks, KT, TT, TPB, H):
    sb, sem = held
    SCALE = float(HEAD) ** -0.5
    D = KT * P

    kT = [sb(f"kT_{n}", [P, 2, H], F32R) for n in ("hi", "lo")]
    vv = [sb(f"v_{n}", [P, 2, TPB, HEAD], F32R) for n in ("hi", "lo")]
    qo = [sb(f"qo_{n}", [P, HPG + 1, 2, H], F32R) for n in ("hi", "lo")]
    ring = [sb(f"ring_{n}", [P, 3, D], F32R) for n in ("hi", "lo")]
    prob = sb("prob", [P, 1280], F32)
    pT = [sb(f"pT_{n}", [P, 1280], F32R) for n in ("hi", "lo")]
    rope = sb("rope", [P, 2, H], F32)
    cos = sb("cos", [P, H], F32)
    sin = sb("sin", [P, H], F32)
    mask = sb("mask", [P, H], F32)
    shift = sb("shift", [P, 4], F32)
    spare = sb("spare", [P, D], F32)
    cq = sb("cq", [P, D], BF16)
    total = sb("total", [P, 4], F32)
    inv = sb("inv", [P, 4], F32)

    score = banks[:, 0:3, :]
    turned = banks[:, 3:5, :]
    mixed = banks[:, 5, :]
    bank = [banks[:, 6, :], banks[:, 7, :]]

    q2_in = [sem(f"q2_in{b}") for b in range(TT // TPB)]
    rows_in = sem("rows_in")
    one_made, scl_done = sem("one_made"), sem("scl_done")
    x_in = [sem(f"x_in{t}") for t in range(TT)]
    tables_in = sem("tables_in")
    ident_made = sem("ident_made")
    pool_link = sem("pool_link")
    var_ready, root_ready = sem("var_ready"), sem("root_ready")
    dve_link = sem("dve_link")
    scaled_mean = sem("scaled_mean")
    scal_in, ctx_in_sem = sem("scal_in"), sem("ctx_in")
    c_scaled, c_rounded, c_quant, c_stored = sem("c_scaled"), sem("c_rounded"), sem("c_quant"), sem("c_stored")
    ln_out_v = sem("ln_out_v")
    ln_out, ln_turned, ln_hi, ln_lo = sem("ln_out"), sem("ln_turned"), sem("ln_hi"), sem("ln_lo")
    raw_in = [sem("raw_in0"), sem("raw_in1")]
    block_hi, block_lo = sem("block_hi"), sem("block_lo")
    piece_done = sem("piece_done")
    a0_used = sem("a0_used")
    added = sem("added")
    rope_parts, rope_sum, rope_hi, rope_done = (sem("rope_parts"), sem("rope_sum"), sem("rope_hi"),
                                                sem("rope_done"))
    v_staged, v_turned, v_hi, v_done = sem("v_staged"), sem("v_turned"), sem("v_hi"), sem("v_done")
    score_done = sem("score_done")
    score_seen = sem("score_seen")
    masked_done = sem("masked_done")
    exp_done = sem("exp_done")
    inv_done, prob_done = sem("inv_done"), sem("prob_done")
    turn_done, pT_hi, pT_lo = sem("turn_done"), sem("pT_hi"), sem("pT_lo")
    mix_done, o_hi, o_lo = sem("mix_done"), sem("o_hi"), sem("o_lo")

    Z2, R2 = scal[:, 3:4], calc[:, 1:2]

    def as32(ap):
        return ap.bitcast(F32)

    place_of = ("prob", "spare", "rope", "prob", "spare", "prob", "spare", "prob")
    before_of = (None, None, None, 0, 1, 3, 4, 5)
    by_vector = (True, False, True, False, True, False, True, False)

    def stage(t):
        return {"prob": prob[:, 0:D], "spare": spare[:], "rope": rope[:].rearrange("p a b -> p (a b)")}[place_of[t]]

    def o_place(h):
        return HPG if h == 0 else h

    def number(g, name, last):
        return len(FIRST) + len(BODY) * g + (LAST if last else BODY).index(name)

    def first_wo(last):
        return 6 + EARLY if last else 12

    def freed(g, name, last):
        base = OPENING + PIECES * g
        return {"Q1": base, "Q2": base, "Q3": base, "Q0'": base + 2, "K'": base + 4, "V'": base + 6,
                "A0": base + (4 if last else 10), "A1": base + (2 if last else 8),
                "B0": base + (6 if last else 12)}[name]

    def source(g, name):
        if name[0] in "QKV":
            w, col = {"Q": (Wq, HPG), "K": (Wk, 1), "V": (Wv, 1)}[name[0]]
            head = g + 1 if name.endswith("'") else g
            head = head * col + (int(name[1]) if name[0] == "Q" else 0)
            return (w[:, bass.ds(head * HEAD, HEAD)].rearrange("(k p) c -> p k c", p=P), KT)
        half, pair = "AB".index(name[0]), int(name[1])
        return (Wo[bass.ds((g * HPG + 2 * pair) * HEAD, 2 * HEAD), half * 512:half * 512 + 512]
                .rearrange("(k p) c -> p k c", p=P), 2)

    block = es.enter_context(nc.Block())

    @block.sync
    def _(sp):
        def load(g, name, last, n, slot):
            if not isinstance(n, int) or n >= 2:
                sp.wait_ge(block_lo, n - 1)
            src, k = source(g, name)
            sp.dma_start(raw[:, slot, :].rearrange("p (k c) -> p k c", k=k), src).then_inc(raw_in[slot], 16)

        for t in range(TT):
            sp.dma_start(resid[:, t, :], x_t[t]).then_inc(x_in[t], 16)
            if t == TPB - 1:
                load(-1, "Q0'", False, 0, 0)
            if t == TPB + 1:
                load(-1, "K'", False, 1, 1)
        for n, v in enumerate(quant_in):
            sp.dma_start(scal[:, n:n + 1], v.rearrange("(a b) -> a b", a=1).to_broadcast([P, 1])).then_inc(scal_in, 16)
        sp.dma_start(cos[:], cos_in).then_inc(tables_in, 16)
        sp.dma_start(sin[:], sin_in).then_inc(tables_in, 16)
        load(-1, "V'", False, 2, 0)
        with sp.Fori(0, GROUPS - 1) as g:
            for i, name in enumerate(BODY):
                load(g, name, False, g * len(BODY) + (3 + i), (3 + i) % 2)
        for i, name in enumerate(LAST):
            n = number(GROUPS - 1, name, True)
            load(GROUPS - 1, name, True, n, n % 2)
        sp.wait_ge(piece_done, OPENING + PIECES * (GROUPS - 1) + 6)
        sp.dma_start(a_rows[:], A_w.rearrange("(n p) c -> p n c", p=P)).then_inc(rows_in, 16)
        sp.dma_start(b_rows[:], B_w.rearrange("(n p) c -> p n c", p=P)).then_inc(rows_in, 16)
        for b in range(TT // TPB):
            if b == 1:
                sp.wait_ge(c_stored, 16 * 2 * GROUPS)
            else:
                sp.wait_ge(c_stored, 16 * KT)
            sp.dma_start(q2[:, b * KT:(b + 1) * KT, :],
                         q2_rows[b * D:(b + 1) * D, :].rearrange("(k p) n -> p k n", p=P)).then_inc(q2_in[b], 16)
        sp.wait_ge(rows_in, 32)

    @block.gpsimd
    def _(pool):
        link = Links(pool, pool_link)
        link(nc.gpsimd.memset(ident[:], 0.0))
        link(nc.gpsimd.memset(mask[:], 0.0))
        nc.gpsimd.affine_select(out=ident[:], in_=ident[:], compare_op=ALU.not_equal, fill=1.0, base=0,
                                pattern=[[-1, P]], channel_multiplier=1).then_inc(ident_made, 1)
        nc.gpsimd.affine_select(out=mask[:, H - P:H], in_=mask[:, H - P:H], compare_op=ALU.is_ge, fill=MASKED,
                                base=0, pattern=[[-1, P]], channel_multiplier=1).then_inc(ident_made, 1)
        pool.wait_ge(ident_made, 2)
        nc.gpsimd.tensor_copy(identb[:], ident[:]).then_inc(ident_made, 1)
        nc.gpsimd.memset(one[:], 1.0).then_inc(one_made, 1)

        def split(n, name, slot):
            pool.wait_ge(block_hi, n + 1)
            nc.gpsimd.tensor_tensor(ring[1][:, PLACE[name], :], raw[:, slot, :],
                                    as32(ring[0][:, PLACE[name], :]), ALU.subtract).then_inc(block_lo, 1)

        def rope_add(n):
            pool.wait_ge(rope_parts, n + 1)
            nc.gpsimd.tensor_tensor(rope[:, 0, :], rope[:, 0, :], rope[:, 1, :], ALU.add).then_inc(rope_sum, 1)

        def body(g, last):
            def sp(name):
                if last:
                    n = number(g, name, True)
                    split(n, name, n % 2)
                else:
                    i = BODY.index(name)
                    split(g * len(BODY) + (3 + i), name, (3 + i) % 2)
            rb = g * ROPED + 4
            sp("Q2")
            rope_add(rb)
            sp("Q3")
            rope_add(rb + 1)
            if last:
                rope_add(rb + 2)
                rope_add(rb + 3)
                sp("A0")
                rope_add(rb + 4)
                sp("A1")
                rope_add(rb + 5)
                sp("B0")
                sp("B1")
                return
            sp("Q0'")
            rope_add(rb + 2)
            rope_add(rb + 3)
            sp("K'")
            rope_add(rb + 4)
            rope_add(rb + 5)
            sp("V'")
            for n in range(6, 10):
                rope_add(rb + n)
            sp("A0")
            sp("A1")
            sp("B0")
            sp("B1")
            split(g * len(BODY) + 13, "Q1", 1)

        split(0, "Q0'", 0)
        split(1, "K'", 1)
        split(2, "V'", 0)
        rope_add(0)
        rope_add(1)
        rope_add(2)
        split(3, "Q1", 1)
        rope_add(3)
        with pool.Fori(0, GROUPS - 1) as g:
            body(g, False)
        body(GROUPS - 1, True)

    @block.scalar
    def _(act):
        def root(n):
            act.wait_ge(var_ready, n + 1)
            h = n % 2
            nc.scalar.activation(lnw[:, 1, h * TPB:(h + 1) * TPB], lnw[:, 0, h * TPB:(h + 1) * TPB],
                                 ACT.Sqrt).then_inc(root_ready, 1)

        def ln_scale(t):
            act.wait_ge(scaled_mean, 1 if t < TPB else 2)
            if before_of[t] is not None:
                act.wait_ge(ln_turned, 2 * before_of[t] + 2)
            nc.scalar.activation(stage(t), resid[:, t, :], ACT.Identity, bias=mean_rstd[:, t:t + 1],
                                 scale=rstd[:, t:t + 1]).then_inc(ln_out, 1)

        def ln_high(t):
            for n in (2 * t, 2 * t + 1):
                k0 = 4 * (n % 2)
                act.wait_ge(ln_turned, n + 1)
                nc.scalar.copy(xn[0][:, k0:k0 + 4, t * P:(t + 1) * P], ln_bank(score, turned, n)).then_inc(ln_hi, 1)

        def split(n, name, slot, uses, free):
            act.wait_ge(raw_in[slot], uses)
            if name == "B1":
                act.wait_ge(a0_used, free)
            elif free is not None:
                act.wait_ge(piece_done, free)
            nc.scalar.copy(ring[0][:, PLACE[name], :], raw[:, slot, :]).then_inc(block_hi, 1)

        def rope_high(n, dst):
            act.wait_ge(rope_sum, n + 1)
            nc.scalar.copy(dst, rope[:, 0, :]).then_inc(rope_hi, 1)

        def v_high(n, b):
            act.wait_ge(v_turned, n + 1)
            nc.scalar.copy(vv[0][:, b, :, :], turned[:, b, :].rearrange("p (j c) -> p j c", c=HEAD)).then_inc(v_hi, 1)

        def body(g, last):
            def sp(name):
                if last:
                    n = number(g, name, True)
                    split(n, name, n % 2, 16 * (n // 2 + 1), g + 1 if name == "B1" else freed(g, name, True))
                else:
                    i = BODY.index(name)
                    slot = (3 + i) % 2
                    split(None, name, slot, g * (16 * len(BODY) // 2) + 16 * ((3 + i) // 2 + 1),
                          g + 1 if name == "B1" else freed(g, name, False))
            rb = g * ROPED + 4
            ub = g * 8

            def probs_high(u):
                for c in range(3):
                    act.wait_ge(turn_done, ub * 3 + (3 * u + c + 1))
                    if c == 0 and u > 0:
                        act.wait_ge(mix_done, ub + u)
                    nc.scalar.copy(pT[0][:, CHUNKS[c][0]:CHUNKS[c][0] + CHUNK_WIDTH[c]],
                                   turned_chunk(turned, mixed, c)).then_inc(pT_hi, 1)

            def exps(u):
                for n, i in enumerate(TILE_ORDER):
                    sl = slice(PROB_AT[i], PROB_AT[i] + P * (i + 1))
                    act.wait_ge(masked_done, ub * 4 + (4 * u + n + 1))
                    nc.scalar.activation(prob[:, sl], prob[:, sl], ACT.Exp, bias=shift[:, i:i + 1], scale=-1.0,
                                         accum_out=total[:, i:i + 1]).then_inc(exp_done, 1)

            def out_high(u):
                act.wait_ge(mix_done, ub + (u + 1))
                nc.scalar.copy(qo[0][:, o_place(u // 2), u % 2, :], mixed[:]).then_inc(o_hi, 1)

            def scale_ctx(j):
                act.wait_ge(ctx_in_sem, g * 32 + 16 * (j + 1))
                nc.scalar.activation(spare[:], spare[:], ACT.Identity, bias=Z2, scale=R2).then_inc(c_scaled, 1)

            def store_ctx(j):
                act.wait_ge(c_quant, g * 2 + (j + 1))
                act.dma_start(q2_rows[bass.ds((g * 2 + j) * P, P), :], cq[:]).then_inc(c_stored, 16)

            load_ctx(g * 2)
            for u in range(8):
                if u > 0:
                    probs_high(u - 1)
                    if u < 7 or not last:
                        h = u - 1
                        rope_high(rb + h, qo[0][:, (h // 2 + 1) % HPG, h % 2, :])
                exps_first = {0: "Q2", 1: "Q3"}
                if u in exps_first:
                    sp(exps_first[u])
                elif not last and u in (2, 4, 6):
                    sp({2: "Q0'", 4: "K'", 6: "V'"}[u])
                elif last and u in (4, 5, 6):
                    sp({4: "A0", 5: "A1", 6: "B0"}[u])
                exps(u)
                if u > 0:
                    out_high(u - 1)
            probs_high(7)
            if last:
                out_high(7)
                scale_ctx(0)
                store_ctx(0)
                load_ctx(g * 2 + 1)
                sp("B1")
                scale_ctx(1)
                store_ctx(1)
                root(2)
                act.wait_ge(block_lo, number(g, "B1", True) + 1)
                act.wait_ge(scl_done, 1)
                for t in range(2):
                    nc.scalar.activation(raw[:, t, :], resid[:, t, :], ACT.Identity, bias=scl[:, 1, t:t + 1],
                                         scale=scl[:, 0, t:t + 1])
                root(3)
                return
            rope_high(rb + 7, qo[0][:, 0, 1, :])
            rope_high(rb + 8, kT[0][:, 0, :])
            out_high(7)
            rope_high(rb + 9, kT[0][:, 1, :])
            sp("A0")
            sp("A1")
            sp("B0")
            v_high(g * 2 + 2, 0)
            v_high(g * 2 + 3, 1)
            scale_ctx(0)
            store_ctx(0)
            load_ctx(g * 2 + 1)
            sp("B1")
            split(None, "Q1", 1, g * (16 * len(BODY) // 2) + 16 * 7, OPENING + PIECES * g + 12 + TT)
            scale_ctx(1)
            store_ctx(1)

        def load_ctx(n):
            act.dma_start(spare[:], ctx_rows[bass.ds(n * P, P), :]).then_inc(ctx_in_sem, 16)

        root(0)
        ln_scale(1)
        ln_high(0)
        split(0, "Q0'", 0, 16, None)
        ln_high(1)
        ln_scale(3)
        ln_high(2)
        ln_high(3)
        split(1, "K'", 1, 16, None)
        root(1)
        split(2, "V'", 0, 32, None)
        ln_scale(5)
        ln_high(4)
        ln_high(5)
        ln_scale(7)
        rope_high(0, qo[0][:, 0, 0, :])
        ln_high(6)
        ln_high(7)
        rope_high(1, kT[0][:, 0, :])
        v_high(0, 0)
        rope_high(2, qo[0][:, 0, 1, :])
        split(3, "Q1", 1, 32, 4)
        rope_high(3, kT[0][:, 1, :])
        v_high(1, 1)
        with act.Fori(0, GROUPS - 1) as g:
            body(g, False)
        body(GROUPS - 1, True)

    @block.vector
    def _(dve):
        link = Links(dve, dve_link)

        def ln_low(n):
            t, k0 = n // 2, 4 * (n % 2)
            dve.wait_ge(ln_hi, n + 1)
            nc.vector.tensor_tensor(xn[1][:, k0:k0 + 4, t * P:(t + 1) * P], ln_bank(score, turned, n),
                                    as32(xn[0][:, k0:k0 + 4, t * P:(t + 1) * P]), ALU.subtract).then_inc(ln_lo, 1)

        def ln_rows(h):
            ts = slice(h * TPB, (h + 1) * TPB)
            dve.wait_ge(root_ready, h + 1)
            row_scale_out(nc, lnw, rstd, ts, link)
            nc.vector.scalar_tensor_tensor(mean_rstd[:, ts], moments[:, ts, 0], -1.0, rstd[:, ts],
                                           ALU.mult, ALU.mult).then_inc(scaled_mean, 1)

        def ln_stats(t):
            dve.wait_ge(x_in[t], 16)
            row_stats(nc, resid, stats, moments, t, link)

        def ln_scale(t):
            dve.wait_ge(scaled_mean, t // TPB + 1)
            if before_of[t] is not None:
                dve.wait_ge(ln_turned, 2 * before_of[t] + 2)
            nc.vector.tensor_scalar(stage(t), resid[:, t, :], rstd[:, t:t + 1], mean_rstd[:, t:t + 1],
                                    ALU.mult, ALU.add).then_inc(ln_out_v, 1)

        for t in range(TPB):
            ln_stats(t)
        row_scale_in(nc, moments, lnw, slice(0, TPB), var_ready)
        ln_rows(0)
        ln_scale(0)
        ln_scale(2)
        ln_stats(TPB)
        for n in range(TT):
            ln_low(n)
        for t in range(TPB + 1, TT):
            ln_stats(t)
        row_scale_in(nc, moments, lnw, slice(TPB, TT), var_ready)
        ln_rows(1)
        ln_scale(4)

        def rope_products(m, n):
            b = bank[m[1]]
            if not isinstance(n, int) or n > 0:
                dve.wait_ge(rope_done, n)
            dve.wait_ge(piece_done, m[0] + 1)
            nc.vector.tensor_tensor(rope[:, 0, :], b[:], cos[:], ALU.mult)
            nc.vector.tensor_tensor(rope[0:64, 1, :], b[64:128, :], sin[64:128, :], ALU.mult)
            (nc.vector.tensor_tensor(rope[64:128, 1, :], b[0:64, :], sin[0:64, :], ALU.mult)
             .then_inc(rope_parts, 1))

        def rope_low(n, hi, lo):
            dve.wait_ge(rope_hi, n + 1)
            nc.vector.tensor_tensor(lo, rope[:, 0, :], as32(hi), ALU.subtract).then_inc(rope_done, 1)

        def v_stage(m, n, b):
            dve.wait_ge(rope_done, n)
            dve.wait_ge(piece_done, m[0] + 1)
            nc.vector.tensor_copy(rope[:, b, :], bank[m[1]][:]).then_inc(v_staged, 1)

        def v_low(n, b):
            dve.wait_ge(v_hi, n + 1)
            nc.vector.tensor_tensor(vv[1][:, b, :, :], turned[:, b, :].rearrange("p (j c) -> p j c", c=HEAD),
                                    as32(vv[0][:, b, :, :]), ALU.subtract).then_inc(v_done, 1)

        def quant_rows(h):
            ts = slice(h * TPB, (h + 1) * TPB)
            dve.wait_ge(root_ready, h + 3)
            row_scale_out(nc, lnw, rstd, ts, link)
            link(nc.vector.tensor_scalar(scl[:, 0, ts], rstd[:, ts], calc[:, 0:1], None, ALU.mult))
            link(nc.vector.tensor_tensor(lnw[:, 2, ts], moments[:, ts, 0], scl[:, 0, ts], ALU.mult))
            nc.vector.tensor_scalar(scl[:, 1, ts], lnw[:, 2, ts], -1.0, scal[:, 1:2], ALU.mult,
                                    ALU.add).then_inc(scl_done, 1)

        def body(g, last):
            rb, ub = g * ROPED + 4, g * 8
            mb = OPENING + PIECES * g if isinstance(g, int) else g * PIECES + OPENING

            def m(j):
                return mb + j, j % 2

            def probs_low(u):
                for c in range(3):
                    sl = slice(CHUNKS[c][0], CHUNKS[c][0] + CHUNK_WIDTH[c])
                    dve.wait_ge(pT_hi, ub * 3 + (3 * u + c + 1))
                    nc.vector.tensor_tensor(pT[1][:, sl], turned_chunk(turned, mixed, c), as32(pT[0][:, sl]),
                                            ALU.subtract).then_inc(pT_lo, 1)

            def peaks(u):
                for n, i in enumerate(TILE_ORDER):
                    w = P * (i + 1)
                    s, c = SCORE_AT[i]
                    if n != 2:
                        dve.wait_ge(score_done, ub * 4 + (4 * u + TILES_NEEDED[n]))
                        dve.sem_inc(score_seen, 1)
                    nc.vector.tensor_tensor_reduce(
                        out=prob[:, PROB_AT[i]:PROB_AT[i] + w], in0=score[:, s, c:c + w], in1=mask[:, H - w:H],
                        scale=-SCALE, scalar=-NEVER, op0=ALU.add, op1=ALU.min,
                        accum_out=shift[:, i:i + 1]).then_inc(masked_done, 1)

            def normalise(u):
                dve.wait_ge(exp_done, ub * 4 + (4 * u + 4))
                nc.vector.reciprocal(inv[:], total[:]).then_inc(inv_done, 1)
                dve.wait_ge(inv_done, ub + (u + 1))
                for i in TILE_ORDER:
                    sl = slice(PROB_AT[i], PROB_AT[i] + P * (i + 1))
                    ins = nc.vector.tensor_scalar(prob[:, sl], prob[:, sl], inv[:, i:i + 1], None, ALU.mult)
                ins.then_inc(prob_done, 1)

            def out_low(u):
                dve.wait_ge(o_hi, ub + (u + 1))
                nc.vector.tensor_tensor(qo[1][:, o_place(u // 2), u % 2, :], mixed[:],
                                        as32(qo[0][:, o_place(u // 2), u % 2, :]), ALU.subtract).then_inc(o_lo, 1)

            def add_piece(j, t, half):
                dve.wait_ge(piece_done, mb + (j + 1))
                sl = slice(half * 512, half * 512 + 512)
                nc.vector.tensor_tensor(resid[:, t, sl], bank[j % 2][:], resid[:, t, sl], ALU.add).then_inc(added, 1)

            def q_slot(h):
                return (h // 2 + 1) % HPG, h % 2

            for u in range(8):
                if u > 0:
                    probs_low(u - 1)
                peaks(u)
                if u > 0 and (u < 7 or not last):
                    s, b = q_slot(u - 1)
                    rope_low(rb + (u - 1), qo[0][:, s, b, :], qo[1][:, s, b, :])
                if u >= 6 and last:
                    add_piece(6 + 3 * (u - 6), 3 * (u - 6), 0)
                normalise(u)
                if u > 0:
                    out_low(u - 1)
                if u < 6 or not last:
                    rope_products(m(u), rb + u)
                else:
                    add_piece(7 + 3 * (u - 6), 1 + 3 * (u - 6), 0)
                    add_piece(8 + 3 * (u - 6), 2 + 3 * (u - 6), 0)
            probs_low(7)
            if last:
                add_piece(first_wo(last), 0, 0)
                add_piece(first_wo(last) + 1, 1, 0)
                out_low(7)
            else:
                rope_low(rb + 7, qo[0][:, 0, 1, :], qo[1][:, 0, 1, :])
                rope_products(m(8), rb + 8)
                out_low(7)
                rope_low(rb + 8, kT[0][:, 0, :], kT[1][:, 0, :])
                rope_products(m(9), rb + 9)
                rope_low(rb + 9, kT[0][:, 1, :], kT[1][:, 1, :])
                v_stage(m(10), rb + 10, 0)
                v_stage(m(11), rb + 10, 1)
                v_low(g * 2 + 2, 0)
            def quant_ctx(j):
                dve.wait_ge(c_scaled, g * 2 + (j + 1))
                nc.vector.tensor_scalar(spare[:], spare[:], MAGIC, MAGIC, ALU.add, ALU.max).then_inc(c_rounded, 1)
                dve.wait_ge(c_rounded, g * 2 + (j + 1))
                if j == 1 or not isinstance(g, int) or g > 0:
                    dve.wait_ge(c_stored, g * 32 + 16 * j)
                nc.vector.tensor_scalar(cq[:], spare[:], MAGIC + 255.0, MAGIC + MIDDLE,
                                        ALU.min, ALU.subtract).then_inc(c_quant, 1)

            w = first_wo(last)
            for half in range(2):
                for t in range(2 if half == 0 and last else 0, TT):
                    add_piece(w + half * TT + t, t, half)
                    if half == 0 and t == 0 and not last:
                        v_low(g * 2 + 3, 1)
                    if t == (3, 1)[half]:
                        quant_ctx(half)
                    if half == 1 and last:
                        dve.wait_ge(added, 2 * TT * (g + 1) + EARLY - TT + t + 2)
                        row_stats(nc, resid, stats, moments, t, link)
                        if t % TPB == TPB - 1:
                            row_scale_in(nc, moments, lnw, slice(t + 1 - TPB, t + 1), var_ready)
                        if t == TPB:
                            quant_rows(0)
            if last:
                quant_rows(1)

        dve.sem_inc(added, 1)
        dve.wait_ge(tables_in, 32)
        rope_products((0, 0), 0)
        for n in range(TT, TT + 4):
            ln_low(n)
            if n == TT + 1:
                ln_scale(6)
        rope_low(0, qo[0][:, 0, 0, :], qo[1][:, 0, 0, :])
        rope_products((1, 1), 1)
        for n in range(TT + 4, 2 * TT):
            ln_low(n)
        rope_low(1, kT[0][:, 0, :], kT[1][:, 0, :])
        v_stage((2, 0), 2, 0)
        v_low(0, 0)
        dve.wait_ge(scal_in, 64)
        quant_constants(nc, scal, calc, D, link)
        rope_products((3, 1), 2)
        rope_low(2, qo[0][:, 0, 1, :], qo[1][:, 0, 1, :])
        rope_products((4, 0), 3)
        rope_low(3, kT[0][:, 1, :], kT[1][:, 1, :])
        v_stage((5, 1), 4, 1)
        v_low(1, 1)
        with dve.Fori(0, GROUPS - 1) as g:
            body(g, False)
        body(GROUPS - 1, True)

    @block.tensor
    def _(pe):
        PASSES = ((0, 0), (0, 1), (1, 0))

        pe.wait_ge(ident_made, 3)

        def ln_turn(t):
            pe.wait_ge(ln_out_v if by_vector[t] else ln_out, t // 2 + 1)
            for n in (2 * t, 2 * t + 1):
                k0 = 4 * (n % 2)
                if n >= 4:
                    pe.wait_ge(ln_lo, n - 3)
                dst = ln_bank(score, turned, n)
                for k in range(4):
                    ins = nc.tensor.transpose(dst[:, k, :], stage(t)[:, (k0 + k) * P:(k0 + k + 1) * P], ident[:])
                ins.then_inc(ln_turned, 1)

        def project(par, name, b, n, steps=range(24)):
            place = PLACE[name]
            for s in steps:
                k, (a, c) = s // 3, PASSES[s % 3]
                if s == 0:
                    if b == 0:
                        pe.wait_ge(block_lo, n + 1)
                ins = nc.tensor.matmul(bank[par][:], ring[a][:, place, k * P:(k + 1) * P],
                                       xn[c][:, k, b * H:(b + 1) * H], start=(s == 0), stop=(s == 23))
                if s == 23:
                    ins.then_inc(piece_done, 1)

        def turn_values(n, b):
            pe.wait_ge(v_staged, n + 1)
            for j in range(TPB):
                ins = nc.tensor.transpose(turned[:, b, j * P:(j + 1) * P], rope[:, b, j * P:(j + 1) * P], ident[:])
            ins.then_inc(v_turned, 1)

        def body(g, last):
            rb, ub = g * ROPED + 4, g * 8

            def scores(u):
                h, b = u // 2, u % 2
                pe.wait_ge(rope_done, rb - 1 + u)
                if u > 0:
                    pe.wait_ge(masked_done, ub * 4 + 4 * u)
                for i in TILE_ORDER:
                    w = P * (i + 1)
                    s, c = SCORE_AT[i]
                    dst = score[:, s, c:c + w]
                    for p, (a, e) in enumerate(PASSES):
                        ins = nc.tensor.matmul(dst, qo[a][:, h, b, i * P:(i + 1) * P], kT[e][:, b, 0:w],
                                               start=(p == 0), stop=(p == 2))
                    ins.then_inc(score_done, 1)

            def turn_probs(u):
                pe.wait_ge(prob_done, ub + (u + 1))
                if u > 0:
                    pe.wait_ge(pT_lo, ub * 3 + 3 * u)
                    pe.wait_ge(o_lo, ub + u)
                for c in range(3):
                    dst = turned_chunk(turned, mixed, c)
                    for j in CHUNKS[c][1]:
                        for i in range(j, TPB):
                            col = KEYS_AT[j] - CHUNKS[c][0] + (i - j) * P
                            ins = nc.tensor.transpose(dst[:, col:col + P],
                                                      prob[:, PROB_AT[i] + j * P:PROB_AT[i] + (j + 1) * P], ident[:])
                    ins.then_inc(turn_done, 1)

            def mix(u):
                b = u % 2
                pe.wait_ge(v_done, g * 2 + (1 + b))
                pe.wait_ge(pT_lo, ub * 3 + (3 * u + 3))
                for j in range(TPB):
                    w = H - j * P
                    for p, (a, c) in enumerate(PASSES):
                        ins = nc.tensor.matmul(mixed[:, j * P:H], vv[a][:, b, j, :],
                                               pT[c][:, KEYS_AT[j]:KEYS_AT[j] + w],
                                               start=(j == 0 and p == 0), stop=(j == TPB - 1 and p == 2))
                ins.then_inc(mix_done, 1)

            def filler(u, steps):
                name = ("Q1", "Q1", "Q2", "Q2", "Q3", "Q3", "Q0'", "Q0'", "K'", "K'", "V'", "V'")[u]
                n = number(g, name, True) if last else g * len(BODY) + (3 + BODY.index(name))
                if steps[0] == 0:
                    if u < 2:
                        pe.wait_ge(added, g * (2 * TT) + 1)
                    else:
                        pe.wait_ge(rope_parts, rb + (u - 1))
                project(u % 2, name, u % 2, n, steps)

            def out_part(j, t, half, pairs, opens=True, closes=True):
                if opens:
                    before = j - 2 - (6 if last else first_wo(last))
                    if before >= 0:
                        pe.wait_ge(added, g * (2 * TT) + (before + 2))
                    elif last:
                        pe.wait_ge(rope_parts, rb + (j - 1))
                    else:
                        pe.wait_ge(v_staged, g * 2 + (before + 5))
                for pair in pairs:
                    name = "AB"[half] + str(pair)
                    if t == 0:
                        n = number(g, name, True) if last else g * len(BODY) + (3 + BODY.index(name))
                        pe.wait_ge(block_lo, n + 1)
                    for k in (2 * pair, 2 * pair + 1):
                        for p, (a, c) in enumerate(PASSES):
                            ins = nc.tensor.matmul(
                                bank[j % 2][:], qo[a][:, o_place(k), t // TPB, (t % TPB) * P:(t % TPB + 1) * P],
                                ring[c][:, PLACE[name], (k % 2) * 512:(k % 2) * 512 + 512],
                                start=(opens and k == 2 * pairs[0] and p == 0),
                                stop=(closes and k == 2 * pairs[-1] + 1 and p == 2))
                if closes:
                    ins.then_inc(piece_done, 1)
                elif half == 0 and t == TT - 1:
                    ins.then_inc(a0_used, 1)

            def early(e):
                out_part(6 + e, e, 0, (0,))

            for u in range(8):
                scores(u)
                some = u < 6 or not last
                if some:
                    filler(u, range(0, 6))
                else:
                    early(3 * (u - 6))
                if u > 0:
                    mix(u - 1)
                if some:
                    filler(u, range(6, 24))
                else:
                    early(3 * (u - 6) + 1)
                    early(3 * (u - 6) + 2)
                turn_probs(u)
            w = first_wo(last)
            if not last:
                filler(8, range(24))
            else:
                pe.wait_ge(o_lo, ub + 7)
                out_part(w, 0, 0, (1,))
                out_part(w + 1, 1, 0, (1,))
            mix(7)
            if not last:
                filler(9, range(24))
                filler(10, range(24))
                filler(11, range(24))
                turn_values(g * 2 + 2, 0)
            if last:
                out_part(w + 2, 2, 0, (1,))
                out_part(w + 3, 3, 0, (1,))
            pe.wait_ge(o_lo, ub + 8)

            def out_pair(t, half):
                for pair in range(2):
                    for n in (t, t + 1):
                        out_part(w + half * TT + n, n, half, (pair,), opens=pair == 0, closes=pair == 1)

            if last:
                for t in range(4, EARLY):
                    out_part(w + t, t, 0, (1,))
                out_pair(TT - 2, 0)
            for half in range(1 if last else 0, 2):
                out_pair(0, half)
                if half == 0 and not last:
                    turn_values(g * 2 + 3, 1)
                for t in range(2, TT - 2 if half == 0 else TT):
                    out_part(w + half * TT + t, t, half, (0, 1))
                if half == 0:
                    out_pair(TT - 2, half)

        for t in range(TPB):
            ln_turn(t)
        pe.wait_ge(ln_lo, TT)
        project(0, "Q0'", 0, 0)
        project(1, "K'", 0, 1, range(0, 9))
        ln_turn(4)
        ln_turn(5)
        project(1, "K'", 0, 1, range(9, 24))
        ln_turn(6)
        ln_turn(7)
        pe.wait_ge(rope_parts, 1)
        project(0, "V'", 0, 2)
        pe.wait_ge(ln_lo, 2 * TT)
        pe.wait_ge(rope_parts, 2)
        project(1, "Q0'", 1, 0, range(0, 9))
        turn_values(0, 0)
        project(1, "Q0'", 1, 0, range(9, 24))
        project(0, "K'", 1, 1)
        pe.wait_ge(rope_parts, 3)
        project(1, "V'", 1, 2)
        turn_values(1, 1)
        with pe.Fori(0, GROUPS - 1) as g:
            body(g, False)
        body(GROUPS - 1, True)
        pe.wait_ge(masked_done, 4 * 8 * GROUPS)
        pe.wait_ge(one_made, 1)
        for n in range(2 * TT // TPB - 1):
            if n % 2 == 0:
                pe.wait_ge(q2_in[n // 2], 16)
            for k in range(KT):
                nc.tensor.matmul(banks[:, n, :], one[:], q2[:, (n // 2) * KT + k, (n % 2) * 512:(n % 2) * 512 + 512],
                                 start=(k == 0), stop=(k == KT - 1))


def ln_bank(score, turned, n):
    b = score[:, n % 4, :] if n % 4 < 3 else turned[:, 0, :]
    return b.rearrange("p (k c) -> p k c", c=P)


def turned_chunk(turned, mixed, c):
    return turned[:, c, :] if c < 2 else mixed[:, 0:256]


def mix_and_experts(nc, held, es, out_t, Wr, keys, resid, ident, identb, stats, moments, rstd, lnw, mean_rstd,
                    scal, calc, scl, one, raw, a_rows, b_rows, q2, banks, KT, TT, TPB, H):
    sb, sem = held
    D = KT * P
    N = EXPERTS * RANK
    NT = N // P
    NB = TT // TPB
    AHEAD = 2
    PASSES = ((0, 0), (0, 1), (1, 0))

    wT = [sb(f"wT_{n}", [P, KT, EXPERTS + N], F32R) for n in ("hi", "lo")]
    bT = [sb(f"bT_{n}", [P, NT, D], F32R) for n in ("hi", "lo")]
    mT = [x[:, :, 0:EXPERTS] for x in wT]
    aT = [x[:, :, EXPERTS:] for x in wT]
    colterm = sb("colterm", [P, NB, D], F32)
    rowterm = sb("rowterm", [P, TT], F32)
    rraw = sb("rraw", [ROUTER, D], F32)
    kraw = sb("kraw", [EXPERTS, ROUTER], F32)
    keysT = sb("keysT", [ROUTER, EXPERTS], F32)
    v1 = raw
    q1 = sb("q1", [P, 2, D], BF16)
    q1T = sb("q1T", [P, 2, KT, P], BF16)
    part = sb("part", [P, 2, 512], F32)
    norm = sb("norm", [P, D], F32)
    xe = [sb(f"xe_{n}", [P, KT, P], F32R) for n in ("hi", "lo")]
    zg = sb("zg", [P, N], F32)
    zT = [sb(f"zT_{n}", [P, NT, P], F32R) for n in ("hi", "lo")]
    seen = sb("seen", [P, EXPERTS], F32)
    left = sb("left", [P, 2, EXPERTS], F32)
    weight = sb("weight", [P, 3, EXPERTS], F32)
    top = sb("top", [P, 2, 8], F32)
    peak = sb("peak", [P, 3], F32)

    pb = [banks[:, 0, :], banks[:, 1, :]]
    HALF = (EXPERTS + N) // 2
    EXPERTS_A = (HALF - EXPERTS) // RANK
    hb = [banks[:, 2, :], banks[:, 3, :]]
    mb = hb[0]
    lb = [banks[:, n, :].rearrange("p (k c) -> p k c", c=P) for n in (4, 5)]
    zb = banks[:, 6, :].rearrange("p (k c) -> p k c", c=P)
    qb = banks[:, 6, :].bitcast(BF16).rearrange("p (k c) -> p k c", c=P)
    rb = banks[:, 7, 0:2 * TT].rearrange("p (t c) -> p t c", c=2)

    r_in, k_in = sem("r_in"), sem("k_in")
    dve_link = sem("dve_link_e")
    v_scaled, v_quant, q_turned, q_copied = sem("v_scaled"), sem("v_quant"), sem("q_turned"), sem("q_copied")
    f_turned, f_hi, f_lo = sem("f_turned"), sem("f_hi"), sem("f_lo")
    p_done = sem("p_done")
    sum_done, col_done = sem("sum_done"), sem("col_done")
    summed, row_done = sem("summed"), sem("row_done")
    col_added = sem("col_added")
    m_read, m_added = sem("m_read"), sem("m_added")
    var3, root3, scale3 = sem("var3"), sem("root3"), sem("scale3")
    n_done = sem("n_done")
    mT_done, mT_hi, mT_lo = sem("mT_done"), sem("mT_hi"), sem("mT_lo")
    s_read = sem("s_read")
    z_done, z_gated = sem("z_done"), sem("z_gated")
    peak_done, exp_done = sem("peak_done"), sem("exp_done_e")
    o_added, stored = sem("o_added"), sem("stored")

    Z1, S12 = scal[:, 1:2], calc[:, 4:5]
    COL, ROW, BOTH = (calc[:, n:n + 1] for n in (5, 6, 7))

    lb_order = [("a", 0), ("a", 1), ("k", 0)] + [("a", f) for f in range(2, 8)]
    pb_order = [("mul", m) for m in range(2 * AHEAD)]
    for i in range(TT):
        lb_order += [("x", 2 * i), ("x", 2 * i + 1)]
        if i + AHEAD < TT:
            pb_order += [("mul", 2 * (i + AHEAD)), ("mul", 2 * (i + AHEAD) + 1)]
        if i == 0:
            lb_order += [("b", f) for f in range(6)]
        if i >= 1:
            lb_order += [("z", i - 1)]
            pb_order += [("out", 2 * (i - 1)), ("out", 2 * (i - 1) + 1)]
        if i == 1:
            lb_order += [("b", f) for f in range(6, 8)]
    lb_order += [("z", TT - 1)]
    pb_order += [("out", 2 * TT - 2), ("out", 2 * TT - 1)]
    LB = {f: n for n, f in enumerate(lb_order)}
    in_lb = [f for f in lb_order if f[0] != "z"]
    IN_LB = {f: n for n, f in enumerate(in_lb)}
    PB = {f: n for n, f in enumerate(pb_order)}

    def target(kind, f):
        if kind == "x":
            return [x[:, 4 * (f % 2):4 * (f % 2) + 4, :] for x in xe]
        if kind == "a":
            return [x[:, 4 * (f % 2):4 * (f % 2) + 4, (f // 2) * P:(f // 2 + 1) * P] for x in aT]
        if kind == "b":
            return [x[:, :, f * P:(f + 1) * P] for x in bT]
        return [x[:] for x in zT]

    def filled(kind, f):
        return zb if kind == "z" else lb[IN_LB[kind, f] % 2]

    block = es.enter_context(nc.Block())

    @block.sync
    def _(sp):
        sp.dma_start(kraw[:], keys).then_inc(k_in, 16)
        sp.dma_start(rraw[:], Wr).then_inc(r_in, 16)
        for t in range(TT - 1):
            sp.wait_ge(o_added, 2 * t + 2)
            sp.dma_start(out_t[t], resid[:, t, :]).then_inc(stored, 16)
        for half in range(2):
            sl = slice(half * 512, half * 512 + 512)
            sp.wait_ge(o_added, 2 * TT - 1 + half)
            sp.dma_start(out_t[TT - 1][:, sl], resid[:, TT - 1, sl]).then_inc(stored, 16)
        sp.wait_ge(stored, 16 * (TT + 1))

    @block.gpsimd
    def _(pool):
        for t in range(TT):
            pool.wait_ge(col_done, 2 * (t // TPB + 1))
            if t >= 2:
                pool.wait_ge(v_scaled, t - 1)
            nc.gpsimd.tensor_tensor(resid[:, t, :], resid[:, t, :], colterm[:, t // TPB, :], ALU.add).then_inc(col_added, 1)

    @block.scalar
    def _(act):
        def scale_tile(t):
            act.wait_ge(v_quant, t - 1)
            nc.scalar.activation(v1[:, t % 2, :], resid[:, t, :], ACT.Identity, bias=scl[:, 1, t:t + 1],
                                 scale=scl[:, 0, t:t + 1]).then_inc(v_scaled, 1)

        def copy_turned(t):
            act.wait_ge(q_turned, t + 1)
            if t >= 2:
                act.wait_ge(p_done, PB["mul", 2 * (t - 2) + 1] + 1)
            nc.scalar.copy(q1T[:, t % 2, :, :], qb).then_inc(q_copied, 1)

        def high(kind, f):
            act.wait_ge(f_turned, LB[kind, f] + 1)
            if kind == "x" and f >= 2:
                act.wait_ge(z_done, f // 2)
            if kind == "z" and f >= 1:
                act.wait_ge(p_done, PB["out", 2 * f - 1] + 1)
            if kind == "k":
                nc.scalar.copy(keysT[:], filled(kind, f)[0:ROUTER, 0, 0:EXPERTS]).then_inc(f_hi, 1)
            else:
                nc.scalar.copy(target(kind, f)[0], filled(kind, f)).then_inc(f_hi, 1)

        def read_product(t):
            for half in range(2):
                m = 2 * t + half
                act.wait_ge(p_done, PB["mul", m] + 1)
                act.wait_ge(row_done, t + 1)
                if m >= 2:
                    act.wait_ge(m_added, m - 1)
                nc.scalar.activation(part[:, half, :], pb[PB["mul", m] % 2], ACT.Identity,
                                     bias=rowterm[:, t:t + 1], scale=S12).then_inc(m_read, 1)

        def root(t):
            act.wait_ge(var3, t + 1)
            nc.scalar.activation(lnw[:, 1, t:t + 1], lnw[:, 0, t:t + 1], ACT.Sqrt).then_inc(root3, 1)

        def normalise(t):
            act.wait_ge(scale3, t + 1)
            if t >= 1:
                act.wait_ge(f_turned, LB["x", 2 * t - 1] + 1)
            nc.scalar.activation(norm[:], resid[:, t, :], ACT.Identity, bias=mean_rstd[:, t:t + 1],
                                 scale=rstd[:, t:t + 1]).then_inc(n_done, 1)

        def column_term(n):
            if n == 2 * NB - 1:
                act.wait_ge(sum_done, 1)
            nc.scalar.activation(colterm[:, n // 2, (n % 2) * 512:(n % 2) * 512 + 512], banks[:, n, :],
                                 ACT.Identity, bias=BOTH, scale=COL).then_inc(col_done, 1)

        def exponentials(t):
            act.wait_ge(peak_done, t + 1)
            nc.scalar.activation(weight[:, 0, :], seen[:], ACT.Exp, bias=peak[:, 0:1]).then_inc(exp_done, 1)

        def highs(kind, fills):
            for f in fills:
                high(kind, f)

        column_term(0)
        column_term(1)
        highs("a", range(2))
        copy_turned(0)
        column_term(2)
        column_term(3)
        high("k", 0)
        scale_tile(2)
        read_product(0)
        copy_turned(1)
        highs("a", range(2, 4))
        scale_tile(3)
        root(0)
        normalise(0)
        high("a", 4)
        read_product(1)
        act.wait_ge(mT_done, 1)
        nc.scalar.copy(mT[0], mb.rearrange("p (k e) -> p k e", e=EXPERTS)).then_inc(mT_hi, 1)
        highs("a", range(5, 8))
        copy_turned(2)
        highs("x", range(2))
        highs("b", range(2))
        root(1)
        highs("b", range(2, 4))
        read_product(2)
        normalise(1)
        scale_tile(4)
        highs("b", range(4, 6))
        root(2)
        copy_turned(3)
        exponentials(0)
        for i in range(1, TT):
            highs("x", (2 * i, 2 * i + 1))
            if i + 4 < TT:
                scale_tile(i + 4)
            if i + 1 < TT:
                normalise(i + 1)
            if i + AHEAD < TT:
                read_product(i + AHEAD)
            high("z", i - 1)
            if i + AHEAD < TT:
                root(i + AHEAD)
            if i == 1:
                highs("b", range(6, 8))
            exponentials(i)
            if i + 3 < TT:
                copy_turned(i + 3)
        high("z", TT - 1)

    @block.vector
    def _(dve):
        link = Links(dve, dve_link)

        def quantise(t):
            if t >= 2:
                dve.wait_ge(v_scaled, t - 1)
            link(nc.vector.tensor_scalar(v1[:, t % 2, :], v1[:, t % 2, :], MAGIC, MAGIC, ALU.add, ALU.max))
            if t >= 2:
                dve.wait_ge(q_turned, t - 1)
            nc.vector.tensor_scalar(q1[:, t % 2, :], v1[:, t % 2, :], MAGIC + 255.0, MAGIC + MIDDLE,
                                    ALU.min, ALU.subtract).then_inc(v_quant, 1)

        def low(kind, f):
            dve.wait_ge(f_hi, LB[kind, f] + 1)
            if kind == "k":
                dve.wait_ge(f_lo, LB[kind, f])
                dve.sem_inc(f_lo, 1)
                return
            h, l = target(kind, f)
            nc.vector.tensor_tensor(l, filled(kind, f), h.bitcast(F32), ALU.subtract).then_inc(f_lo, 1)

        def row_term(t):
            dve.wait_ge(summed, t + 1)
            nc.vector.tensor_scalar(rowterm[:, t:t + 1], rb[:, t, 0:1], ROW, None, ALU.mult).then_inc(row_done, 1)

        def add_product(t):
            dve.wait_ge(col_added, t + 1)
            for half in range(2):
                sl = slice(half * 512, half * 512 + 512)
                dve.wait_ge(m_read, 2 * t + half + 1)
                nc.vector.tensor_tensor(resid[:, t, sl], part[:, half, :], resid[:, t, sl], ALU.add).then_inc(m_added, 1)
            dve.wait_ge(m_added, 2 * t + 2)
            row_stats(nc, resid, stats, moments, t, link)
            row_scale_in(nc, moments, lnw, slice(t, t + 1), var3)

        def scale_of(t):
            dve.wait_ge(root3, t + 1)
            row_scale_out(nc, lnw, rstd, slice(t, t + 1), link)
            nc.vector.scalar_tensor_tensor(mean_rstd[:, t:t + 1], moments[:, t, 0:1], -1.0, rstd[:, t:t + 1],
                                           ALU.mult, ALU.mult).then_inc(scale3, 1)

        def gate(t):
            dve.wait_ge(z_done, t + 1)
            nc.vector.tensor_copy(seen[:], hb[0][:, 0:EXPERTS]).then_inc(s_read, 1)
            dve.wait_ge(s_read, t + 1)
            link(nc.vector.max(top[:, 0, :], seen[:]))
            nc.vector.tensor_scalar(peak[:, 0:1], top[:, 0, 0:1], -1.0, None, ALU.mult).then_inc(peak_done, 1)
            link(nc.vector.match_replace(left[:, 0, :], top[:, 0, :], seen[:], NEVER))
            link(nc.vector.max(top[:, 1, :], left[:, 0, :]))
            link(nc.vector.match_replace(left[:, 1, :], top[:, 1, :], left[:, 0, :], NEVER))
            dve.wait_ge(exp_done, t + 1)
            link(nc.vector.scalar_tensor_tensor(weight[:, 1, :], left[:, 1, :], NEVER, weight[:, 0, :],
                                                ALU.is_equal, ALU.mult, accum_out=peak[:, 1:2]))
            link(nc.vector.reciprocal(peak[:, 2:3], peak[:, 1:2]))
            link(nc.vector.tensor_scalar(weight[:, 2, :], weight[:, 1, :], peak[:, 2:3], SCALING, ALU.mult, ALU.mult))
            if t >= 1:
                dve.wait_ge(f_turned, LB["z", t - 1] + 1)
            for bank, at, lo, hi in ((hb[0], EXPERTS, 0, EXPERTS_A), (hb[1], 0, EXPERTS_A, EXPERTS)):
                n = hi - lo
                ins = nc.vector.tensor_tensor(
                    zg[:, lo * RANK:hi * RANK].rearrange("p (e r) -> p e r", r=RANK),
                    bank[:, at:at + n * RANK].rearrange("p (e r) -> p e r", r=RANK),
                    weight[:, 2, lo:hi].unsqueeze(2).to_broadcast([P, n, RANK]), ALU.mult)
            ins.then_inc(z_gated, 1)

        def add_out(t):
            for half in range(2):
                sl = slice(half * 512, half * 512 + 512)
                n = PB["out", 2 * t + half]
                dve.wait_ge(p_done, n + 1)
                nc.vector.tensor_tensor(resid[:, t, sl], pb[n % 2], resid[:, t, sl], ALU.add).then_inc(o_added, 1)

        def lows(kind, fills):
            for f in fills:
                low(kind, f)

        quantise(0)
        lows("a", range(2))
        quantise(1)
        low("k", 0)
        row_term(0)
        add_product(0)
        low("a", 2)
        scale_of(0)
        low("a", 3)
        row_term(1)
        quantise(2)
        low("a", 4)
        low("a", 5)
        dve.wait_ge(mT_hi, 1)
        nc.vector.tensor_tensor(mT[1], mb.rearrange("p (k e) -> p k e", e=EXPERTS), mT[0].bitcast(F32),
                                ALU.subtract).then_inc(mT_lo, 1)
        lows("a", range(6, 8))
        lows("x", range(2))
        add_product(1)
        row_term(2)
        lows("b", range(2))
        scale_of(1)
        quantise(3)
        lows("b", range(2, 4))
        add_product(2)
        lows("b", range(4, 6))
        scale_of(2)
        quantise(4)
        gate(0)
        for i in range(1, TT):
            lows("x", (2 * i, 2 * i + 1))
            if i + 4 < TT:
                quantise(i + 4)
            if i + AHEAD < TT:
                row_term(i + AHEAD)
                add_product(i + AHEAD)
            low("z", i - 1)
            if i + AHEAD < TT:
                scale_of(i + AHEAD)
            if i == 1:
                lows("b", range(6, 8))
            gate(i)
            add_out(i - 1)
        low("z", TT - 1)
        add_out(TT - 1)

    @block.tensor
    def _(pe):
        def pb_free(kind, f):
            n = PB[kind, f] - 2
            if n < 0:
                return
            was = pb_order[n][0]
            pe.wait_ge({"mul": m_read, "out": o_added}[was], sum(x[0] == was for x in pb_order[:n + 1]))

        def turn_fill(kind, f):
            b = filled(kind, f)
            if kind == "z":
                pe.wait_ge(q_copied, min(f + 4, TT))
            elif IN_LB[kind, f] >= 2:
                pe.wait_ge(f_lo, LB[in_lb[IN_LB[kind, f] - 2]] + 1)
            if kind == "x":
                if f % 2 == 0:
                    pe.wait_ge(n_done, f // 2 + 1)
                blocks = [(b[:, k, :], norm[:, (4 * (f % 2) + k) * P:(4 * (f % 2) + k + 1) * P]) for k in range(4)]
            elif kind == "a":
                blocks = [(b[:, k, :], a_rows[:, f // 2, (4 * (f % 2) + k) * P:(4 * (f % 2) + k + 1) * P])
                          for k in range(4)]
            elif kind == "b":
                blocks = [(b[:, j, :], b_rows[:, f, j * P:(j + 1) * P]) for j in range(NT)]
            elif kind == "k":
                pe.wait_ge(k_in, 16)
                blocks = [(b[0:ROUTER, 0, 0:EXPERTS], kraw[:])]
            else:
                pe.wait_ge(z_gated, f + 1)
                blocks = [(b[:, j, :], zg[:, j * P:(j + 1) * P]) for j in range(NT)]
            for dst, src in blocks:
                rows = src.shape[0]
                ins = nc.tensor.transpose(dst, src, ident[0:rows, 0:rows])
            ins.then_inc(f_turned, 1)

        def turn_quantised(t):
            pe.wait_ge(v_quant, t + 1)
            if t >= 1:
                pe.wait_ge(q_copied, t)
            if t >= 4:
                pe.wait_ge(f_lo, LB["z", t - 4] + 1)
            for k in range(KT):
                ins = nc.tensor.transpose(qb[:, k, :], q1[:, t % 2, k * P:(k + 1) * P], identb[:])
            ins.then_inc(q_turned, 1)

        def multiply(t):
            pe.wait_ge(q_copied, t + 1)
            if t >= 1:
                pe.wait_ge(row_done, t)
            for k in range(KT):
                ins = nc.tensor.matmul(rb[:, t, :], q1T[:, t % 2, k, :], one[:, 0:2], start=(k == 0), stop=(k == KT - 1))
            ins.then_inc(summed, 1)
            if t == 0:
                pe.wait_ge(col_done, 2)
            for half in range(2):
                pb_free("mul", 2 * t + half)
                for k in range(KT):
                    ins = nc.tensor.matmul(pb[PB["mul", 2 * t + half] % 2], q1T[:, t % 2, k, :],
                                           q2[:, (t // TPB) * KT + k, half * 512:half * 512 + 512],
                                           start=(k == 0), stop=(k == KT - 1))
                ins.then_inc(p_done, 1)

        def router_matrix():
            pe.wait_ge(r_in, 16)
            pe.wait_ge(f_hi, LB["k", 0] + 1)
            pe.wait_ge(col_done, 2 * NB)
            for k in range(KT):
                ins = nc.tensor.matmul(mb[:, k * EXPERTS:(k + 1) * EXPERTS], rraw[:, k * P:(k + 1) * P], keysT[:],
                                       start=True, stop=True)
            ins.then_inc(mT_done, 1)

        def hidden(t, ks):
            if ks[0] == 0:
                pe.wait_ge(f_lo, LB["x", 2 * t + 1] + 1)
                if t == 0:
                    pe.wait_ge(mT_lo, 1)
                else:
                    pe.wait_ge(z_gated, t)
            for k in ks:
                for p, (a, c) in enumerate(PASSES):
                    for n in range(2):
                        ins = nc.tensor.matmul(hb[n][:, 0:HALF], xe[a][:, k, :], wT[c][:, k, n * HALF:(n + 1) * HALF],
                                               start=(k == 0 and p == 0), stop=(k == KT - 1 and p == 2))
            if ks[-1] == KT - 1:
                ins.then_inc(z_done, 1)

        def expand(t):
            pe.wait_ge(f_lo, (LB["z", t] if t else LB["b", KT - 1]) + 1)
            for half in range(2):
                pb_free("out", 2 * t + half)
                for j in range(NT):
                    for p, (a, c) in enumerate(PASSES):
                        ins = nc.tensor.matmul(pb[PB["out", 2 * t + half] % 2], zT[a][:, j, :],
                                               bT[c][:, j, half * 512:half * 512 + 512],
                                               start=(j == 0 and p == 0), stop=(j == NT - 1 and p == 2))
                ins.then_inc(p_done, 1)

        def turn_fills(kind, fills):
            for f in fills:
                turn_fill(kind, f)

        turn_fills("a", range(2))
        turn_quantised(0)
        for k in range(KT):
            ins = nc.tensor.matmul(banks[:, 2 * NB - 1, :], one[:], q2[:, (NB - 1) * KT + k, D - 512:D],
                                   start=(k == 0), stop=(k == KT - 1))
        ins.then_inc(sum_done, 1)
        turn_fill("k", 0)
        multiply(0)
        turn_quantised(1)
        turn_fills("a", range(2, 4))
        multiply(1)
        turn_fill("a", 4)
        router_matrix()
        turn_fills("a", range(5, 8))
        turn_quantised(2)
        for i in range(TT):
            turn_fills("x", (2 * i, 2 * i + 1))
            if i + AHEAD < TT:
                multiply(i + AHEAD)
            if i == 0:
                turn_fills("b", range(2))
            if i >= 1:
                turn_fill("z", i - 1)
            hidden(i, range(0, KT // 2))
            if i == 0:
                turn_fills("b", range(2, 4))
            if i == 1:
                turn_fills("b", range(6, 8))
            hidden(i, range(KT // 2, KT))
            if i == 0:
                turn_fills("b", range(4, 6))
            if i + 3 < TT:
                turn_quantised(i + 3)
            if i >= 1:
                expand(i - 1)
        turn_fill("z", TT - 1)
        expand(TT - 1)


def rope_tables():
    exponents = np.arange(0, HEAD, 2, dtype=np.float32) / np.float32(HEAD)
    inv_freq = (np.float32(1.0) / np.power(np.float32(ROPE_THETA), exponents)).astype(np.float32)
    freqs = np.outer(np.arange(512, dtype=np.float32), inv_freq).astype(np.float32)
    cos = np.cos(freqs).T
    sin = np.sin(freqs).T
    return (np.ascontiguousarray(np.concatenate([cos, cos]), np.float32),
            np.ascontiguousarray(np.concatenate([sin, -sin]), np.float32))


_INS = ["x", "ctx_4096", "L0_attn_Wq", "L0_attn_Wk", "L0_attn_Wv", "L0_attn_Wo", "L0_xattn_x1_scale",
        "L0_xattn_x1_zp", "L0_xattn_x2_scale", "L0_xattn_x2_zp", "L0_ffn_A_w", "L0_ffn_B_w",
        "L0_ffn_Wq_w", "L0_ffn_keys"]


def kernel(**inputs):
    import concourse.bacc as bacc
    from concourse.bass_utils import run_bass_kernel_spmd

    nc = bacc.Bacc("TRN2", target_bir_lowering=False, num_devices=1, **BACC)
    arrays = {f"in_{n}": np.ascontiguousarray(inputs[n]) for n in _INS}
    arrays["in_cos"], arrays["in_sin"] = rope_tables()
    args = [nc.dram_tensor(n, a.shape, mybir.dt.from_np(a.dtype), kind="ExternalInput").ap() for n, a in arrays.items()]
    x = arrays["in_x"]
    out = nc.dram_tensor("out", x.shape, F32, kind="ExternalOutput").ap()
    build(nc, *args, out)
    r = run_bass_kernel_spmd(nc, [arrays], core_ids=[0])
    return r.results[0]["out"]
```
